# Optimizing a Trainium2 kernel written in Bass

```python
import numpy as np
import jax
import jax.numpy as jnp

def _softmax(x, axis=-1):
    return jax.nn.softmax(x, axis=axis)

def _gelu(x):
    return jax.nn.gelu(x, approximate=True)

def _silu(x):
    return jax.nn.silu(x)

def _sigmoid(x):
    return jax.nn.sigmoid(x)

def _layernorm(x, axis=-1, eps=1e-05):
    m = jnp.mean(x, axis=axis, keepdims=True)
    v = jnp.var(x, axis=axis, keepdims=True)
    return (x - m) / jnp.sqrt(v + eps)

def _scatter_add(tgt, idx, src, axis=0):
    return tgt.at[idx].add(src)

def _segment_sum(src, seg, n):
    return jax.ops.segment_sum(src, seg, n)
kernel_name = 'mk_prb_d2_jaxref_r8_cb4391'

def setup_inputs(seed: int=0):
    np.random.seed(seed)
    _w = jnp.asarray

    def _L0_attn_setup():
        import jax, jax.numpy as jnp
        import numpy as np
        DIM = 128
        NUM_HEADS = 16
        HEAD_DIM = DIM // NUM_HEADS
        EPS_NORM = 1e-12
        EPS_LN = 1e-05
        key = jax.random.key(seed)
        ks = jax.random.split(key, 6)
        x = jax.random.normal(ks[0], (4, 256, DIM), dtype=jnp.float32)
        ln_w = jnp.ones((DIM,), jnp.float32)
        ln_b = jnp.zeros((DIM,), jnp.float32)
        limit = float(np.sqrt(6.0 / (DIM + 3 * DIM)))
        qkv_w = jax.random.uniform(ks[1], (3 * DIM, DIM), jnp.float32, -limit, limit)
        qkv_b = jnp.zeros((3 * DIM,), jnp.float32)
        out_w = 0.02 * jax.random.normal(ks[2], (DIM, DIM), dtype=jnp.float32)
        out_b = jnp.zeros((DIM,), jnp.float32)
        return {'x': x, 'ln_w': ln_w, 'ln_b': ln_b, 'qkv_w': qkv_w, 'qkv_b': qkv_b, 'out_w': out_w, 'out_b': out_b}
    _L0_attn_in = _L0_attn_setup()

    def _L0_ffn_setup():
        import jax, jax.numpy as jnp
        import numpy as np
        D = 128
        H = 512
        E = 64
        K = 3
        B, S = (2, 256)
        C = 64
        key = jax.random.key(seed)
        ks = jax.random.split(key, 6)
        s = 0.02
        return {'x': jax.random.normal(ks[0], (B, S, D), jnp.float32), 'gate_w': jax.random.normal(ks[1], (D, E), jnp.float32) * s, 'gate_b': jnp.zeros((E,), jnp.float32), 'w1': jax.random.normal(ks[2], (E, D, H), jnp.float32) * s, 'b1': jnp.zeros((E, H), jnp.float32), 'w2': jax.random.normal(ks[3], (E, H, D), jnp.float32) * s, 'b2': jnp.zeros((E, D), jnp.float32)}
    _L0_ffn_in = _L0_ffn_setup()

    def _L1_attn_setup():
        import jax, jax.numpy as jnp
        import numpy as np
        NEG_BIG = -1e+38

        def _wkv_scan(w, u, k, v, aa0, bb0, pp0):
            kT = jnp.moveaxis(k, 1, 0)
            vT = jnp.moveaxis(v, 1, 0)

            def step(carry, kv):
                aa, bb, pp = carry
                kt, vt = kv
                ww = u + kt
                p = jnp.maximum(pp, ww)
                e1 = jnp.exp(pp - p)
                e2 = jnp.exp(ww - p)
                y = (e1 * aa + e2 * vt) / (e1 * bb + e2)
                ww2 = pp + w
                p2 = jnp.maximum(ww2, kt)
                e1 = jnp.exp(ww2 - p2)
                e2 = jnp.exp(kt - p2)
                return ((e1 * aa + e2 * vt, e1 * bb + e2, p2), y)
            (aa, bb, pp), yT = jax.lax.scan(step, (aa0, bb0, pp0), (kT, vT))
            return (jnp.moveaxis(yT, 0, 1), aa, bb, pp)

        def _reference_tuple_inner(x, W_rvk, W_out, time_decay, time_first):
            B, T, C = x.shape
            rvk = jnp.einsum('btc,dc->btd', x, W_rvk)
            r, v, k = jnp.split(rvk, 3, axis=-1)
            w = -jnp.exp(time_decay)
            u = time_first
            aa0 = jnp.zeros((B, C), dtype=x.dtype)
            bb0 = jnp.zeros((B, C), dtype=x.dtype)
            pp0 = jnp.full((B, C), NEG_BIG, dtype=x.dtype)
            wkv, aa, bb, pp = _wkv_scan(w, u, k, v, aa0, bb0, pp0)
            rwkv = jax.nn.sigmoid(r) * wkv
            out = jnp.einsum('btc,dc->btd', rwkv, W_out)
            h = aa
            c = jnp.stack([bb, pp], axis=-1).reshape(B, 2 * C)
            return (out, h, c)
        key = jax.random.key(seed)
        k1, k2, k3 = jax.random.split(key, 3)
        B, T, C = (32, 128, 128)
        x = jax.random.normal(k1, (B, T, C), dtype=jnp.float32)
        W_rvk = jax.random.normal(k2, (3 * C, C), dtype=jnp.float32) * (1.0 / np.sqrt(C))
        W_out = jax.random.normal(k3, (C, C), dtype=jnp.float32) * (1.0 / np.sqrt(C))
        time_decay = jnp.ones((C,), dtype=jnp.float32)
        time_first = jnp.ones((C,), dtype=jnp.float32)
        return {'x': x, 'W_rvk': W_rvk, 'W_out': W_out, 'time_decay': time_decay, 'time_first': time_first}
    _L1_attn_in = _L1_attn_setup()

    def _L1_ffn_setup():
        import jax, jax.numpy as jnp
        import numpy as np
        NUM_EXPERTS = 8
        TOP_K = 2
        key = jax.random.key(seed)
        ks = jax.random.split(key, 6)
        B, S, D, H, E = (4, 128, 128, 256, NUM_EXPERTS)
        x = jax.random.normal(ks[0], (B, S, D), dtype=jnp.float32)
        Wg = jax.random.normal(ks[1], (D, E), dtype=jnp.float32) * 0.02
        W1 = jax.random.normal(ks[2], (E, D, H), dtype=jnp.float32) * 0.02
        b1 = jax.random.normal(ks[3], (E, H), dtype=jnp.float32) * 0.02
        W2 = jax.random.normal(ks[4], (E, H, D), dtype=jnp.float32) * 0.02
        b2 = jax.random.normal(ks[5], (E, D), dtype=jnp.float32) * 0.02
        return {'x': x, 'Wg': Wg, 'W1': W1, 'b1': b1, 'W2': W2, 'b2': b2}
    _L1_ffn_in = _L1_ffn_setup()
    _d = {'L0_attn_x': _L0_attn_in['x'], 'L0_attn_ln_w': _L0_attn_in['ln_w'], 'L0_attn_ln_b': _L0_attn_in['ln_b'], 'L0_attn_qkv_w': _L0_attn_in['qkv_w'], 'L0_attn_qkv_b': _L0_attn_in['qkv_b'], 'L0_attn_out_w': _L0_attn_in['out_w'], 'L0_attn_out_b': _L0_attn_in['out_b'], 'L0_ffn_gate_w': _L0_ffn_in['gate_w'], 'L0_ffn_gate_b': _L0_ffn_in['gate_b'], 'L0_ffn_w1': _L0_ffn_in['w1'], 'L0_ffn_b1': _L0_ffn_in['b1'], 'L0_ffn_w2': _L0_ffn_in['w2'], 'L0_ffn_b2': _L0_ffn_in['b2'], 'L1_attn_W_rvk': _L1_attn_in['W_rvk'], 'L1_attn_W_out': _L1_attn_in['W_out'], 'L1_attn_time_decay': _L1_attn_in['time_decay'], 'L1_attn_time_first': _L1_attn_in['time_first'], 'L1_ffn_Wg': _L1_ffn_in['Wg'], 'L1_ffn_W1': _L1_ffn_in['W1'], 'L1_ffn_b1': _L1_ffn_in['b1'], 'L1_ffn_W2': _L1_ffn_in['W2'], 'L1_ffn_b2': _L1_ffn_in['b2']}
    _x0 = _d['L0_attn_x']
    _d['L0_attn_x'] = jax.random.normal(jax.random.fold_in(jax.random.key(seed), 1), (2, 1024, 128), dtype=_x0.dtype)
    del _x0
    return _d

def reference(L0_attn_x, L0_attn_ln_w, L0_attn_ln_b, L0_attn_qkv_w, L0_attn_qkv_b, L0_attn_out_w, L0_attn_out_b, L0_ffn_gate_w, L0_ffn_gate_b, L0_ffn_w1, L0_ffn_b1, L0_ffn_w2, L0_ffn_b2, L1_attn_W_rvk, L1_attn_W_out, L1_attn_time_decay, L1_attn_time_first, L1_ffn_Wg, L1_ffn_W1, L1_ffn_b1, L1_ffn_W2, L1_ffn_b2):

    def _L0_attn_ref(x, ln_w, ln_b, qkv_w, qkv_b, out_w, out_b):
        import jax, jax.numpy as jnp
        import numpy as np
        DIM = 128
        NUM_HEADS = 16
        HEAD_DIM = DIM // NUM_HEADS
        EPS_NORM = 1e-12
        EPS_LN = 1e-05
        B, N, D = x.shape
        mu = jnp.mean(x, axis=-1, keepdims=True)
        var = jnp.mean(jnp.square(x - mu), axis=-1, keepdims=True)
        h = (x - mu) / jnp.sqrt(var + EPS_LN) * ln_w + ln_b
        qkv = h @ qkv_w.T + qkv_b
        qkv = qkv.reshape(B, N, 3, NUM_HEADS, HEAD_DIM)
        q, k, v = (jnp.transpose(qkv[:, :, i], (0, 2, 1, 3)) for i in range(3))
        q = q / jnp.maximum(jnp.linalg.norm(q, axis=-1, keepdims=True), EPS_NORM)
        k = k / jnp.maximum(jnp.linalg.norm(k, axis=-1, keepdims=True), EPS_NORM)
        scale = HEAD_DIM ** 0.5
        attn = jnp.einsum('bhqd,bhkd->bhqk', q, k) * scale
        attn = jax.nn.softmax(attn, axis=-1)
        out = jnp.einsum('bhqk,bhkd->bhqd', attn, v)
        out = jnp.transpose(out, (0, 2, 1, 3)).reshape(B, N, D)
        return x + out @ out_w.T + out_b

    def _L0_ffn_ref(x, gate_w, gate_b, w1, b1, w2, b2):
        import jax, jax.numpy as jnp
        import numpy as np
        D = 128
        H = 512
        E = 64
        K = 3
        B, S = (2, 256)
        C = 64
        xf = x.reshape(-1, D)
        T = xf.shape[0]
        logits = xf @ gate_w + gate_b
        top_l, top_i = jax.lax.top_k(logits, K)
        gates = jax.nn.softmax(top_l, axis=-1)
        fe = top_i.reshape(-1)
        fg = gates.reshape(-1)
        tok = jnp.repeat(jnp.arange(T), K)
        oh = jax.nn.one_hot(fe, E, dtype=jnp.int32)
        pos = (jnp.cumsum(oh, axis=0) * oh).sum(-1) - 1
        valid = pos < C
        buf = jnp.zeros((E, C, D), x.dtype).at[fe, pos].set(xf[tok], mode='drop')
        h = jax.nn.gelu(jnp.einsum('ecd,edh->ech', buf, w1) + b1[:, None, :], approximate=False)
        y = jnp.einsum('ech,ehd->ecd', h, w2) + b2[:, None, :]
        rows = y[fe, jnp.minimum(pos, C - 1)] * (fg * valid.astype(x.dtype))[:, None]
        out = jnp.zeros_like(xf).at[tok].add(rows)
        return out.reshape(x.shape)

    def _L1_attn_ref(x, W_rvk, W_out, time_decay, time_first):
        import jax, jax.numpy as jnp
        import numpy as np
        NEG_BIG = -1e+38

        def _wkv_scan(w, u, k, v, aa0, bb0, pp0):
            kT = jnp.moveaxis(k, 1, 0)
            vT = jnp.moveaxis(v, 1, 0)

            def step(carry, kv):
                aa, bb, pp = carry
                kt, vt = kv
                ww = u + kt
                p = jnp.maximum(pp, ww)
                e1 = jnp.exp(pp - p)
                e2 = jnp.exp(ww - p)
                y = (e1 * aa + e2 * vt) / (e1 * bb + e2)
                ww2 = pp + w
                p2 = jnp.maximum(ww2, kt)
                e1 = jnp.exp(ww2 - p2)
                e2 = jnp.exp(kt - p2)
                return ((e1 * aa + e2 * vt, e1 * bb + e2, p2), y)
            (aa, bb, pp), yT = jax.lax.scan(step, (aa0, bb0, pp0), (kT, vT))
            return (jnp.moveaxis(yT, 0, 1), aa, bb, pp)

        def _reference_tuple_inner(x, W_rvk, W_out, time_decay, time_first):
            B, T, C = x.shape
            rvk = jnp.einsum('btc,dc->btd', x, W_rvk)
            r, v, k = jnp.split(rvk, 3, axis=-1)
            w = -jnp.exp(time_decay)
            u = time_first
            aa0 = jnp.zeros((B, C), dtype=x.dtype)
            bb0 = jnp.zeros((B, C), dtype=x.dtype)
            pp0 = jnp.full((B, C), NEG_BIG, dtype=x.dtype)
            wkv, aa, bb, pp = _wkv_scan(w, u, k, v, aa0, bb0, pp0)
            rwkv = jax.nn.sigmoid(r) * wkv
            out = jnp.einsum('btc,dc->btd', rwkv, W_out)
            h = aa
            c = jnp.stack([bb, pp], axis=-1).reshape(B, 2 * C)
            return (out, h, c)
        return _reference_tuple_inner(x, W_rvk, W_out, time_decay, time_first)[0]

    def _L1_ffn_ref(x, Wg, W1, b1, W2, b2):
        import jax, jax.numpy as jnp
        import numpy as np
        NUM_EXPERTS = 8
        TOP_K = 2
        B, S, D = x.shape
        E, _, H = W1.shape
        OUT = W2.shape[2]
        xm = x.reshape(-1, D)
        logits = xm @ Wg
        probs = jax.nn.softmax(logits, axis=-1)
        topk_p, topk_i = jax.lax.top_k(probs, TOP_K)
        flat_e = topk_i.reshape(-1)
        flat_p = topk_p.reshape(-1)
        order = jnp.argsort(flat_e)
        tok_idx = order // TOP_K
        e_sorted = flat_e[order]
        p_sorted = flat_p[order]
        xs = xm[tok_idx]
        y = jnp.zeros((xs.shape[0], OUT), dtype=xs.dtype)
        for e in range(E):
            h = jax.nn.relu(xs @ W1[e] + b1[e])
            ye = h @ W2[e] + b2[e]
            m = (e_sorted == e)[:, None].astype(xs.dtype)
            y = y + m * ye
        y = y * p_sorted[:, None]
        out = jnp.zeros((B * S, OUT), dtype=y.dtype).at[tok_idx].add(y)
        return out.reshape(B, S, OUT)
    x = L0_attn_x
    xn = _layernorm(x, axis=-1)
    x = x + _L0_attn_ref(xn, L0_attn_ln_w, L0_attn_ln_b, L0_attn_qkv_w, L0_attn_qkv_b, L0_attn_out_w, L0_attn_out_b) + _L0_ffn_ref(xn, L0_ffn_gate_w, L0_ffn_gate_b, L0_ffn_w1, L0_ffn_b1, L0_ffn_w2, L0_ffn_b2)
    xn = _layernorm(x, axis=-1)
    x = x + _L1_attn_ref(xn, L1_attn_W_rvk, L1_attn_W_out, L1_attn_time_decay, L1_attn_time_first) + _L1_ffn_ref(xn, L1_ffn_Wg, L1_ffn_W1, L1_ffn_b1, L1_ffn_W2, L1_ffn_b2)
    return x

_drawn_inputs = setup_inputs


def setup_inputs(seed=0):
    import zlib

    import numpy as np

    out = dict(_drawn_inputs(seed))
    spreads = {'L0_attn_ln_w': (1.0, 0.6),
     'L0_attn_ln_b': (0.0, 0.8),
     'L0_attn_qkv_b': (0.0, 0.602),
     'L0_attn_out_b': (0.0, 0.1),
     'L0_ffn_gate_b': (0.0, 0.334),
     'L0_ffn_b1': (0.0, 0.8),
     'L0_ffn_b2': (0.0, 0.37),
     'L1_attn_time_decay': (1.0, 0.6),
     'L1_attn_time_first': (1.0, 0.6)}
    factors = {'L0_attn_qkv_w': 4.711,
     'L0_attn_out_w': 3.334,
     'L0_ffn_w1': 4.961,
     'L0_ffn_w2': 4.493,
     'L1_ffn_Wg': 8.0,
     'L1_ffn_W1': 8.0,
     'L1_ffn_b1': 8.0,
     'L1_ffn_W2': 8.0,
     'L1_ffn_b2': 8.0}
    for name, (base, spread) in spreads.items():
        noise = np.random.default_rng([zlib.crc32(name.encode()), seed]).standard_normal(out[name].shape)
        drawn = base * np.exp(spread * noise) if base else spread * noise
        out[name] = jnp.asarray(drawn.astype(out[name].dtype))
    for name, factor in factors.items():
        out[name] = (out[name] * factor).astype(out[name].dtype)
    return out
```

```python
from contextlib import ExitStack

import concourse.bass as bass
from concourse import mybir

ALU = mybir.AluOpType
ACT = mybir.ActivationFunctionType
AX = mybir.AxisListType.X
F32 = mybir.dt.float32
F16 = mybir.dt.float16
BF16 = mybir.dt.bfloat16
U32 = mybir.dt.uint32

P = 128
D = 128
LN_EPS = 1e-5
NORM_EPS = 1e-12
NEG_BIG = -1e38


def build(nc, x_d, ln_w_d, ln_b_d, qkv_w_d, qkv_b_d, out_w_d, out_b_d, gate_w_d, gate_b_d, w1_d, b1_d, w2_d, b2_d,
          rvk_w_d, rout_w_d, decay_d, first_d, wg_d, mw1_d, mb1_d, mw2_d, mb2_d, out_d):
    B, N, _ = x_d.shape
    T = B * N
    NT = T // P
    CH = 4
    NC = NT // CH
    BLK = CH * P
    HEADS, HD = 16, 8
    HG = 4
    NHG = HEADS // HG
    NG = NC * NHG
    KT_TILES = N // P
    VW = 16
    E0, TOPK, CAP, H0 = w1_d.shape[0], 3, 64, w1_d.shape[2]
    SLOTS = E0 * CAP
    NPAIR = E0 // 2
    E1, H1 = mw1_d.shape[0], mw1_d.shape[2]
    HC0 = H0 // P
    HC1 = H1 // P
    SCALE = float(HD) ** 0.5
    RING = 4
    MOE_FROM = NG - NPAIR // RING

    x_v = x_d.rearrange("b n d -> (b n) d").rearrange("(t p) d -> p t d", p=P)
    out_v = out_d.rearrange("b n d -> (b n) d").rearrange("(t p) d -> p t d", p=P)
    slot_in = nc.dram_tensor("slot_in", [SLOTS, D], F32, kind="Internal").ap()
    slot_out = nc.dram_tensor("slot_out", [SLOTS, D], F32, kind="Internal").ap()

    with ExitStack() as ctx:
        def sb(name, shape, dt=F32):
            return ctx.enter_context(nc.sbuf_tensor(name, shape, dt))

        def sem(name):
            return ctx.enter_context(nc.semaphore(name))

        RA = sb("region_a", [P, 11776])
        RB = sb("region_b", [P, 16384])

        def carve(region, at, words, dt=F32):
            v = region[:, at:at + words]
            return v if dt == F32 else v.bitcast(dt)

        X = carve(RA, 0, 2048).rearrange("p (t d) -> p t d", d=D)
        QKA = carve(RA, 2048, 4096).rearrange("p (s t d) -> p s t d", s=2, d=D)
        KS = carve(RA, 6144, 1024, F16).rearrange("p (n w d) -> p n w d", w=4, d=HD)
        QS = carve(RA, 7168, 1024, F16).rearrange("p (n w d) -> p n w d", w=4, d=HD)
        LG = carve(RA, 8192, 1024).rearrange("p (t e) -> p t e", e=E0)
        TMP = carve(RA, 9216, 1024)
        EQ = carve(RA, 10240, 1536, BF16).rearrange("p (k t e) -> p k t e", k=TOPK, e=E0)
        RW = 2816
        ring_w1 = [carve(RA, RW * i, 1024).rearrange("p (e n) -> p e n", e=2) for i in range(RING)]
        ring_w2 = [carve(RA, RW * i + 1024, 1024).rearrange("p (e c d) -> p e c d", e=2, d=D) for i in range(RING)]
        ring_b1 = [carve(RA, RW * i + 2048, 512) for i in range(RING)]
        ring_b2 = carve(RA, 0, RW * RING).rearrange("p (i w) -> p i w", i=RING)[:, :, 2560:2688]
        ring_in = [carve(RA, RW * i + 2688, 128) for i in range(RING)]
        KT = carve(RB, 0, 4096, F16).rearrange("p (g n) -> p g n", g=NHG)
        QT = carve(RB, 4096, 4096, F16).rearrange("p (g n) -> p g n", g=NHG)
        VA = carve(RB, 8192, 4096).rearrange("p (t h w) -> p t h w", h=HEADS, w=VW)
        PR = carve(RB, 12288, 4096).rearrange("p (a j n) -> p a j n", a=2, j=HG)
        HN = carve(RB, 12288, 2048).rearrange("p (t d) -> p t d", d=D)
        XNT = carve(RB, 14336, 1024).rearrange("p (a n) -> p a n", a=2)
        HT = carve(RB, 15360, 1024).rearrange("p (a n) -> p a n", a=2)
        YG = carve(RB, 0, 6144).rearrange("p (t k d) -> p t k d", k=TOPK, d=D)
        HS = carve(RB, 14336, 2048).rearrange("p (a c n) -> p a c n", a=2, c=HC1)
        wkv = [carve(RB, 6144 + 512 * i, 512) for i in range(16)]
        KX, VX, ER, D1, D2, PM, F1, F2, EV, NU, DE, T1, RWa, RWb, OTT, _ = wkv
        RWT = [RWa, RWb]

        BASE = sb("base", [P, NT, D])
        XN = sb("xn", [P, NT, D])
        ident = sb("ident", [P, P])
        ident16 = sb("ident16", [P, P], F16)
        before = sb("before", [P, P], BF16)
        ones = sb("ones", [P, P], BF16)
        iota_e = sb("iota_e", [P, E0])
        WL = TMP.rearrange("p (j n) -> p j n", n=P)
        WT = sb("w_cols", [P, 8, P])
        SMALL = sb("small_rows", [20, P])
        COL = sb("small_cols", [P, 20])
        qkv_b = sb("qkv_b", [P, 3 * D])
        gate_w = sb("gate_w", [P, E0])
        gate_b = sb("gate_b", [P, E0])
        out_b = sb("out_b", [P, D])
        WG = sb("wg", [P, E1])
        MW1 = sb("mw1", [P, E1, H1])
        MW2 = sb("mw2", [P, E1, HC1, D])
        MB2 = sb("mb2", [E1, D])
        ST = sb("bn", [P, NT, 6])
        MV = sb("mean_var", [P, NT, 2])
        SD = sb("std", [P, NT])
        RS = sb("rstd", [P, NT])
        NQ = sb("norm2", [P, 128])
        NS = sb("norm", [P, 128])
        MX = sb("top", [P, NT, 8])
        IX = sb("top_i", [P, NT, 8], U32)
        IXF = sb("top_if", [P, NT, TOPK])
        GE = sb("gates", [P, NT, TOPK])
        GS = sb("gate_sum", [P, NT])
        POS = sb("pos", [P, TOPK, NT])
        VAL = sb("valid", [P, TOPK, NT])
        SLF = sb("slot_f", [P, TOPK, NT])
        SLG = sb("slot_gather", [P, TOPK, NT], U32)
        SLS = sb("slot_scatter", [P, TOPK, NT], U32)
        MH = sb("mask_bf", [P, NT, E0], BF16)
        MPRE = sb("mask_prefix", [P, NT, E0], BF16)
        OH = sb("heads_out", [P, NC, CH, NHG, 32])
        OTs = sb("av_out", [P, 2, BLK])
        STG = sb("staged_kqv", [P, 4096])
        KST = carve(STG, 0, 1024, F16).rearrange("p (a n) -> p a n", a=2)
        QST = carve(STG, 1024, 2048, F16).rearrange("p (a j n) -> p a j n", a=2, j=HG)
        VST = carve(STG, 3072, 1024).rearrange("p (a s j w) -> p a s j w", a=2, s=KT_TILES, j=HG)
        HB = sb("h_rows", [P, RING, H0])
        BT = sb("slot_in_t", [P, RING * P])
        HTS = sb("h_cols", [P, 2, H0])
        Y = sb("y", [P, 2, 2, D])
        XN2 = carve(STG, 0, 512).rearrange("p (t d) -> p t d", d=D)
        XN2T = carve(STG, 512, 1024).rearrange("p (a n) -> p a n", a=2)
        GTT = carve(STG, 1536, 1024).rearrange("p (a n) -> p a n", a=2)
        G8 = sb("g8", [P, 2, CH, E1])
        L8 = sb("l8", [P, CH, E1])
        P8 = sb("p8", [P, CH, E1])
        M8 = sb("m8", [P, CH, 8])
        I8 = sb("i8", [P, CH, 8], U32)
        I8F = sb("i8f", [P, CH, 2])
        S4 = sb("s4", [P, CH])
        WDEC = sb("w_decay", [P, 1])
        PP, AA, BB = (HB[:].rearrange("p i n -> p (i n)")[:, (BLK + 1) * i:(BLK + 1) * (i + 1)] for i in range(3))
        NEGW = sb("neg_w", [P, 1])

        ps = [ctx.enter_context(nc.psum_tensor(f"bank{i}", [P, 512], F32)) if i > 3 else None for i in range(8)]
        S = ctx.enter_context(nc.psum_tensor("scores", [P, HG, 512], F32))
        for i in range(4):
            ps[i] = S[:, i]
        AV = ps[4]

        LNW, LNB, DECAY, FIRST = (COL[:, 16 + i:17 + i] for i in range(4))

        names = """w_in c_in l1_in const_ready zero_ready zeroed base_done pool_chain dve_chain
            var_ready std_ready xn_ready hn_ready wt_ps wt_sb xnt_ps xnt_sb hnt_ps ht_sb qkv_ps qkv_sb lg_ps lg_sb
            sq_ready nq_ready ns_ready qn_ready hi_ready lo_k lo_q kt_ps qt_ps kt_sb qt_sb
            staged qk_ready exp_done av_done a_evac ep_ps ep_used top_ready gexp_ready mask_ready count_ready slots_ready
            scattered bt_ps bt_sb up_done h_sb gelu_done htr_ps htr_sb down_done y_sb
            ot_ps ot_sb x1_ps x1_sb var2_ready std2_ready xn2_ready xn2t_ps xn2t_sb lg2_ps l8_ready p8_exp g_ready
            rvk_ps rvk_sb gt_ps gt_sb d_ready d_exp pool_wkv rw_ready decay_exp up2 relu_done down2 acc_done fin_ps fin_sb""".split()
        s = {n: sem(n) for n in names}
        x_in = [sem(f"x_in{c}") for c in range(NC)]
        ring_in_a = [sem(f"ring_a{i}") for i in range(RING)]
        ring_in_b = [sem(f"ring_b{i}") for i in range(RING)]
        ring_in_x = [sem(f"ring_x{i}") for i in range(RING)]
        y_out = [sem(f"y_out{i}") for i in range(2)]
        gathered = [sem(f"gathered{c}") for c in range(NC)]
        out_done = [sem(f"out_done{i}") for i in range(2)]

        def chain(eng, name):
            count = [0]

            def link(ins):
                count[0] += 1
                ins.then_inc(s[name], 1)
                eng.wait_ge(s[name], count[0])
            return link

        block = ctx.enter_context(nc.Block())

        @block.sync
        def _(sp):
            for c in range(NC):
                sp.dma_start(X[:, CH * c:CH * c + CH, :], x_v[:, CH * c:CH * c + CH, :]).then_inc(x_in[c], 16)
            sp.dma_start(qkv_b[:], qkv_b_d.partition_broadcast(P)).then_inc(s["c_in"], 16)
            sp.dma_start(gate_w[:], gate_w_d).then_inc(s["c_in"], 16)
            sp.dma_start(gate_b[:], gate_b_d.partition_broadcast(P)).then_inc(s["c_in"], 16)
            sp.dma_start(out_b[:], out_b_d.partition_broadcast(P)).then_inc(s["c_in"], 16)
            sp.wait_ge(s["zero_ready"], 1)
            half = slot_in.rearrange("(a p r) d -> a p (r d)", a=2, p=P)
            for a in range(2):
                sp.dma_start(half[a], HB[:].rearrange("p i n -> p (i n)")).then_inc(s["zeroed"], 16)
            sp.dma_start(WG[:], wg_d).then_inc(s["l1_in"], 16)
            sp.dma_start(MW1[:], mw1_d.rearrange("e p h -> p e h")).then_inc(s["l1_in"], 16)
            sp.dma_start(MW2[:], mw2_d.rearrange("e (c p) d -> p e c d", p=P)).then_inc(s["l1_in"], 16)
            sp.dma_start(MB2[:], mb2_d).then_inc(s["l1_in"], 16)

            def load_up(m, i):
                sp.dma_start(ring_w1[i], w1_d[bass.ds(2 * m, 2)].rearrange("e p h -> p e h")).then_inc(ring_in_a[i], 16)
                for e in range(2):
                    rows = slice(CAP * e, CAP * e + CAP)
                    sp.dma_start(ring_b1[i][rows, :], b1_d[bass.ds(2 * m + e, 1)].rearrange("a n -> (a n)").partition_broadcast(CAP)
                                 ).then_inc(ring_in_a[i], 16)

            def load_down(m, i):
                sp.dma_start(ring_w2[i].rearrange("p e c d -> p e (c d)"),
                             w2_d[bass.ds(2 * m, 2)].rearrange("e (p c) d -> p e (c d)", c=HC0)).then_inc(ring_in_b[i], 16)
                for e in range(2):
                    rows = slice(CAP * e, CAP * e + CAP)
                    sp.dma_start(ring_b2[rows, i, :], b2_d[bass.ds(2 * m + e, 1)].rearrange("a n -> (a n)").partition_broadcast(CAP)
                                 ).then_inc(ring_in_b[i], 16)

            def load_slots(m, i):
                sp.dma_start(ring_in[i], slot_in[bass.ds(P * m, P)]).then_inc(ring_in_x[i], 16)

            def store_y(G, h):
                sp.wait_ge(s["y_sb"], 2 * G + h + 1)
                sp.dma_start(slot_out[bass.ds(P * (RING * G + 2 * h), 2 * P)].rearrange("(a p) d -> p a d", p=P),
                             Y[:, h]).then_inc(y_out[h], 16)

            sp.wait_ge(s["slots_ready"], 1)
            sp.wait_ge(s["base_done"], 2)
            for i in range(RING):
                load_up(i, i)
                load_down(i, i)
            sp.wait_ge(s["scattered"], 16 * TOPK * NT)
            for i in range(RING):
                load_slots(i, i)
            with sp.Fori(0, NPAIR // RING - 1) as G:
                sp.wait_ge(s["bt_ps"], G + 1)
                for i in range(RING):
                    load_slots(RING * G + (RING + i), i)
                for i in range(RING):
                    sp.wait_ge(s["h_sb"], RING * G + (i + 1))
                    load_up(RING * G + (RING + i), i)
                for h in range(2):
                    store_y(G, h)
                    for i in (2 * h, 2 * h + 1):
                        load_down(RING * G + (RING + i), i)
            for h in range(2):
                store_y(NPAIR // RING - 1, h)
            for c in range(NC):
                sp.wait_ge(s["acc_done"], E1 * (c + 1))
                sp.dma_start(out_v[:, CH * c:CH * c + CH, :], BASE[:, CH * c:CH * c + CH, :]).then_inc(out_done[c % 2], 16)
            for a in range(2):
                sp.wait_ge(out_done[a], 16 * NC // 2)

        @block.gpsimd
        def _(pool):
            link = chain(pool, "pool_chain")
            g = nc.gpsimd
            link(g.memset(ident[:], 0.0))
            g.affine_select(out=ident[:], in_=ident[:], compare_op=ALU.not_equal, fill=1.0, base=0,
                            pattern=[[-1, P]], channel_multiplier=1).then_inc(s["const_ready"], 1)
            g.memset(HB[:], 0.0).then_inc(s["zero_ready"], 1)
            link(g.memset(ident16[:], 0.0))
            g.affine_select(out=ident16[:], in_=ident16[:], compare_op=ALU.not_equal, fill=1.0, base=0,
                            pattern=[[-1, P]], channel_multiplier=1)
            g.memset(ones[:], 1.0)
            link(g.memset(before[:], 1.0))
            g.affine_select(out=before[:], in_=before[:], compare_op=ALU.is_gt, fill=0.0, base=0,
                            pattern=[[1, P]], channel_multiplier=-1)
            g.iota(iota_e[:], [[1, E0]], base=0, channel_multiplier=0, allow_small_or_imprecise_dtypes=True)
            link(g.memset(VA, 0.0))
            g.memset(VA[:, :, :, HD:HD + 1], 1.0)
            g.memset(QST, 0.0).then_inc(s["const_ready"], 1)
            pool.wait_ge(s["xn_ready"], 1)
            pool.wait_ge(s["c_in"], 64)
            g.tensor_tensor(BASE[:], X, XN[:], ALU.add).then_inc(s["base_done"], 1)
            pool.wait_ge(s["base_done"], 1)
            g.tensor_tensor(BASE[:], BASE[:], out_b[:].unsqueeze(1).to_broadcast([P, NT, D]), ALU.add).then_inc(s["base_done"], 1)
            for c in range(NC):
                pool.wait_ge(s["hi_ready"], c + 1)
                qa = QKA[:, 0, CH * c:CH * c + CH, :].rearrange("p t (h d) -> p (t h) d", d=HD)
                g.tensor_tensor(QS[:, :, 2:4, :], qa.unsqueeze(2).to_broadcast([P, CH * HEADS, 2, HD]), QS[:, :, 0:2, :],
                                ALU.subtract).then_inc(s["lo_q"], 1)
            pool.wait_ge(s["zeroed"], 32)
            pool.wait_ge(s["slots_ready"], 1)
            for k in range(TOPK):
                for t in range(NT):
                    g.indirect_dma_start(slot_in, bass.IndirectOffsetOnAxis(SLS[:, k, t:t + 1], 0), XN[:, t, :], None,
                                         bounds_check=SLOTS - 1, oob_is_err=False).then_inc(s["scattered"], 16)
            for h in range(2):
                pool.wait_ge(y_out[h], 16 * (NPAIR // RING))
            pool.wait_ge(s["staged"], NG)
            for c in range(NC):
                for t in range(CH * c, CH * c + CH):
                    for k in range(TOPK):
                        g.indirect_dma_start(YG[:, t, k, :], None, slot_out, bass.IndirectOffsetOnAxis(SLG[:, k, t:t + 1], 0),
                                             bounds_check=SLOTS - 1, oob_is_err=True).then_inc(gathered[c], 16)
            for c in range(NC):
                pool.wait_ge(s["d_ready"], 4 * c + 1)
                if c:
                    pool.wait_ge(s["rw_ready"], c)
                g.tensor_tensor(D2, KX, PP[:, 1:BLK + 1], ALU.subtract).then_inc(s["pool_wkv"], 1)
                pool.wait_ge(s["d_ready"], 4 * c + 3)
                g.tensor_tensor(F1, PP[:, 0:BLK], PM, ALU.subtract).then_inc(s["pool_wkv"], 1)
                pool.wait_ge(s["d_exp"], 4 * c + 2)
                g.tensor_tensor(EV, D2, VX, ALU.mult).then_inc(s["pool_wkv"], 1)
                pool.wait_ge(s["d_exp"], 4 * c + 4)
                g.tensor_tensor(T1, F2, VX, ALU.mult).then_inc(s["pool_wkv"], 1)

        @block.scalar
        def _(act):
            a = nc.scalar
            for dst, src in ((WL[:, 0:3], qkv_w_d.rearrange("(j p) d -> p j d", p=P)), (WL[:, 3], out_w_d),
                             (WL[:, 4:7], rvk_w_d.rearrange("(j p) d -> p j d", p=P)), (WL[:, 7], rout_w_d),
                             (SMALL[0:16], mb1_d.rearrange("e (c p) -> (e c) p", p=P)),
                             (SMALL[16:17], ln_w_d.unsqueeze(0)), (SMALL[17:18], ln_b_d.unsqueeze(0)),
                             (SMALL[18:19], decay_d.unsqueeze(0)), (SMALL[19:20], first_d.unsqueeze(0))):
                act.dma_start(dst, src).then_inc(s["w_in"], 16)
            for i, (dst, n) in enumerate(((WT[:, 0:4].rearrange("p j n -> p (j n)"), 512),
                                          (WT[:, 4:8].rearrange("p j n -> p (j n)"), 512), (COL[:], 20))):
                act.wait_ge(s["wt_ps"], i + 1)
                a.activation(dst, ps[4 + i][:, 0:n], ACT.Copy).then_inc(s["wt_sb"], 1)
            for i in range(2):
                act.wait_ge(s["var_ready"], i + 1)
                a.activation(SD[:], MV[:, :, 1], ACT.Sqrt).then_inc(s["std_ready"], 1)
            act.wait_ge(s["wt_sb"], 3)
            for c in range(NC):
                act.wait_ge(s["xnt_ps"], c + 1)
                if c >= 2:
                    act.wait_ge(s["lg_ps"], c - 1)
                a.activation(XNT[:, c % 2], ps[c % 2][:], ACT.Copy).then_inc(s["xnt_sb"], 1)
                act.wait_ge(s["hnt_ps"], c + 1)
                if c >= 2:
                    act.wait_ge(s["qkv_ps"], CH * (c - 1))
                a.activation(HT[:, c % 2], ps[2 + c % 2][:], ACT.Identity, bias=LNB, scale=LNW).then_inc(s["ht_sb"], 1)
            for c in range(NC):
                chunk = slice(CH * c, CH * c + CH)
                act.wait_ge(s["qkv_sb"], CH * (c + 1))
                if c:
                    act.wait_ge(s["nq_ready"], c)
                a.activation(TMP.rearrange("p (s n) -> p s n", s=2), QKA[:, :, chunk, :].rearrange("p s t d -> p s (t d)"),
                             ACT.Square).then_inc(s["sq_ready"], 1)
                act.wait_ge(s["nq_ready"], c + 1)
                a.activation(NS[:], NQ[:], ACT.Sqrt).then_inc(s["ns_ready"], 1)
                act.wait_ge(s["qn_ready"], c + 1)
                for si, dst, where in ((1, KS, slice(0, 4, 2)), (0, QS, slice(0, 2))):
                    if c:
                        act.wait_ge(s["kt_ps" if si else "qt_ps"], c)
                    src = QKA[:, si, chunk, :].rearrange("p t (h d) -> p (t h) d", d=HD)
                    last = a.activation(dst[:, :, where, :], src.unsqueeze(2).to_broadcast([P, CH * HEADS, 2, HD]), ACT.Copy)
                last.then_inc(s["hi_ready"], 1)
                act.wait_ge(s["kt_ps"], c + 1)
                a.activation(KT[:, :, BLK * c:BLK * c + BLK], S[:, 0:2].rearrange("p b n -> p (b n)").bitcast(F16)
                             .rearrange("p (g n) -> p g n", g=NHG), ACT.Copy).then_inc(s["kt_sb"], 1)
            a.activation(WDEC[:], DECAY, ACT.Exp).then_inc(s["decay_exp"], 1)

            def exps(n, first=False):
                for h in range(2):
                    act.wait_ge(s["qk_ready"], 2 * n + (h + 1))
                    if not first and h == 0:
                        act.wait_ge(s["av_done"], n - 1)
                    a.activation(PR[:, par[0], 2 * h:2 * h + 2, :], S[:, 2 * h:2 * h + 2, :], ACT.Exp, scale=SCALE
                                 ).then_inc(s["exp_done"], 1)
                par[0] ^= 1

            par = [0]

            def gelus(G):
                for i in range(RING):
                    act.wait_ge(s["h_sb"], RING * G + (i + 1))
                    a.activation(HB[:, i], HB[:, i], ACT.Gelu).then_inc(s["gelu_done"], 1)

            def group(g0, n0, G=None):
                for st in range(KT_TILES):
                    exps(n0 + st)
                    if st == 4 and G is not None:
                        gelus(G)

            for n in range(KT_TILES):
                exps(n, first=n < 2)
                if n == 6:
                    act.wait_ge(s["top_ready"], 1)
                    a.activation(GE[:], GE[:], ACT.Exp).then_inc(s["gexp_ready"], 1)
            with act.Fori(1, MOE_FROM) as gi:
                group(gi, KT_TILES * gi)
            with act.Fori(0, NG - MOE_FROM) as G:
                group(None, KT_TILES * G + KT_TILES * MOE_FROM, G)

            def sqrt2(c):
                act.wait_ge(s["var2_ready"], c + 1)
                a.activation(SD[:, 0:CH], MV[:, 0:CH, 1], ACT.Sqrt).then_inc(s["std2_ready"], 1)

            def before_norm(c):
                act.wait_ge(s["ot_ps"], c + 1)
                if c:
                    act.wait_ge(s["x1_ps"], c)
                a.activation(OTT, ps[6][:], ACT.Copy).then_inc(s["ot_sb"], 1)

            def after_norm(c):
                act.wait_ge(s["xn2t_ps"], c + 1)
                if c >= 2:
                    act.wait_ge(s["up2"], E1 * HC1 * (c - 1))
                a.activation(XN2T[:, c % 2], ps[6][:], ACT.Copy).then_inc(s["xn2t_sb"], 1)

            def rvk(c):
                if c:
                    act.wait_ge(s["rw_ready"], c)
                act.wait_ge(s["rvk_ps"], 3 * c + 1)
                a.activation(KX, ps[6][:], ACT.Copy).then_inc(s["rvk_sb"], 1)
                act.wait_ge(s["rvk_ps"], 3 * c + 2)
                a.activation(VX, ps[7][:], ACT.Copy).then_inc(s["rvk_sb"], 1)
                act.wait_ge(s["l8_ready"], c + 1)
                a.activation(P8[:], L8[:], ACT.Exp).then_inc(s["p8_exp"], 1)
                act.wait_ge(s["rvk_ps"], 3 * c + 3)
                a.activation(ER, ps[6][:], ACT.Exp, scale=-1.0).then_inc(s["rvk_sb"], 1)

            def gates_cols(c):
                act.wait_ge(s["gt_ps"], c + 1)
                a.activation(GTT[0:E1, c % 2], ps[7][0:E1], ACT.Copy).then_inc(s["gt_sb"], 1)

            def wkv_exps(c):
                act.wait_ge(s["d_ready"], 4 * c + 2)
                a.activation(D1, D1, ACT.Exp).then_inc(s["d_exp"], 1)
                act.wait_ge(s["pool_wkv"], 4 * c + 1)
                a.activation(D2, D2, ACT.Exp).then_inc(s["d_exp"], 1)
                act.wait_ge(s["pool_wkv"], 4 * c + 2)
                a.activation(F1, F1, ACT.Exp).then_inc(s["d_exp"], 1)
                act.wait_ge(s["d_ready"], 4 * c + 4)
                a.activation(F2, F2, ACT.Exp).then_inc(s["d_exp"], 1)

            def relus(c, e):
                for k in range(HC1):
                    n = HC1 * (E1 * c + e) + k
                    act.wait_ge(s["up2"], n + 1)
                    if E1 * c + e >= 2 and k == 0:
                        act.wait_ge(s["down2"], E1 * c + e - 1)
                    a.activation(HS[:, e % 2, k], ps[2 * (e % 2) + k][:], ACT.Relu, bias=COL[:, HC1 * e + k:HC1 * e + k + 1]
                                 ).then_inc(s["relu_done"], 1)

            before_norm(0)
            sqrt2(0)
            after_norm(0)
            rvk(0)
            gates_cols(0)
            for c in range(NC):
                for e in range(E1):
                    relus(c, e)
                    if e == 0:
                        wkv_exps(c)
                    if c + 1 < NC:
                        if e == 2:
                            before_norm(c + 1)
                            sqrt2(c + 1)
                        if e == 4:
                            after_norm(c + 1)
                        if e == 6:
                            rvk(c + 1)
                        if e == 7:
                            gates_cols(c + 1)

        @block.vector
        def _(dve):
            link = chain(dve, "dve_chain")
            v = nc.vector

            def normalise(src, dst, i, waits=False):
                for t in range(NT):
                    if waits and t % CH == 0:
                        dve.wait_ge(x_in[t // CH], 16)
                    last = v.bn_stats(ST[:, t, :], src[:, t, :])
                link(last)
                for t in range(NT):
                    last = v.bn_aggr(MV[:, t, :], ST[:, t, :])
                link(last)
                v.tensor_scalar(MV[:, :, 1], MV[:, :, 1], LN_EPS, None, ALU.add).then_inc(s["var_ready"], 1)
                dve.wait_ge(s["std_ready"], i + 1)
                link(v.reciprocal(RS[:], SD[:]))
                for t in range(NT):
                    last = v.tensor_scalar(dst[:, t, :], src[:, t, :], MV[:, t, 0:1], RS[:, t:t + 1], ALU.subtract, ALU.mult)
                    if dst is HN and t % CH == CH - 1:
                        last.then_inc(s["hn_ready"], 1)
                if dst is not HN:
                    last.then_inc(s["xn_ready"], 1)
                    dve.wait_ge(s["xn_ready"], 1)

            normalise(X, XN, 0, waits=True)
            normalise(XN, HN, 1)

            dve.wait_ge(s["c_in"], 64)
            dve.wait_ge(s["const_ready"], 2)
            for c in range(NC):
                for t in range(CH * c, CH * c + CH):
                    dve.wait_ge(s["qkv_ps"], t + 1)
                    q = ps[4 + t % 3]
                    v.tensor_tensor(QKA[:, :, t, :], q[:, 0:2 * D].rearrange("p (s d) -> p s d", s=2),
                                    qkv_b[:, 0:2 * D].rearrange("p (s d) -> p s d", s=2), ALU.add)
                    v.tensor_tensor(VA[:, t, :, 0:HD], q[:, 2 * D:3 * D].rearrange("p (h d) -> p h d", d=HD),
                                    qkv_b[:, 2 * D:3 * D].rearrange("p (h d) -> p h d", d=HD), ALU.add).then_inc(s["qkv_sb"], 1)
                dve.wait_ge(s["lg_ps"], c + 1)
                v.tensor_tensor(LG[:, CH * c:CH * c + CH, :], ps[7][:, 0:CH * E0].rearrange("p (t e) -> p t e", e=E0),
                                gate_b[:].unsqueeze(1).to_broadcast([P, CH, E0]), ALU.add).then_inc(s["lg_sb"], 1)
            for c in range(NC):
                chunk = slice(CH * c, CH * c + CH)
                dve.wait_ge(s["sq_ready"], c + 1)
                if c:
                    dve.wait_ge(s["ns_ready"], c)
                v.tensor_reduce(NQ[:], TMP.rearrange("p (n d) -> p n d", d=HD), AX, ALU.add).then_inc(s["nq_ready"], 1)
                dve.wait_ge(s["ns_ready"], c + 1)
                link(v.tensor_scalar(NS[:], NS[:], NORM_EPS, None, ALU.max))
                link(v.reciprocal(NS[:], NS[:]))
                for si in range(2):
                    qk = QKA[:, si, chunk, :].rearrange("p t (h d) -> p (t h) d", d=HD)
                    n = NS[:, 64 * si:64 * si + 64].unsqueeze(2).to_broadcast([P, CH * HEADS, HD])
                    last = v.tensor_tensor(qk, qk, n, ALU.mult)
                last.then_inc(s["qn_ready"], 1)
                dve.wait_ge(s["hi_ready"], c + 1)
                ka = QKA[:, 1, chunk, :].rearrange("p t (h d) -> p (t h) d", d=HD)
                v.tensor_tensor(KS[:, :, 1:4:2, :], ka.unsqueeze(2).to_broadcast([P, CH * HEADS, 2, HD]), KS[:, :, 0:4:2, :],
                                ALU.subtract).then_inc(s["lo_k"], 1)
                dve.wait_ge(s["qt_ps"], c + 1)
                v.tensor_copy(QT[:, :, BLK * c:BLK * c + BLK], S[:, 2:4].rearrange("p b n -> p (b n)").bitcast(F16)
                              .rearrange("p (g n) -> p g n", g=NHG)).then_inc(s["qt_sb"], 1)

            def stage(g):
                c, hg, a = g // NHG, g % NHG, g % 2
                b = c * BLK // N
                if g >= 2:
                    dve.wait_ge(s["qk_ready"], 2 * KT_TILES * (g - 1))
                    dve.wait_ge(s["av_done"], KT_TILES * (g - 1))
                v.tensor_copy(KST[:, a], KT[:, hg, N * b:N * b + N])
                for j in range(HG):
                    rows = slice(32 * j, 32 * j + 32)
                    v.tensor_copy(QST[rows, a, j, :], QT[rows, hg, BLK * c:BLK * c + BLK])
                v.tensor_copy(VST[:, a].rearrange("p s j w -> p s (j w)"),
                              VA[:, KT_TILES * b:KT_TILES * (b + 1), HG * hg:HG * hg + HG, :].rearrange("p t h w -> p t (h w)")
                              ).then_inc(s["staged"], 1)

            def evacuate(g):
                dve.wait_ge(s["av_done"], KT_TILES * (g + 1))
                if g >= 2:
                    dve.wait_ge(s["ep_ps"], g - 1)
                v.tensor_copy(OTs[:, g % 2], AV[:]).then_inc(s["a_evac"], 1)

            def divide(g):
                dve.wait_ge(s["ep_ps"], g + 1)
                o = ps[7][:].rearrange("p (t j w) -> p t j w", t=CH, w=32)
                sums = NQ[:, 0:CH * HG].rearrange("p (t j) -> p t j", t=CH)
                link(v.reciprocal(sums, o[:, :, :, HD]))
                for t in range(CH):
                    last = v.tensor_tensor(OH[:, g // NHG, t, g % NHG, :].rearrange("p (j d) -> p j d", d=HD), o[:, t, :, 0:HD],
                                           sums[:, t, :].unsqueeze(2).to_broadcast([P, HG, HD]), ALU.mult)
                last.then_inc(s["ep_used"], 1)

            dve.wait_ge(s["kt_sb"], NC)
            stage(0)
            stage(1)

            for t in range(NT):
                last = v.max(MX[:, t, :], LG[:, t, :])
            link(last)
            for t in range(NT):
                last = v.max_index(IX[:, t, :], MX[:, t, :], LG[:, t, :])
            link(last)
            v.tensor_tensor(GE[:], MX[:, :, 0:TOPK], MX[:, :, 0:1].to_broadcast([P, NT, TOPK]), ALU.subtract
                            ).then_inc(s["top_ready"], 1)
            link(v.tensor_copy(IXF[:], IX[:, :, 0:TOPK]))
            for k in range(TOPK):
                last = v.tensor_tensor(EQ[:, k], iota_e[:].unsqueeze(1).to_broadcast([P, NT, E0]),
                                       IXF[:, :, k:k + 1].to_broadcast([P, NT, E0]), ALU.is_equal)
            link(last)
            link(v.tensor_tensor(MH[:], EQ[:, 0], EQ[:, 1], ALU.add))
            link(v.tensor_tensor(MH[:], MH[:], EQ[:, 2], ALU.add))
            link(v.memset(MPRE[:, 0, :], 0.0))
            for t in range(1, NT):
                last = v.tensor_tensor(MPRE[:, t, :], MPRE[:, t - 1, :], MH[:, t - 1, :], ALU.add)
                if t < NT - 1:
                    link(last)
            last.then_inc(s["mask_ready"], 1)
            dve.wait_ge(s["gexp_ready"], 1)
            link(v.tensor_reduce(GS[:], GE[:], AX, ALU.add))
            link(v.reciprocal(GS[:], GS[:]))
            link(v.tensor_tensor(GE[:], GE[:], GS[:].unsqueeze(2).to_broadcast([P, NT, TOPK]), ALU.mult))

            def slots():
                dve.wait_ge(s["count_ready"], 1)
                tmp = TMP.rearrange("p (t e) -> p t e", e=E0)
                for k in range(TOPK):
                    for h in range(2):
                        rows = slice(NT // 2 * h, NT // 2 * (h + 1))
                        last = v.tensor_tensor(tmp[:, rows, :], ps[5 + h][:].rearrange("p (t e) -> p t e", e=E0), EQ[:, k, rows, :], ALU.mult)
                    link(last)
                    link(v.tensor_reduce(POS[:, k, :], tmp, AX, ALU.add))
                link(v.tensor_scalar(VAL[:], POS[:], float(CAP), None, ALU.is_lt))
                link(v.tensor_scalar(SLF[:], POS[:], float(CAP - 1), None, ALU.min))
                ix = IXF[:].rearrange("p t k -> p k t")
                link(v.scalar_tensor_tensor(SLF[:], ix, float(CAP), SLF[:], ALU.mult, ALU.add))
                link(v.tensor_copy(SLG[:], SLF[:]))
                link(v.tensor_scalar(POS[:], POS[:], float(CAP), float(2 * SLOTS), ALU.is_ge, ALU.mult))
                link(v.tensor_tensor(SLF[:], SLF[:], POS[:], ALU.add))
                link(v.tensor_copy(SLS[:], SLF[:]))
                v.tensor_tensor(GE[:], GE[:], VAL[:].rearrange("p k t -> p t k"), ALU.mult).then_inc(s["slots_ready"], 1)

            def moe_in(G):
                dve.wait_ge(s["bt_ps"], G + 1)
                if G:
                    dve.wait_ge(s["up_done"], RING * G)
                v.tensor_copy(BT[:], ps[6][:]).then_inc(s["bt_sb"], 1)

            def moe_h(G, i):
                dve.wait_ge(s["up_done"], RING * G + i + 1)
                if G:
                    dve.wait_ge(s["htr_ps"], RING * (G - 1) + i + 1)
                dve.wait_ge(ring_in_a[i], 48 * (G + 1))
                v.tensor_tensor(HB[:, i], ps[5 + i % 2][:], ring_b1[i], ALU.add).then_inc(s["h_sb"], 1)

            def moe_out(G):
                for h in range(2):
                    for i in (2 * h, 2 * h + 1):
                        n = RING * G + i
                        dve.wait_ge(s["htr_ps"], n + 1)
                        if i == 0 and G:
                            dve.wait_ge(s["down_done"], 2 * G)
                        if i == 2:
                            dve.wait_ge(s["down_done"], 2 * G + 1)
                        v.tensor_copy(HTS[:, i % 2], ps[5 + i % 2][:]).then_inc(s["htr_sb"], 1)
                        if i == 2:
                            moe_y(G, 0)
                moe_y(G, 1)

            def moe_y(G, h):
                dve.wait_ge(s["down_done"], 2 * G + h + 1)
                if G:
                    dve.wait_ge(y_out[h], 16 * G)
                for i in (2 * h, 2 * h + 1):
                    dve.wait_ge(ring_in_b[i], 48 * (G + 1))
                v.tensor_tensor(Y[:, h], ps[7][:, 0:2 * D].rearrange("p (a d) -> p a d", d=D), ring_b2[:, 2 * h:2 * h + 2, :],
                                ALU.add).then_inc(s["y_sb"], 1)

            for g in range(1, NG):
                G = g - MOE_FROM
                evacuate(g - 1)
                if G >= 0:
                    moe_in(G)
                if g + 1 < NG:
                    stage(g + 1)
                if G >= 0:
                    moe_h(G, 0)
                divide(g - 1)
                if G >= 0:
                    for i in range(1, RING):
                        moe_h(G, i)
                    moe_out(G)
                if g == 1:
                    slots()
            evacuate(NG - 1)
            divide(NG - 1)

            def combine(c):
                dve.wait_ge(gathered[c], 16 * TOPK * CH)
                for k in range(TOPK):
                    for t in range(CH * c, CH * c + CH):
                        last = v.scalar_tensor_tensor(BASE[:, t, :], YG[:, t, k, :], GE[:, t, k:k + 1], BASE[:, t, :], ALU.mult, ALU.add)
                    link(last)

            def x1_norm(c):
                chunk = slice(CH * c, CH * c + CH)
                dve.wait_ge(s["x1_ps"], c + 1)
                xs = BASE[:, chunk, :]
                v.tensor_tensor(xs, xs, ps[7][:].rearrange("p (t d) -> p t d", d=D), ALU.add).then_inc(s["x1_sb"], 1)
                dve.wait_ge(s["x1_sb"], c + 1)
                for t in range(CH):
                    last = v.bn_stats(ST[:, t, :], BASE[:, CH * c + t, :])
                link(last)
                for t in range(CH):
                    last = v.bn_aggr(MV[:, t, :], ST[:, t, :])
                link(last)
                v.tensor_scalar(MV[:, 0:CH, 1], MV[:, 0:CH, 1], LN_EPS, None, ALU.add).then_inc(s["var2_ready"], 1)
                dve.wait_ge(s["std2_ready"], c + 1)
                link(v.reciprocal(RS[:, 0:CH], SD[:, 0:CH]))
                if c:
                    dve.wait_ge(s["xn2t_ps"], c)
                for t in range(CH):
                    last = v.tensor_scalar(XN2[:, t, :], BASE[:, CH * c + t, :], MV[:, t, 0:1], RS[:, t:t + 1], ALU.subtract, ALU.mult)
                last.then_inc(s["xn2_ready"], 1)

            def gates(c):
                dve.wait_ge(s["lg2_ps"], c + 1)
                lg = ps[7][:, 0:CH * E1].rearrange("p (t e) -> p t e", e=E1)
                link(v.tensor_reduce(S4[:], lg, AX, ALU.max))
                v.tensor_tensor(L8[:], lg, S4[:].unsqueeze(2).to_broadcast([P, CH, E1]), ALU.subtract).then_inc(s["l8_ready"], 1)
                dve.wait_ge(s["p8_exp"], c + 1)
                link(v.tensor_reduce(S4[:], P8[:], AX, ALU.add))
                link(v.reciprocal(S4[:], S4[:]))
                link(v.tensor_tensor(P8[:], P8[:], S4[:].unsqueeze(2).to_broadcast([P, CH, E1]), ALU.mult))
                for t in range(CH):
                    last = v.max(M8[:, t, :], P8[:, t, :])
                link(last)
                for t in range(CH):
                    last = v.max_index(I8[:, t, :], M8[:, t, :], P8[:, t, :])
                link(last)
                link(v.tensor_copy(I8F[:], I8[:, :, 0:2]))
                g8 = G8[:, c % 2]
                iota = iota_e[:, 0:E1].unsqueeze(1).to_broadcast([P, CH, E1])
                v.tensor_tensor(g8, iota, I8F[:, :, 0:1].to_broadcast([P, CH, E1]), ALU.is_equal)
                link(v.tensor_tensor(L8[:], iota, I8F[:, :, 1:2].to_broadcast([P, CH, E1]), ALU.is_equal))
                link(v.tensor_tensor(g8, g8, L8[:], ALU.add))
                v.tensor_tensor(g8, g8, P8[:], ALU.mult).then_inc(s["g_ready"], 1)

            def time_mix(c):
                scan = v.tensor_tensor_scan
                dve.wait_ge(s["rvk_sb"], 3 * c + 3)
                for st, first in ((PP, NEG_BIG), (AA, 0.0), (BB, 0.0)):
                    if (c * BLK) % N == 0:
                        last = v.memset(st[:, 0:1], first)
                    else:
                        last = v.tensor_copy(st[:, 0:1], st[:, BLK:BLK + 1])
                link(last)
                now, new = slice(0, BLK), slice(1, BLK + 1)
                scan(PP[:, new], NEGW[:].to_broadcast([P, BLK]), KX, PP[:, 0:1], ALU.add, ALU.max).then_inc(s["d_ready"], 1)
                dve.wait_ge(s["d_ready"], 4 * c + 1)
                v.scalar_tensor_tensor(D1, PP[:, now], NEGW[:], PP[:, new], ALU.add, ALU.subtract).then_inc(s["d_ready"], 1)
                v.scalar_tensor_tensor(PM, KX, FIRST, PP[:, now], ALU.add, ALU.max).then_inc(s["d_ready"], 1)
                dve.wait_ge(s["d_ready"], 4 * c + 3)
                v.scalar_tensor_tensor(F2, KX, FIRST, PM, ALU.add, ALU.subtract).then_inc(s["d_ready"], 1)

            def time_mix_out(c):
                scan = v.tensor_tensor_scan
                now, new = slice(0, BLK), slice(1, BLK + 1)
                dve.wait_ge(s["d_exp"], 4 * c + 2)
                scan(BB[:, new], D1, D2, BB[:, 0:1], ALU.mult, ALU.add)
                dve.wait_ge(s["pool_wkv"], 4 * c + 3)
                link(scan(AA[:, new], D1, EV, AA[:, 0:1], ALU.mult, ALU.add))
                dve.wait_ge(s["d_exp"], 4 * c + 4)
                v.tensor_tensor(NU, F1, AA[:, now], ALU.mult)
                link(v.tensor_tensor(DE, F1, BB[:, now], ALU.mult))
                link(v.tensor_tensor(DE, DE, F2, ALU.add))
                dve.wait_ge(s["pool_wkv"], 4 * c + 4)
                v.tensor_tensor(NU, NU, T1, ALU.add)
                link(v.scalar_tensor_tensor(DE, ER, 1.0, DE, ALU.add, ALU.mult))
                link(v.reciprocal(DE, DE))
                if c >= 2:
                    dve.wait_ge(s["fin_ps"], c - 1)
                v.tensor_tensor(RWT[c % 2], NU, DE, ALU.mult).then_inc(s["rw_ready"], 1)

            def accumulate(c, e):
                dve.wait_ge(s["down2"], E1 * c + e + 1)
                for t in range(CH):
                    y = BASE[:, CH * c + t, :]
                    last = v.scalar_tensor_tensor(y, ps[4 + e % 2][:, D * t:D * t + D], G8[:, c % 2, t, e:e + 1], y, ALU.mult, ALU.add)
                last.then_inc(s["acc_done"], 1)
                dve.wait_ge(s["acc_done"], E1 * c + e + 1)

            def mixed(c):
                dve.wait_ge(s["fin_ps"], c + 1)
                xs = BASE[:, CH * c:CH * c + CH, :]
                v.tensor_tensor(xs, xs, ps[6][:].rearrange("p (t d) -> p t d", d=D), ALU.add).then_inc(s["fin_sb"], 1)
                dve.wait_ge(s["fin_sb"], c + 1)

            dve.wait_ge(s["decay_exp"], 1)
            link(v.tensor_scalar(NEGW[:], WDEC[:], -1.0, None, ALU.mult))
            combine(0)
            x1_norm(0)
            gates(0)
            for c in range(NC):
                time_mix(c)
                for e in range(E1):
                    accumulate(c, e)
                    if e == 0:
                        time_mix_out(c)
                    if e == 2:
                        mixed(c)
                    if c + 1 < NC:
                        if e == 1:
                            combine(c + 1)
                        if e == 2:
                            x1_norm(c + 1)
                        if e == 5:
                            gates(c + 1)

        @block.tensor
        def _(pe):
            mm, tr = nc.tensor.matmul, nc.tensor.transpose
            pe.wait_ge(s["const_ready"], 1)
            pe.wait_ge(s["w_in"], 16 * 9)
            for i in range(2):
                for j in range(4):
                    last = tr(ps[4 + i][:, P * j:P * j + P], WL[:, 4 * i + j, :], ident[:])
                last.then_inc(s["wt_ps"], 1)
            tr(ps[6][:, 0:20], SMALL[:], ident[0:20, 0:20]).then_inc(s["wt_ps"], 1)

            def turn(c):
                for src, bank, done, freed in ((XN, c % 2, "xnt_ps", "xnt_sb"), (HN, 2 + c % 2, "hnt_ps", "ht_sb")):
                    if src is HN:
                        pe.wait_ge(s["hn_ready"], c + 1)
                    if c >= 2:
                        pe.wait_ge(s[freed], c - 1)
                    for j in range(CH):
                        last = tr(ps[bank][:, P * j:P * j + P], src[:, CH * c + j, :], ident[:])
                    last.then_inc(s[done], 1)

            def project(c):
                pe.wait_ge(s["ht_sb"], c + 1)
                for j in range(CH):
                    t = CH * c + j
                    if t >= 3:
                        pe.wait_ge(s["qkv_sb"], t - 2)
                    mm(ps[4 + t % 3][:, 0:3 * D], HT[:, c % 2, P * j:P * j + P], WT[:, 0:3].rearrange("p j n -> p (j n)"),
                       start=True, stop=True).then_inc(s["qkv_ps"], 1)
                pe.wait_ge(s["xnt_sb"], c + 1)
                if c:
                    pe.wait_ge(s["lg_sb"], c)
                for j in range(CH):
                    last = mm(ps[7][:, E0 * j:E0 * j + E0], XNT[:, c % 2, P * j:P * j + P], gate_w[:], start=True, stop=True)
                last.then_inc(s["lg_ps"], 1)

            pe.wait_ge(s["xn_ready"], 1)
            pe.wait_ge(s["wt_sb"], 3)
            pe.wait_ge(s["c_in"], 64)
            turn(0)
            for c in range(NC):
                if c + 1 < NC:
                    turn(c + 1)
                project(c)

            pe.wait_ge(s["const_ready"], 2)
            pe.wait_ge(s["ht_sb"], NC)
            for c in range(NC):
                for src, bank, lo, ready, done, freed in ((KS, 0, "lo_k", "hi_ready", "kt_ps", "kt_sb"),
                                                          (QS, 2, "lo_q", "hi_ready", "qt_ps", "qt_sb")):
                    pe.wait_ge(s[ready], c + 1)
                    pe.wait_ge(s[lo], c + 1)
                    if c:
                        pe.wait_ge(s[freed], c)
                    cols = src.rearrange("p (t g j) w d -> p t g (j w d)", t=CH, g=NHG)
                    for g in range(NHG):
                        dst = S[:, bank + g // 2].bitcast(F16).rearrange("p (g t n) -> p g t n", g=2, t=CH)
                        for t in range(CH):
                            last = tr(dst[:, g % 2, t, :], cols[:, t, g, :], ident16[:])
                    last.then_inc(s[done], 1)

            def scores(n, st, a, h, first=False, new=None):
                if new is not None:
                    pe.wait_ge(s["staged"], new)
                if not first:
                    pe.wait_ge(s["exp_done"], 2 * n + (h - 1))
                for j in (2 * h, 2 * h + 1):
                    last = mm(S[:, j], KST[:, a, P * st:P * st + P], QST[:, a, j, :], start=True, stop=True)
                last.then_inc(s["qk_ready"], 1)

            def values(n, st, a, half, g=None):
                if half == 0:
                    pe.wait_ge(s["exp_done"], 2 * n + 2)
                    if g is not None:
                        pe.wait_ge(s["a_evac"], g)
                cols = slice(BLK // 2 * half, BLK // 2 * (half + 1))
                for j in range(HG):
                    last = mm(AV[32 * j:32 * j + VW, cols], VST[:, a, st, j, :], PR[:, st % 2, j, cols],
                              start=(st == 0 and half == 0), stop=(st == KT_TILES - 1), skip_group_check=True)
                if half:
                    last.then_inc(s["av_done"], 1)

            def tokens_out(g, a, y=None):
                pe.wait_ge(s["a_evac"], g)
                if y is not None:
                    pe.wait_ge(s["y_sb"], y)
                for t in range(CH):
                    last = tr(ps[7][:, P * t:P * t + P], OTs[:, 1 - a, P * t:P * t + P], ident[:])
                last.then_inc(s["ep_ps"], 1)

            def slots_in(G, first):
                for i in range(RING):
                    pe.wait_ge(ring_in_x[i], 16 * G + 16)
                if not first:
                    pe.wait_ge(s["htr_sb"], RING * G)
                for i in range(RING):
                    last = tr(ps[6][:, P * i:P * i + P], ring_in[i], ident[:])
                last.then_inc(s["bt_ps"], 1)

            def up(G, i):
                pe.wait_ge(ring_in_a[i], 48 * G + 48)
                pe.wait_ge(s["bt_sb"], G + 1)
                if i >= 2:
                    pe.wait_ge(s["h_sb"], RING * G + (i - 1))
                if i == 0:
                    pe.wait_ge(s["bt_sb"], G + 1)
                for e in range(2):
                    last = mm(ps[5 + i % 2][CAP * e:CAP * e + CAP, :], BT[:, P * i + CAP * e:P * i + CAP * e + CAP], ring_w1[i][:, e, :],
                              start=True, stop=True)
                last.then_inc(s["up_done"], 1)

            def hidden(G, i):
                pe.wait_ge(s["gelu_done"], RING * G + (i + 1))
                if i < 2:
                    pe.wait_ge(s["h_sb"], RING * G + (i + 3))
                else:
                    pe.wait_ge(s["htr_sb"], RING * G + (i - 1))
                cols = HB[:, i].rearrange("p (m c) -> p c m", c=HC0)
                for c in range(HC0):
                    last = tr(ps[5 + i % 2][:, P * c:P * c + P], cols[:, c, :], ident[:])
                last.then_inc(s["htr_ps"], 1)

            def down(G, g, h):
                if h:
                    pe.wait_ge(s["y_sb"], 2 * G + 1)
                else:
                    pe.wait_ge(s["ep_used"], g)
                for i in (2 * h, 2 * h + 1):
                    pe.wait_ge(s["htr_sb"], RING * G + (i + 1))
                    pe.wait_ge(ring_in_b[i], 48 * G + 48)
                    for c in range(HC0):
                        for e in range(2):
                            last = mm(ps[7][CAP * e:CAP * e + CAP, D * (i % 2):D * (i % 2) + D],
                                      HTS[:, i % 2, P * c + CAP * e:P * c + CAP * e + CAP], ring_w2[i][:, e, c, :],
                                      start=(c == 0), stop=(c == HC0 - 1), skip_group_check=True)
                last.then_inc(s["down_done"], 1)

            def group(g, a, first=False, last=False, G=None, first_G=False):
                for st in range(KT_TILES):
                    n = KT_TILES * g + st
                    if st < KT_TILES - 1:
                        scores(n + 1, st + 1, a, 1)
                    elif not last:
                        scores(n + 1, 0, 1 - a, 1)
                    values(n, st, a, 0, g=g if st == 0 and not first else None)
                    if st < KT_TILES - 2:
                        scores(n + 2, st + 2, a, 0)
                    elif not last:
                        scores(n + 2, st + 2 - KT_TILES, 1 - a, 0, new=g + 2 if st == KT_TILES - 2 else None)
                    values(n, st, a, 1)
                    if st == 1 and not first:
                        if G is None:
                            tokens_out(g, a)
                        else:
                            tokens_out(g, a, y=None if first_G else 2 * G)
                    if G is not None:
                        if st == 0:
                            slots_in(G, first_G)
                        if st == 1:
                            up(G, 0)
                            up(G, 1)
                        if 2 <= st <= 3:
                            up(G, st)
                        if st == 5:
                            hidden(G, 0)
                            hidden(G, 1)
                        if st == 6:
                            down(G, g, 0)
                            hidden(G, 2)
                            hidden(G, 3)
                        if st == 7:
                            down(G, g, 1)

            pe.wait_ge(s["kt_sb"], NC)
            pe.wait_ge(s["qt_sb"], NC)
            pe.wait_ge(s["lg_sb"], NC)
            scores(0, 0, 0, 0, first=True, new=1)
            scores(0, 0, 0, 1, first=True)
            scores(1, 1, 0, 0)
            group(0, 0, first=True)
            group(1, 1)
            pe.wait_ge(s["mask_ready"], 1)
            for h in range(2):
                rows = slice(NT // 2 * h, NT // 2 * (h + 1))
                mm(ps[5 + h][:], before[:], MH[:, rows, :].rearrange("p t e -> p (t e)"), start=True, stop=False)
                last = mm(ps[5 + h][:], ones[:], MPRE[:, rows, :].rearrange("p t e -> p (t e)"), start=False, stop=True)
            last.then_inc(s["count_ready"], 1)
            with pe.Fori(1, MOE_FROM // 2) as i:
                group(2 * i, 0)
                group(2 * i + 1, 1)
            pe.wait_ge(s["slots_ready"], 1)
            group(MOE_FROM, 0, G=0, first_G=True)
            group(MOE_FROM + 1, 1, G=1)
            with pe.Fori(1, (NG - MOE_FROM) // 2 - 1) as i:
                group(2 * i + MOE_FROM, 0, G=2 * i)
                group(2 * i + (MOE_FROM + 1), 1, G=2 * i + 1)
            group(NG - 2, 0, G=NG - 2 - MOE_FROM)
            group(NG - 1, 1, last=True, G=NG - 1 - MOE_FROM)
            tokens_out(NG, 0, y=2 * (NG - MOE_FROM))

            def attention_out(c):
                pe.wait_ge(s["ep_used"], NHG * (c + 1))
                if c:
                    pe.wait_ge(s["xn2t_sb"], c)
                for t in range(CH):
                    last = tr(ps[6][:, P * t:P * t + P], OH[:, c, t].rearrange("p g w -> p (g w)"), ident[:])
                last.then_inc(s["ot_ps"], 1)
                pe.wait_ge(s["ot_sb"], c + 1)
                if c:
                    pe.wait_ge(s["gt_sb"], c)
                else:
                    pe.wait_ge(s["ep_used"], NG)
                for t in range(CH):
                    last = mm(ps[7][:, P * t:P * t + P], OTT[:, P * t:P * t + P], WT[:, 3, :], start=True, stop=True)
                last.then_inc(s["x1_ps"], 1)

            def normed(c):
                pe.wait_ge(s["xn2_ready"], c + 1)
                for t in range(CH):
                    last = tr(ps[6][:, P * t:P * t + P], XN2[:, t, :], ident[:])
                last.then_inc(s["xn2t_ps"], 1)

            def mix_in(c):
                pe.wait_ge(s["xn2t_sb"], c + 1)
                for t in range(CH):
                    last = mm(ps[7][:, E1 * t:E1 * t + E1], XN2T[:, c % 2, P * t:P * t + P], WG[:], start=True, stop=True)
                last.then_inc(s["lg2_ps"], 1)
                for n, (j, bank) in enumerate(((6, 6), (5, 7), (4, 6))):
                    if n == 1:
                        pe.wait_ge(s["l8_ready"], c + 1)
                    if n == 2:
                        pe.wait_ge(s["rvk_sb"], 3 * c + 1)
                    mm(ps[bank][:], WT[:, j, :], XN2T[:, c % 2, :], start=True, stop=True).then_inc(s["rvk_ps"], 1)

            def gates_out(c):
                pe.wait_ge(s["g_ready"], c + 1)
                pe.wait_ge(s["rvk_sb"], 3 * c + 2)
                for t in range(CH):
                    last = tr(ps[7][0:E1, P * t:P * t + P], G8[:, c % 2, t, :], ident[:])
                last.then_inc(s["gt_ps"], 1)

            def up2(c, e):
                for k in range(HC1):
                    n = HC1 * (E1 * c + e) + k
                    if n >= 4:
                        pe.wait_ge(s["relu_done"], n - 3)
                    mm(ps[2 * (e % 2) + k][:], MW1[:, e, P * k:P * k + P], XN2T[:, c % 2, :], start=True, stop=True).then_inc(s["up2"], 1)

            def down2(c, e):
                n = E1 * c + e
                pe.wait_ge(s["relu_done"], HC1 * (n + 1))
                if n >= 2:
                    pe.wait_ge(s["acc_done"], n - 1)
                for t in range(CH):
                    for k in range(HC1):
                        last = mm(ps[4 + e % 2][:, D * t:D * t + D], HS[:, e % 2, k, P * t:P * t + P], MW2[:, e, k, :],
                                  start=(k == 0), stop=(k == HC1 - 1))
                last.then_inc(s["down2"], 1)

            def finish(c):
                pe.wait_ge(s["rw_ready"], c + 1)
                pe.wait_ge(s["gt_sb"], c + 1)
                pe.wait_ge(s["rvk_sb"], 3 * c + 3)
                for t in range(CH):
                    cols = slice(P * t, P * t + P)
                    mm(ps[6][:, cols], RWT[c % 2][:, cols], WT[:, 7, :], start=True, stop=False)
                    last = mm(ps[6][:, cols], GTT[0:E1, c % 2, cols], MB2[:], start=False, stop=True)
                last.then_inc(s["fin_ps"], 1)

            pe.wait_ge(s["l1_in"], 64)
            attention_out(0)
            normed(0)
            mix_in(0)
            gates_out(0)
            for c in range(NC):
                up2(c, 0)
                for e in range(E1):
                    if e + 1 < E1:
                        up2(c, e + 1)
                    down2(c, e)
                    if e == 1:
                        finish(c)
                    if c + 1 < NC:
                        if e == 2:
                            pe.wait_ge(s["fin_sb"], c + 1)
                            attention_out(c + 1)
                        if e == 4:
                            normed(c + 1)
                        if e == 5:
                            mix_in(c + 1)
                        if e == 7:
                            gates_out(c + 1)


_INS = ["L0_attn_x", "L0_attn_ln_w", "L0_attn_ln_b", "L0_attn_qkv_w", "L0_attn_qkv_b", "L0_attn_out_w", "L0_attn_out_b",
        "L0_ffn_gate_w", "L0_ffn_gate_b", "L0_ffn_w1", "L0_ffn_b1", "L0_ffn_w2", "L0_ffn_b2", "L1_attn_W_rvk", "L1_attn_W_out",
        "L1_attn_time_decay", "L1_attn_time_first", "L1_ffn_Wg", "L1_ffn_W1", "L1_ffn_b1", "L1_ffn_W2", "L1_ffn_b2"]


def kernel(**inputs):
    import numpy as np
    import concourse.bacc as bacc
    from concourse.bass_utils import run_bass_kernel_spmd

    nc = bacc.Bacc("TRN2", target_bir_lowering=False, num_devices=1)
    arrays, args = {}, []
    for name in _INS:
        a = np.ascontiguousarray(inputs[name])
        arrays[f"in_{name}"] = a
        args.append(nc.dram_tensor(f"in_{name}", a.shape, mybir.dt.from_np(a.dtype), kind="ExternalInput").ap())
    args.append(nc.dram_tensor("out_0", inputs["L0_attn_x"].shape, F32, kind="ExternalOutput").ap())
    build(nc, *args)
    return run_bass_kernel_spmd(nc, [arrays], core_ids=[0]).results[0]["out_0"]
```

```python
from contextlib import ExitStack

import concourse.bass as bass
from concourse import mybir

ALU = mybir.AluOpType
ACT = mybir.ActivationFunctionType
AX = mybir.AxisListType.X
F32 = mybir.dt.float32
F16 = mybir.dt.float16
BF16 = mybir.dt.bfloat16
U32 = mybir.dt.uint32

P = 128
D = 128
LN_EPS = 1e-5
NORM_EPS = 1e-12
NEG_BIG = -1e38


def build(nc, x_d, ln_w_d, ln_b_d, qkv_w_d, qkv_b_d, out_w_d, out_b_d, gate_w_d, gate_b_d, w1_d, b1_d, w2_d, b2_d,
          rvk_w_d, rout_w_d, decay_d, first_d, wg_d, mw1_d, mb1_d, mw2_d, mb2_d, out_d):
    B, N, _ = x_d.shape
    T = B * N
    NT = T // P
    CH = 4
    NC = NT // CH
    BLK = CH * P
    HEADS, HD = 16, 8
    HG = 4
    NHG = HEADS // HG
    NG = NC * NHG
    KT_TILES = N // P
    VW = 16
    E0, TOPK, CAP, H0 = w1_d.shape[0], 3, 64, w1_d.shape[2]
    SLOTS = E0 * CAP
    NPAIR = E0 // 2
    E1, H1 = mw1_d.shape[0], mw1_d.shape[2]
    HC0 = H0 // P
    HC1 = H1 // P
    SCALE = float(HD) ** 0.5
    RING = 4
    ROUNDS = NPAIR // RING
    MOE_FROM = NG - 1 - ROUNDS
    PBUF = 4

    x_v = x_d.rearrange("b n d -> (b n) d").rearrange("(t p) d -> p t d", p=P)
    out_v = out_d.rearrange("b n d -> (b n) d").rearrange("(t p) d -> p t d", p=P)
    slot_in = nc.dram_tensor("slot_in", [SLOTS, D], F32, kind="Internal").ap()
    slot_out = nc.dram_tensor("slot_out", [SLOTS, D], F32, kind="Internal").ap()

    with ExitStack() as ctx:
        def sb(name, shape, dt=F32):
            return ctx.enter_context(nc.sbuf_tensor(name, shape, dt))

        def sem(name):
            return ctx.enter_context(nc.semaphore(name))

        RA = sb("region_a", [P, 11776])
        RB = sb("region_b", [P, 20480])

        def carve(region, at, words, dt=F32):
            v = region[:, at:at + words]
            return v if dt == F32 else v.bitcast(dt)

        X = carve(RA, 0, 2048).rearrange("p (t d) -> p t d", d=D)
        QKA = carve(RA, 2048, 4096).rearrange("p (s t d) -> p s t d", s=2, d=D)
        KS = carve(RA, 6144, 1024, F16).rearrange("p (n w d) -> p n w d", w=4, d=HD)
        QS = carve(RA, 7168, 1024, F16).rearrange("p (n w d) -> p n w d", w=4, d=HD)
        LG = carve(RA, 8192, 1024).rearrange("p (t e) -> p t e", e=E0)
        TMP = carve(RA, 9216, 1024)
        EQ = carve(RA, 10240, 1536, BF16).rearrange("p (k t e) -> p k t e", k=TOPK, e=E0)
        RW = 2816
        ring_w1 = [carve(RA, RW * i, 1024).rearrange("p (e n) -> p e n", e=2) for i in range(RING)]
        ring_w2 = [carve(RA, RW * i + 1024, 1024).rearrange("p (e c d) -> p e c d", e=2, d=D) for i in range(RING)]
        ring_b1 = [carve(RA, RW * i + 2048, 512) for i in range(RING)]
        ring_b2 = carve(RA, 0, RW * RING).rearrange("p (i w) -> p i w", i=RING)[:, :, 2560:2688]
        ring_in = [carve(RA, RW * i + 2688, 128) for i in range(RING)]
        MW1 = carve(RA, 0, 2048).rearrange("p (e h) -> p e h", e=E1)
        MW2 = carve(RA, 2048, 2048).rearrange("p (e c d) -> p e c d", e=E1, d=D)
        KT = carve(RB, 0, 4096, F16).rearrange("p (g n) -> p g n", g=NHG)
        QT = carve(RB, 4096, 4096, F16).rearrange("p (g n) -> p g n", g=NHG)
        VA = carve(RB, 8192, 4096).rearrange("p (t h w) -> p t h w", h=HEADS, w=VW)
        PR = carve(RB, 12288, 8192).rearrange("p (a j n) -> p a j n", a=PBUF, j=HG)
        HN = carve(RB, 12288, 2048).rearrange("p (t d) -> p t d", d=D)
        XNT = carve(RB, 14336, 1024).rearrange("p (a n) -> p a n", a=2)
        HT = carve(RB, 15360, 1024).rearrange("p (a n) -> p a n", a=2)
        YG = carve(RB, 0, 6144).rearrange("p (t k d) -> p t k d", k=TOPK, d=D)
        HS = carve(RB, 14336, 2048).rearrange("p (a c n) -> p a c n", a=2, c=HC1)
        wkv = [carve(RB, 6144 + 512 * i, 512) for i in range(16)]
        KX, VX, ER, D1, D2, PM, F1, F2, EV, NU, DE, T1, RWa, RWb, OTT, _ = wkv
        RWT = [RWa, RWb]

        BASE = sb("base", [P, NT, D])
        XN = sb("xn", [P, NT, D])
        ident = sb("ident", [P, P])
        ident16 = sb("ident16", [P, P], F16)
        before = sb("before", [P, P], BF16)
        ones = sb("ones", [P, P], BF16)
        iota_e = sb("iota_e", [P, E0])
        WL = TMP.rearrange("p (j n) -> p j n", n=P)
        WT = sb("w_cols", [P, 8, P])
        SMALL = sb("small_rows", [20, P])
        COL = sb("small_cols", [P, 20])
        qkv_b = sb("qkv_b", [P, 3 * D])
        gate_w = sb("gate_w", [P, E0])
        gate_b = sb("gate_b", [P, E0])
        out_b = sb("out_b", [P, D])
        WG = sb("wg", [P, E1])
        MB2 = sb("mb2", [E1, D])
        ST = sb("bn", [P, NT, 6])
        MV = sb("mean_var", [P, NT, 2])
        SD = sb("std", [P, NT])
        RS = sb("rstd", [P, NT])
        NQ = sb("norm2", [P, 128])
        NS = sb("norm", [P, 128])
        MX = sb("top", [P, NT, 8])
        IX = sb("top_i", [P, NT, 8], U32)
        IXF = sb("top_if", [P, NT, TOPK])
        GE = sb("gates", [P, NT, TOPK])
        GS = sb("gate_sum", [P, NT])
        POS = sb("pos", [P, TOPK, NT])
        VAL = sb("valid", [P, TOPK, NT])
        SLF = sb("slot_f", [P, TOPK, NT])
        SLG = sb("slot_gather", [P, TOPK, NT], U32)
        SLS = sb("slot_scatter", [P, TOPK, NT], U32)
        MH = sb("mask_bf", [P, NT, E0], BF16)
        MPRE = sb("mask_prefix", [P, NT, E0], BF16)
        OH = sb("heads_out", [P, NC, CH, NHG, 32])
        OTs = sb("av_out", [P, 2, BLK])
        STG = sb("staged_kqv", [P, 4096])
        KST = carve(STG, 0, 1024, F16).rearrange("p (a n) -> p a n", a=2)
        QST = carve(STG, 1024, 2048, F16).rearrange("p (a j n) -> p a j n", a=2, j=HG)
        VST = carve(STG, 3072, 1024).rearrange("p (a s j w) -> p a s j w", a=2, s=KT_TILES, j=HG)
        HB = sb("h_rows", [P, RING, H0])
        BT = sb("slot_in_t", [P, RING * P])
        HTS = XN[:].rearrange("p (i t) d -> p i (t d)", i=RING)
        Y = sb("y", [P, RING, D])
        XN2 = carve(STG, 0, 512).rearrange("p (t d) -> p t d", d=D)
        XN2T = carve(STG, 512, 1024).rearrange("p (a n) -> p a n", a=2)
        GTT = carve(STG, 1536, 1024).rearrange("p (a n) -> p a n", a=2)
        G8 = sb("g8", [P, 2, CH, E1])
        L8 = sb("l8", [P, CH, E1])
        P8 = sb("p8", [P, CH, E1])
        M8 = sb("m8", [P, CH, 8])
        I8 = sb("i8", [P, CH, 8], U32)
        I8F = sb("i8f", [P, CH, 2])
        S4 = sb("s4", [P, CH])
        WDEC = sb("w_decay", [P, 1])
        PP, AA, BB = (HB[:].rearrange("p i n -> p (i n)")[:, (BLK + 1) * i:(BLK + 1) * (i + 1)] for i in range(3))
        NEGW = sb("neg_w", [P, 1])

        ps = [ctx.enter_context(nc.psum_tensor(f"bank{i}", [P, 512], F32)) if i > 3 else None for i in range(8)]
        S = ctx.enter_context(nc.psum_tensor("scores", [P, HG, 512], F32))
        for i in range(4):
            ps[i] = S[:, i]
        AV = ps[4]

        LNW, LNB, DECAY, FIRST = (COL[:, 16 + i:17 + i] for i in range(4))

        names = """w_in c_in l1_in mw_in y_out const_ready zero_ready zeroed base_done pool_chain dve_chain
            var_ready std_ready xn_ready hn_ready wt_ps wt_sb xnt_ps xnt_sb hnt_ps ht_sb qkv_ps qkv_sb lg_ps lg_sb
            sq_ready nq_ready ns_ready qn_ready hi_ready lo_k lo_q kt_ps qt_ps kt_sb qt_sb
            staged qk_ready exp_done av_done a_evac ep_ps ep_used top_ready gexp_ready mask_ready count_ready slots_ready
            scattered bt_ps bt_sb up_done h_sb gelu_done htr_ps htr_sb down_done y_sb
            ot_ps ot_sb x1_ps x1_sb var2_ready std2_ready xn2_ready xn2t_ps xn2t_sb lg2_ps l8_ready p8_exp g_ready
            rvk_ps rvk_sb gt_ps gt_sb d_ready d_exp pool_wkv rw_ready decay_exp up2 relu_done down2 acc_done fin_ps fin_sb""".split()
        s = {n: sem(n) for n in names}
        x_in = [sem(f"x_in{c}") for c in range(NC)]
        ring_in_a = [sem(f"ring_a{i}") for i in range(RING)]
        ring_in_b = [sem(f"ring_b{i}") for i in range(RING)]
        ring_in_x = [sem(f"ring_x{i}") for i in range(RING)]
        
        gathered = [sem(f"gathered{c}") for c in range(NC)]
        out_done = [sem(f"out_done{i}") for i in range(2)]

        def chain(eng, name):
            count = [0]

            def link(ins):
                count[0] += 1
                ins.then_inc(s[name], 1)
                eng.wait_ge(s[name], count[0])
            return link

        block = ctx.enter_context(nc.Block())

        @block.sync
        def _(sp):
            for c in range(NC):
                sp.dma_start(X[:, CH * c:CH * c + CH, :], x_v[:, CH * c:CH * c + CH, :]).then_inc(x_in[c], 16)
            sp.dma_start(qkv_b[:], qkv_b_d.partition_broadcast(P)).then_inc(s["c_in"], 16)
            sp.dma_start(gate_w[:], gate_w_d).then_inc(s["c_in"], 16)
            sp.dma_start(gate_b[:], gate_b_d.partition_broadcast(P)).then_inc(s["c_in"], 16)
            sp.dma_start(out_b[:], out_b_d.partition_broadcast(P)).then_inc(s["c_in"], 16)
            sp.wait_ge(s["zero_ready"], 1)
            half = slot_in.rearrange("(a p r) d -> a p (r d)", a=2, p=P)
            for a in range(2):
                sp.dma_start(half[a], HB[:].rearrange("p i n -> p (i n)")).then_inc(s["zeroed"], 16)
            sp.dma_start(WG[:], wg_d).then_inc(s["l1_in"], 16)
            sp.dma_start(MB2[:], mb2_d).then_inc(s["l1_in"], 16)

            def load_up(m, i):
                sp.dma_start(ring_w1[i], w1_d[bass.ds(2 * m, 2)].rearrange("e p h -> p e h")).then_inc(ring_in_a[i], 16)
                for e in range(2):
                    rows = slice(CAP * e, CAP * e + CAP)
                    sp.dma_start(ring_b1[i][rows, :], b1_d[bass.ds(2 * m + e, 1)].rearrange("a n -> (a n)").partition_broadcast(CAP)
                                 ).then_inc(ring_in_a[i], 16)

            def load_down(m, i):
                sp.dma_start(ring_w2[i].rearrange("p e c d -> p e (c d)"),
                             w2_d[bass.ds(2 * m, 2)].rearrange("e (p c) d -> p e (c d)", c=HC0)).then_inc(ring_in_b[i], 16)
                for e in range(2):
                    rows = slice(CAP * e, CAP * e + CAP)
                    sp.dma_start(ring_b2[rows, i, :], b2_d[bass.ds(2 * m + e, 1)].rearrange("a n -> (a n)").partition_broadcast(CAP)
                                 ).then_inc(ring_in_b[i], 16)

            def load_slots(m, i):
                sp.dma_start(ring_in[i], slot_in[bass.ds(P * m, P)]).then_inc(ring_in_x[i], 16)

            def store_y(G):
                sp.wait_ge(s["y_sb"], G + 1)
                sp.dma_start(slot_out[bass.ds(P * RING * G, P * RING)].rearrange("(i p) d -> p i d", p=P), Y[:]).then_inc(s["y_out"], 16)

            def next_in(G):
                sp.wait_ge(s["bt_ps"], G + 1)
                for i in range(RING):
                    load_slots(RING * G + (RING + i), i)
                for i in range(RING):
                    sp.wait_ge(s["h_sb"], RING * G + (i + 1))
                    load_up(RING * G + (RING + i), i)

            sp.wait_ge(s["slots_ready"], 1)
            sp.wait_ge(s["base_done"], 2)
            for i in range(RING):
                load_up(i, i)
                load_down(i, i)
            sp.wait_ge(s["scattered"], 16 * TOPK * NT)
            for i in range(RING):
                load_slots(i, i)
            next_in(0)
            with sp.Fori(1, ROUNDS - 1) as G:
                next_in(G)
                store_y(G - 1)
                for i in range(RING):
                    load_down(RING * G + i, i)
            store_y(ROUNDS - 2)
            for i in range(RING):
                load_down(RING * (ROUNDS - 1) + i, i)
            store_y(ROUNDS - 1)
            sp.dma_start(MW1, mw1_d.rearrange("e p h -> p e h")).then_inc(s["mw_in"], 16)
            sp.dma_start(MW2, mw2_d.rearrange("e (c p) d -> p e c d", p=P)).then_inc(s["mw_in"], 16)
            for c in range(NC):
                sp.wait_ge(s["acc_done"], E1 * (c + 1))
                sp.wait_ge(s["fin_sb"], c + 1)
                sp.dma_start(out_v[:, CH * c:CH * c + CH, :], BASE[:, CH * c:CH * c + CH, :]).then_inc(out_done[c % 2], 16)
            for a in range(2):
                sp.wait_ge(out_done[a], 16 * NC // 2)

        @block.gpsimd
        def _(pool):
            link = chain(pool, "pool_chain")
            g = nc.gpsimd
            link(g.memset(ident[:], 0.0))
            g.affine_select(out=ident[:], in_=ident[:], compare_op=ALU.not_equal, fill=1.0, base=0,
                            pattern=[[-1, P]], channel_multiplier=1).then_inc(s["const_ready"], 1)
            g.memset(HB[:], 0.0).then_inc(s["zero_ready"], 1)
            link(g.memset(ident16[:], 0.0))
            g.affine_select(out=ident16[:], in_=ident16[:], compare_op=ALU.not_equal, fill=1.0, base=0,
                            pattern=[[-1, P]], channel_multiplier=1)
            g.memset(ones[:], 1.0)
            link(g.memset(before[:], 1.0))
            g.affine_select(out=before[:], in_=before[:], compare_op=ALU.is_gt, fill=0.0, base=0,
                            pattern=[[1, P]], channel_multiplier=-1)
            g.iota(iota_e[:], [[1, E0]], base=0, channel_multiplier=0, allow_small_or_imprecise_dtypes=True)
            link(g.memset(VA, 0.0))
            g.memset(VA[:, :, :, HD:HD + 1], 1.0)
            g.memset(QST, 0.0).then_inc(s["const_ready"], 1)
            pool.wait_ge(s["xn_ready"], 1)
            pool.wait_ge(s["c_in"], 64)
            g.tensor_tensor(BASE[:], X, XN[:], ALU.add).then_inc(s["base_done"], 1)
            pool.wait_ge(s["base_done"], 1)
            g.tensor_tensor(BASE[:], BASE[:], out_b[:].unsqueeze(1).to_broadcast([P, NT, D]), ALU.add).then_inc(s["base_done"], 1)
            for c in range(NC):
                pool.wait_ge(s["hi_ready"], c + 1)
                qa = QKA[:, 0, CH * c:CH * c + CH, :].rearrange("p t (h d) -> p (t h) d", d=HD)
                g.tensor_tensor(QS[:, :, 2:4, :], qa.unsqueeze(2).to_broadcast([P, CH * HEADS, 2, HD]), QS[:, :, 0:2, :],
                                ALU.subtract).then_inc(s["lo_q"], 1)
            pool.wait_ge(s["zeroed"], 32)
            pool.wait_ge(s["slots_ready"], 1)
            for k in range(TOPK):
                for t in range(NT):
                    g.indirect_dma_start(slot_in, bass.IndirectOffsetOnAxis(SLS[:, k, t:t + 1], 0), XN[:, t, :], None,
                                         bounds_check=SLOTS - 1, oob_is_err=False).then_inc(s["scattered"], 16)
            pool.wait_ge(s["y_out"], 16 * ROUNDS)
            pool.wait_ge(s["staged"], NG)

            def gather(c):
                for t in range(CH * c, CH * c + CH):
                    for k in range(TOPK):
                        g.indirect_dma_start(YG[:, t, k, :], None, slot_out, bass.IndirectOffsetOnAxis(SLG[:, k, t:t + 1], 0),
                                             bounds_check=SLOTS - 1, oob_is_err=True).then_inc(gathered[c], 16)

            gather(0)
            gather(1)
            for c in range(NC):
                pool.wait_ge(s["d_ready"], 4 * c + 1)
                if c:
                    pool.wait_ge(s["rw_ready"], c)
                g.tensor_tensor(D2, KX, PP[:, 1:BLK + 1], ALU.subtract).then_inc(s["pool_wkv"], 1)
                pool.wait_ge(s["d_ready"], 4 * c + 3)
                g.tensor_tensor(F1, PP[:, 0:BLK], PM, ALU.subtract).then_inc(s["pool_wkv"], 1)
                pool.wait_ge(s["d_exp"], 4 * c + 2)
                g.tensor_tensor(EV, D2, VX, ALU.mult).then_inc(s["pool_wkv"], 1)
                pool.wait_ge(s["d_exp"], 4 * c + 4)
                g.tensor_tensor(T1, F2, VX, ALU.mult).then_inc(s["pool_wkv"], 1)
                if c + 2 < NC:
                    gather(c + 2)

        @block.scalar
        def _(act):
            a = nc.scalar
            for dst, src in ((WL[:, 0:3], qkv_w_d.rearrange("(j p) d -> p j d", p=P)), (WL[:, 3], out_w_d),
                             (WL[:, 4:7], rvk_w_d.rearrange("(j p) d -> p j d", p=P)), (WL[:, 7], rout_w_d),
                             (SMALL[0:16], mb1_d.rearrange("e (c p) -> (e c) p", p=P)),
                             (SMALL[16:17], ln_w_d.unsqueeze(0)), (SMALL[17:18], ln_b_d.unsqueeze(0)),
                             (SMALL[18:19], decay_d.unsqueeze(0)), (SMALL[19:20], first_d.unsqueeze(0))):
                act.dma_start(dst, src).then_inc(s["w_in"], 16)
            for i, (dst, n) in enumerate(((WT[:, 0:4].rearrange("p j n -> p (j n)"), 512),
                                          (WT[:, 4:8].rearrange("p j n -> p (j n)"), 512), (COL[:], 20))):
                act.wait_ge(s["wt_ps"], i + 1)
                a.activation(dst, ps[4 + i][:, 0:n], ACT.Copy).then_inc(s["wt_sb"], 1)
            for i in range(2):
                act.wait_ge(s["var_ready"], i + 1)
                a.activation(SD[:], MV[:, :, 1], ACT.Sqrt).then_inc(s["std_ready"], 1)
            act.wait_ge(s["wt_sb"], 3)
            for c in range(NC):
                act.wait_ge(s["xnt_ps"], c + 1)
                if c >= 2:
                    act.wait_ge(s["lg_ps"], c - 1)
                a.activation(XNT[:, c % 2], ps[c % 2][:], ACT.Copy).then_inc(s["xnt_sb"], 1)
                act.wait_ge(s["hnt_ps"], c + 1)
                if c >= 2:
                    act.wait_ge(s["qkv_ps"], CH * (c - 1))
                a.activation(HT[:, c % 2], ps[2 + c % 2][:], ACT.Identity, bias=LNB, scale=LNW).then_inc(s["ht_sb"], 1)
            for c in range(NC):
                chunk = slice(CH * c, CH * c + CH)
                act.wait_ge(s["qkv_sb"], CH * (c + 1))
                if c:
                    act.wait_ge(s["nq_ready"], c)
                a.activation(TMP.rearrange("p (s n) -> p s n", s=2), QKA[:, :, chunk, :].rearrange("p s t d -> p s (t d)"),
                             ACT.Square).then_inc(s["sq_ready"], 1)
                act.wait_ge(s["nq_ready"], c + 1)
                a.activation(NS[:], NQ[:], ACT.Sqrt).then_inc(s["ns_ready"], 1)
                act.wait_ge(s["qn_ready"], c + 1)
                for si, dst, where in ((1, KS, slice(0, 4, 2)), (0, QS, slice(0, 2))):
                    if c:
                        act.wait_ge(s["kt_ps" if si else "qt_ps"], c)
                    src = QKA[:, si, chunk, :].rearrange("p t (h d) -> p (t h) d", d=HD)
                    last = a.activation(dst[:, :, where, :], src.unsqueeze(2).to_broadcast([P, CH * HEADS, 2, HD]), ACT.Copy)
                last.then_inc(s["hi_ready"], 1)
                act.wait_ge(s["kt_ps"], c + 1)
                a.activation(KT[:, :, BLK * c:BLK * c + BLK], S[:, 0:2].rearrange("p b n -> p (b n)").bitcast(F16)
                             .rearrange("p (g n) -> p g n", g=NHG), ACT.Copy).then_inc(s["kt_sb"], 1)
            a.activation(WDEC[:], DECAY, ACT.Exp).then_inc(s["decay_exp"], 1)

            def exps(n, st, first=False):
                for h in range(2):
                    act.wait_ge(s["qk_ready"], 2 * n + (h + 1))
                    if not first and h == 0:
                        act.wait_ge(s["av_done"], n - (PBUF - 1))
                    a.activation(PR[:, st % PBUF, 2 * h:2 * h + 2, :], S[:, 2 * h:2 * h + 2, :], ACT.Exp, scale=SCALE
                                 ).then_inc(s["exp_done"], 1)

            def gelus(G):
                for i in range(RING):
                    act.wait_ge(s["h_sb"], RING * G + (i + 1))
                    a.activation(HB[:, i], HB[:, i], ACT.Gelu).then_inc(s["gelu_done"], 1)

            for st in range(KT_TILES):
                exps(st, st, first=st < PBUF)
                if st == 6:
                    act.wait_ge(s["top_ready"], 1)
                    a.activation(GE[:], GE[:], ACT.Exp).then_inc(s["gexp_ready"], 1)
            with act.Fori(1, MOE_FROM) as g:
                for st in range(KT_TILES):
                    exps(KT_TILES * g + st, st)
            with act.Fori(0, ROUNDS) as G:
                for st in range(KT_TILES):
                    exps(KT_TILES * G + (KT_TILES * MOE_FROM + st), st)
                    if st == 4:
                        gelus(G)
            for st in range(KT_TILES):
                exps(KT_TILES * (NG - 1) + st, st)

            def sqrt2(c):
                act.wait_ge(s["var2_ready"], c + 1)
                a.activation(SD[:, 0:CH], MV[:, 0:CH, 1], ACT.Sqrt).then_inc(s["std2_ready"], 1)

            def before_norm(c):
                act.wait_ge(s["ot_ps"], c + 1)
                if c:
                    act.wait_ge(s["x1_ps"], c)
                a.activation(OTT, ps[6][:], ACT.Copy).then_inc(s["ot_sb"], 1)

            def after_norm(c):
                act.wait_ge(s["xn2t_ps"], c + 1)
                if c >= 2:
                    act.wait_ge(s["up2"], E1 * HC1 * (c - 1))
                a.activation(XN2T[:, c % 2], ps[6][:], ACT.Copy).then_inc(s["xn2t_sb"], 1)

            def keys(c):
                if c:
                    act.wait_ge(s["rw_ready"], c)
                act.wait_ge(s["rvk_ps"], 3 * c + 1)
                a.activation(KX, ps[6][:], ACT.Copy).then_inc(s["rvk_sb"], 1)
                act.wait_ge(s["l8_ready"], c + 1)
                a.activation(P8[:], L8[:], ACT.Exp).then_inc(s["p8_exp"], 1)

            def values_receptance(c):
                act.wait_ge(s["rvk_ps"], 3 * c + 2)
                a.activation(VX, ps[7][:], ACT.Copy).then_inc(s["rvk_sb"], 1)
                act.wait_ge(s["rvk_ps"], 3 * c + 3)
                a.activation(ER, ps[6][:], ACT.Exp, scale=-1.0).then_inc(s["rvk_sb"], 1)

            def gates_cols(c):
                act.wait_ge(s["gt_ps"], c + 1)
                a.activation(GTT[0:E1, c % 2], ps[7][0:E1], ACT.Copy).then_inc(s["gt_sb"], 1)

            def state_exps(c):
                act.wait_ge(s["d_ready"], 4 * c + 2)
                a.activation(D1, D1, ACT.Exp).then_inc(s["d_exp"], 1)
                act.wait_ge(s["pool_wkv"], 4 * c + 1)
                a.activation(D2, D2, ACT.Exp).then_inc(s["d_exp"], 1)

            def output_exps(c):
                act.wait_ge(s["pool_wkv"], 4 * c + 2)
                a.activation(F1, F1, ACT.Exp).then_inc(s["d_exp"], 1)
                act.wait_ge(s["d_ready"], 4 * c + 4)
                a.activation(F2, F2, ACT.Exp).then_inc(s["d_exp"], 1)

            def relus(c, e):
                for k in range(HC1):
                    n = HC1 * (E1 * c + e) + k
                    act.wait_ge(s["up2"], n + 1)
                    if E1 * c + e >= 2 and k == 0:
                        act.wait_ge(s["down2"], E1 * c + e - 1)
                    a.activation(HS[:, e % 2, k], ps[2 * (e % 2) + k][:], ACT.Relu, bias=COL[:, HC1 * e + k:HC1 * e + k + 1]
                                 ).then_inc(s["relu_done"], 1)

            before_norm(0)
            sqrt2(0)
            after_norm(0)
            keys(0)
            relus(0, 0)
            values_receptance(0)
            for c in range(NC):
                x = c + 1
                for e in range(E1):
                    if e + 1 < E1:
                        relus(c, e + 1)
                    elif x < NC:
                        relus(x, 0)
                    if c == 0:
                        if e == 0:
                            gates_cols(0)
                        if e == 1:
                            state_exps(0)
                        if e == 2:
                            output_exps(0)
                    if x < NC:
                        if e == 0:
                            before_norm(x)
                        if e == 2:
                            sqrt2(x)
                        if e == 3:
                            after_norm(x)
                        if e == 4:
                            keys(x)
                        if e == 5:
                            values_receptance(x)
                        if e == 6:
                            state_exps(x)
                            gates_cols(x)
                        if e == 7:
                            output_exps(x)

        @block.vector
        def _(dve):
            link = chain(dve, "dve_chain")
            v = nc.vector

            def normalise(src, dst, i, waits=False):
                for t in range(NT):
                    if waits and t % CH == 0:
                        dve.wait_ge(x_in[t // CH], 16)
                    last = v.bn_stats(ST[:, t, :], src[:, t, :])
                link(last)
                for t in range(NT):
                    last = v.bn_aggr(MV[:, t, :], ST[:, t, :])
                link(last)
                v.tensor_scalar(MV[:, :, 1], MV[:, :, 1], LN_EPS, None, ALU.add).then_inc(s["var_ready"], 1)
                dve.wait_ge(s["std_ready"], i + 1)
                link(v.reciprocal(RS[:], SD[:]))
                for t in range(NT):
                    last = v.tensor_scalar(dst[:, t, :], src[:, t, :], MV[:, t, 0:1], RS[:, t:t + 1], ALU.subtract, ALU.mult)
                    if dst is HN and t % CH == CH - 1:
                        last.then_inc(s["hn_ready"], 1)
                if dst is not HN:
                    last.then_inc(s["xn_ready"], 1)
                    dve.wait_ge(s["xn_ready"], 1)

            normalise(X, XN, 0, waits=True)
            normalise(XN, HN, 1)

            dve.wait_ge(s["c_in"], 64)
            dve.wait_ge(s["const_ready"], 2)
            for c in range(NC):
                for t in range(CH * c, CH * c + CH):
                    dve.wait_ge(s["qkv_ps"], t + 1)
                    q = ps[4 + t % 3]
                    v.tensor_tensor(QKA[:, :, t, :], q[:, 0:2 * D].rearrange("p (s d) -> p s d", s=2),
                                    qkv_b[:, 0:2 * D].rearrange("p (s d) -> p s d", s=2), ALU.add)
                    v.tensor_tensor(VA[:, t, :, 0:HD], q[:, 2 * D:3 * D].rearrange("p (h d) -> p h d", d=HD),
                                    qkv_b[:, 2 * D:3 * D].rearrange("p (h d) -> p h d", d=HD), ALU.add).then_inc(s["qkv_sb"], 1)
                dve.wait_ge(s["lg_ps"], c + 1)
                v.tensor_tensor(LG[:, CH * c:CH * c + CH, :], ps[7][:, 0:CH * E0].rearrange("p (t e) -> p t e", e=E0),
                                gate_b[:].unsqueeze(1).to_broadcast([P, CH, E0]), ALU.add).then_inc(s["lg_sb"], 1)
            for c in range(NC):
                chunk = slice(CH * c, CH * c + CH)
                dve.wait_ge(s["sq_ready"], c + 1)
                if c:
                    dve.wait_ge(s["ns_ready"], c)
                v.tensor_reduce(NQ[:], TMP.rearrange("p (n d) -> p n d", d=HD), AX, ALU.add).then_inc(s["nq_ready"], 1)
                dve.wait_ge(s["ns_ready"], c + 1)
                link(v.tensor_scalar(NS[:], NS[:], NORM_EPS, None, ALU.max))
                link(v.reciprocal(NS[:], NS[:]))
                for si in range(2):
                    qk = QKA[:, si, chunk, :].rearrange("p t (h d) -> p (t h) d", d=HD)
                    n = NS[:, 64 * si:64 * si + 64].unsqueeze(2).to_broadcast([P, CH * HEADS, HD])
                    last = v.tensor_tensor(qk, qk, n, ALU.mult)
                last.then_inc(s["qn_ready"], 1)
                dve.wait_ge(s["hi_ready"], c + 1)
                ka = QKA[:, 1, chunk, :].rearrange("p t (h d) -> p (t h) d", d=HD)
                v.tensor_tensor(KS[:, :, 1:4:2, :], ka.unsqueeze(2).to_broadcast([P, CH * HEADS, 2, HD]), KS[:, :, 0:4:2, :],
                                ALU.subtract).then_inc(s["lo_k"], 1)
                dve.wait_ge(s["qt_ps"], c + 1)
                v.tensor_copy(QT[:, :, BLK * c:BLK * c + BLK], S[:, 2:4].rearrange("p b n -> p (b n)").bitcast(F16)
                              .rearrange("p (g n) -> p g n", g=NHG)).then_inc(s["qt_sb"], 1)

            def stage(g):
                c, hg, a = g // NHG, g % NHG, g % 2
                b = c * BLK // N
                if g >= 2:
                    dve.wait_ge(s["qk_ready"], 2 * KT_TILES * (g - 1))
                    dve.wait_ge(s["av_done"], KT_TILES * (g - 1))
                v.tensor_copy(KST[:, a], KT[:, hg, N * b:N * b + N])
                for j in range(HG):
                    rows = slice(32 * j, 32 * j + 32)
                    v.tensor_copy(QST[rows, a, j, :], QT[rows, hg, BLK * c:BLK * c + BLK])
                v.tensor_copy(VST[:, a].rearrange("p s j w -> p s (j w)"),
                              VA[:, KT_TILES * b:KT_TILES * (b + 1), HG * hg:HG * hg + HG, :].rearrange("p t h w -> p t (h w)")
                              ).then_inc(s["staged"], 1)

            def evacuate(g):
                dve.wait_ge(s["av_done"], KT_TILES * (g + 1))
                if g >= 2:
                    dve.wait_ge(s["ep_ps"], g - 1)
                v.tensor_copy(OTs[:, g % 2], AV[:]).then_inc(s["a_evac"], 1)

            def divide(g):
                dve.wait_ge(s["ep_ps"], g + 1)
                o = ps[7][:].rearrange("p (t j w) -> p t j w", t=CH, w=32)
                sums = NQ[:, 0:CH * HG].rearrange("p (t j) -> p t j", t=CH)
                link(v.reciprocal(sums, o[:, :, :, HD]))
                for t in range(CH):
                    last = v.tensor_tensor(OH[:, g // NHG, t, g % NHG, :].rearrange("p (j d) -> p j d", d=HD), o[:, t, :, 0:HD],
                                           sums[:, t, :].unsqueeze(2).to_broadcast([P, HG, HD]), ALU.mult)
                last.then_inc(s["ep_used"], 1)

            dve.wait_ge(s["kt_sb"], NC)
            stage(0)
            stage(1)

            for t in range(NT):
                last = v.max(MX[:, t, :], LG[:, t, :])
            link(last)
            for t in range(NT):
                last = v.max_index(IX[:, t, :], MX[:, t, :], LG[:, t, :])
            link(last)
            v.tensor_tensor(GE[:], MX[:, :, 0:TOPK], MX[:, :, 0:1].to_broadcast([P, NT, TOPK]), ALU.subtract
                            ).then_inc(s["top_ready"], 1)
            link(v.tensor_copy(IXF[:], IX[:, :, 0:TOPK]))
            for k in range(TOPK):
                last = v.tensor_tensor(EQ[:, k], iota_e[:].unsqueeze(1).to_broadcast([P, NT, E0]),
                                       IXF[:, :, k:k + 1].to_broadcast([P, NT, E0]), ALU.is_equal)
            link(last)
            link(v.tensor_tensor(MH[:], EQ[:, 0], EQ[:, 1], ALU.add))
            link(v.tensor_tensor(MH[:], MH[:], EQ[:, 2], ALU.add))
            link(v.memset(MPRE[:, 0, :], 0.0))
            for t in range(1, NT):
                last = v.tensor_tensor(MPRE[:, t, :], MPRE[:, t - 1, :], MH[:, t - 1, :], ALU.add)
                if t < NT - 1:
                    link(last)
            last.then_inc(s["mask_ready"], 1)
            dve.wait_ge(s["gexp_ready"], 1)
            link(v.tensor_reduce(GS[:], GE[:], AX, ALU.add))
            link(v.reciprocal(GS[:], GS[:]))
            link(v.tensor_tensor(GE[:], GE[:], GS[:].unsqueeze(2).to_broadcast([P, NT, TOPK]), ALU.mult))

            def slots():
                dve.wait_ge(s["count_ready"], 1)
                tmp = TMP.rearrange("p (t e) -> p t e", e=E0)
                for k in range(TOPK):
                    for h in range(2):
                        rows = slice(NT // 2 * h, NT // 2 * (h + 1))
                        last = v.tensor_tensor(tmp[:, rows, :], ps[5 + h][:].rearrange("p (t e) -> p t e", e=E0), EQ[:, k, rows, :], ALU.mult)
                    link(last)
                    link(v.tensor_reduce(POS[:, k, :], tmp, AX, ALU.add))
                link(v.tensor_scalar(VAL[:], POS[:], float(CAP), None, ALU.is_lt))
                link(v.tensor_scalar(SLF[:], POS[:], float(CAP - 1), None, ALU.min))
                ix = IXF[:].rearrange("p t k -> p k t")
                link(v.scalar_tensor_tensor(SLF[:], ix, float(CAP), SLF[:], ALU.mult, ALU.add))
                link(v.tensor_copy(SLG[:], SLF[:]))
                link(v.tensor_scalar(POS[:], POS[:], float(CAP), float(2 * SLOTS), ALU.is_ge, ALU.mult))
                link(v.tensor_tensor(SLF[:], SLF[:], POS[:], ALU.add))
                link(v.tensor_copy(SLS[:], SLF[:]))
                v.tensor_tensor(GE[:], GE[:], VAL[:].rearrange("p k t -> p t k"), ALU.mult).then_inc(s["slots_ready"], 1)

            def moe_in(G):
                dve.wait_ge(s["bt_ps"], G + 1)
                if G:
                    dve.wait_ge(s["up_done"], RING * G)
                v.tensor_copy(BT[:], ps[6][:]).then_inc(s["bt_sb"], 1)

            def moe_h(G, i):
                dve.wait_ge(s["up_done"], RING * G + i + 1)
                if G:
                    dve.wait_ge(s["htr_ps"], RING * (G - 1) + i + 1)
                dve.wait_ge(ring_in_a[i], 48 * (G + 1))
                v.tensor_tensor(HB[:, i], ps[5 + i % 2][:], ring_b1[i], ALU.add).then_inc(s["h_sb"], 1)

            def moe_cols(G):
                for i in range(RING):
                    dve.wait_ge(s["htr_ps"], RING * G + i + 1)
                    if i == 0 and G:
                        dve.wait_ge(s["down_done"], G)
                    v.tensor_copy(HTS[:, i], ps[5 + i % 2][:]).then_inc(s["htr_sb"], 1)

            def moe_y(G):
                dve.wait_ge(s["down_done"], G + 1)
                if G:
                    dve.wait_ge(s["y_out"], 16 * G)
                for i in range(RING):
                    dve.wait_ge(ring_in_b[i], 48 * (G + 1))
                v.tensor_tensor(Y[:], ps[7][:].rearrange("p (i d) -> p i d", d=D), ring_b2, ALU.add).then_inc(s["y_sb"], 1)

            for g in range(1, NG):
                G = g - MOE_FROM
                evacuate(g - 1)
                if 0 <= G < ROUNDS:
                    moe_in(G)
                if g + 1 < NG:
                    stage(g + 1)
                if g == NG - 1:
                    moe_y(G - 1)
                divide(g - 1)
                if 0 <= G < ROUNDS:
                    for i in range(RING):
                        moe_h(G, i)
                if 1 <= G < ROUNDS:
                    moe_y(G - 1)
                if 0 <= G < ROUNDS:
                    moe_cols(G)
                if g == 2:
                    slots()
            evacuate(NG - 1)
            divide(NG - 1)

            def combine(c):
                dve.wait_ge(gathered[c], 16 * TOPK * CH)
                for k in range(TOPK):
                    for t in range(CH * c, CH * c + CH):
                        last = v.scalar_tensor_tensor(BASE[:, t, :], YG[:, t, k, :], GE[:, t, k:k + 1], BASE[:, t, :], ALU.mult, ALU.add)
                    link(last)

            def x1_norm(c):
                chunk = slice(CH * c, CH * c + CH)
                dve.wait_ge(s["x1_ps"], c + 1)
                xs = BASE[:, chunk, :]
                v.tensor_tensor(xs, xs, ps[7][:].rearrange("p (t d) -> p t d", d=D), ALU.add).then_inc(s["x1_sb"], 1)
                dve.wait_ge(s["x1_sb"], c + 1)
                for t in range(CH):
                    last = v.bn_stats(ST[:, t, :], BASE[:, CH * c + t, :])
                link(last)
                for t in range(CH):
                    last = v.bn_aggr(MV[:, t, :], ST[:, t, :])
                link(last)
                v.tensor_scalar(MV[:, 0:CH, 1], MV[:, 0:CH, 1], LN_EPS, None, ALU.add).then_inc(s["var2_ready"], 1)

            def x1_scale(c):
                dve.wait_ge(s["std2_ready"], c + 1)
                link(v.reciprocal(RS[:, 0:CH], SD[:, 0:CH]))
                if c:
                    dve.wait_ge(s["xn2t_ps"], c)
                for t in range(CH):
                    last = v.tensor_scalar(XN2[:, t, :], BASE[:, CH * c + t, :], MV[:, t, 0:1], RS[:, t:t + 1], ALU.subtract, ALU.mult)
                last.then_inc(s["xn2_ready"], 1)

            def gates_in(c):
                dve.wait_ge(s["lg2_ps"], c + 1)
                lg = ps[7][:, 0:CH * E1].rearrange("p (t e) -> p t e", e=E1)
                link(v.tensor_reduce(S4[:], lg, AX, ALU.max))
                v.tensor_tensor(L8[:], lg, S4[:].unsqueeze(2).to_broadcast([P, CH, E1]), ALU.subtract).then_inc(s["l8_ready"], 1)

            def gates(c):
                dve.wait_ge(s["p8_exp"], c + 1)
                link(v.tensor_reduce(S4[:], P8[:], AX, ALU.add))
                link(v.reciprocal(S4[:], S4[:]))
                link(v.tensor_tensor(P8[:], P8[:], S4[:].unsqueeze(2).to_broadcast([P, CH, E1]), ALU.mult))
                for t in range(CH):
                    last = v.max(M8[:, t, :], P8[:, t, :])
                link(last)
                for t in range(CH):
                    last = v.max_index(I8[:, t, :], M8[:, t, :], P8[:, t, :])
                link(last)
                link(v.tensor_copy(I8F[:], I8[:, :, 0:2]))
                g8 = G8[:, c % 2]
                iota = iota_e[:, 0:E1].unsqueeze(1).to_broadcast([P, CH, E1])
                v.tensor_tensor(g8, iota, I8F[:, :, 0:1].to_broadcast([P, CH, E1]), ALU.is_equal)
                link(v.tensor_tensor(L8[:], iota, I8F[:, :, 1:2].to_broadcast([P, CH, E1]), ALU.is_equal))
                link(v.tensor_tensor(g8, g8, L8[:], ALU.add))
                v.tensor_tensor(g8, g8, P8[:], ALU.mult).then_inc(s["g_ready"], 1)

            def time_mix(c):
                scan = v.tensor_tensor_scan
                dve.wait_ge(s["rvk_sb"], 3 * c + 3)
                for st, first in ((PP, NEG_BIG), (AA, 0.0), (BB, 0.0)):
                    if (c * BLK) % N == 0:
                        last = v.memset(st[:, 0:1], first)
                    else:
                        last = v.tensor_copy(st[:, 0:1], st[:, BLK:BLK + 1])
                link(last)
                now, new = slice(0, BLK), slice(1, BLK + 1)
                scan(PP[:, new], NEGW[:].to_broadcast([P, BLK]), KX, PP[:, 0:1], ALU.add, ALU.max).then_inc(s["d_ready"], 1)
                dve.wait_ge(s["d_ready"], 4 * c + 1)
                v.scalar_tensor_tensor(D1, PP[:, now], NEGW[:], PP[:, new], ALU.add, ALU.subtract).then_inc(s["d_ready"], 1)
                v.scalar_tensor_tensor(PM, KX, FIRST, PP[:, now], ALU.add, ALU.max).then_inc(s["d_ready"], 1)
                dve.wait_ge(s["d_ready"], 4 * c + 3)
                v.scalar_tensor_tensor(F2, KX, FIRST, PM, ALU.add, ALU.subtract).then_inc(s["d_ready"], 1)

            def time_mix_states(c):
                scan = v.tensor_tensor_scan
                new = slice(1, BLK + 1)
                dve.wait_ge(s["d_exp"], 4 * c + 2)
                scan(BB[:, new], D1, D2, BB[:, 0:1], ALU.mult, ALU.add)
                dve.wait_ge(s["pool_wkv"], 4 * c + 3)
                link(scan(AA[:, new], D1, EV, AA[:, 0:1], ALU.mult, ALU.add))

            def time_mix_out(c):
                now = slice(0, BLK)
                dve.wait_ge(s["d_exp"], 4 * c + 4)
                v.tensor_tensor(NU, F1, AA[:, now], ALU.mult)
                link(v.tensor_tensor(DE, F1, BB[:, now], ALU.mult))
                link(v.tensor_tensor(DE, DE, F2, ALU.add))
                dve.wait_ge(s["pool_wkv"], 4 * c + 4)
                v.tensor_tensor(NU, NU, T1, ALU.add)
                link(v.scalar_tensor_tensor(DE, ER, 1.0, DE, ALU.add, ALU.mult))
                link(v.reciprocal(DE, DE))
                if c >= 2:
                    dve.wait_ge(s["fin_ps"], c - 1)
                v.tensor_tensor(RWT[c % 2], NU, DE, ALU.mult).then_inc(s["rw_ready"], 1)

            def accumulate(c, e):
                if e == 0:
                    dve.wait_ge(s["g_ready"], c + 1)
                dve.wait_ge(s["down2"], E1 * c + e + 1)
                for t in range(CH):
                    y = BASE[:, CH * c + t, :]
                    last = v.scalar_tensor_tensor(y, ps[4 + e % 2][:, D * t:D * t + D], G8[:, c % 2, t, e:e + 1], y, ALU.mult, ALU.add)
                last.then_inc(s["acc_done"], 1)
                dve.wait_ge(s["acc_done"], E1 * c + e + 1)

            def mixed(c):
                dve.wait_ge(s["fin_ps"], c + 1)
                xs = BASE[:, CH * c:CH * c + CH, :]
                v.tensor_tensor(xs, xs, ps[6][:].rearrange("p (t d) -> p t d", d=D), ALU.add).then_inc(s["fin_sb"], 1)
                dve.wait_ge(s["fin_sb"], c + 1)

            dve.wait_ge(s["decay_exp"], 1)
            link(v.tensor_scalar(NEGW[:], WDEC[:], -1.0, None, ALU.mult))
            combine(0)
            x1_norm(0)
            x1_scale(0)
            gates_in(0)
            gates(0)
            for c in range(NC):
                x = c + 1
                for e in range(E1):
                    accumulate(c, e)
                    if c == 0:
                        if e == 0:
                            time_mix(0)
                        if e == 1:
                            time_mix_states(0)
                        if e == 2:
                            time_mix_out(0)
                    if c == 0 and e == 4:
                        mixed(0)
                    if x < NC:
                        if e == 0:
                            combine(x)
                        if e == 1:
                            x1_norm(x)
                        if e == 2:
                            x1_scale(x)
                        if e == 4:
                            gates_in(x)
                        if e == 5:
                            gates(x)
                            time_mix(x)
                        if e == 6:
                            time_mix_states(x)
                        if e == 7:
                            time_mix_out(x)
                    if e == 2 and c:
                        mixed(c)

        @block.tensor
        def _(pe):
            mm, tr = nc.tensor.matmul, nc.tensor.transpose
            pe.wait_ge(s["const_ready"], 1)
            pe.wait_ge(s["w_in"], 16 * 9)
            for i in range(2):
                for j in range(4):
                    last = tr(ps[4 + i][:, P * j:P * j + P], WL[:, 4 * i + j, :], ident[:])
                last.then_inc(s["wt_ps"], 1)
            tr(ps[6][:, 0:20], SMALL[:], ident[0:20, 0:20]).then_inc(s["wt_ps"], 1)

            def turn(c):
                for src, bank, done, freed in ((XN, c % 2, "xnt_ps", "xnt_sb"), (HN, 2 + c % 2, "hnt_ps", "ht_sb")):
                    if src is HN:
                        pe.wait_ge(s["hn_ready"], c + 1)
                    if c >= 2:
                        pe.wait_ge(s[freed], c - 1)
                    for j in range(CH):
                        last = tr(ps[bank][:, P * j:P * j + P], src[:, CH * c + j, :], ident[:])
                    last.then_inc(s[done], 1)

            def project(c):
                pe.wait_ge(s["ht_sb"], c + 1)
                for j in range(CH):
                    t = CH * c + j
                    if t >= 3:
                        pe.wait_ge(s["qkv_sb"], t - 2)
                    mm(ps[4 + t % 3][:, 0:3 * D], HT[:, c % 2, P * j:P * j + P], WT[:, 0:3].rearrange("p j n -> p (j n)"),
                       start=True, stop=True).then_inc(s["qkv_ps"], 1)
                pe.wait_ge(s["xnt_sb"], c + 1)
                if c:
                    pe.wait_ge(s["lg_sb"], c)
                for j in range(CH):
                    last = mm(ps[7][:, E0 * j:E0 * j + E0], XNT[:, c % 2, P * j:P * j + P], gate_w[:], start=True, stop=True)
                last.then_inc(s["lg_ps"], 1)

            pe.wait_ge(s["xn_ready"], 1)
            pe.wait_ge(s["wt_sb"], 3)
            pe.wait_ge(s["c_in"], 64)
            turn(0)
            for c in range(NC):
                if c + 1 < NC:
                    turn(c + 1)
                project(c)

            pe.wait_ge(s["const_ready"], 2)
            pe.wait_ge(s["ht_sb"], NC)
            for c in range(NC):
                for src, bank, lo, ready, done, freed in ((KS, 0, "lo_k", "hi_ready", "kt_ps", "kt_sb"),
                                                          (QS, 2, "lo_q", "hi_ready", "qt_ps", "qt_sb")):
                    pe.wait_ge(s[ready], c + 1)
                    pe.wait_ge(s[lo], c + 1)
                    if c:
                        pe.wait_ge(s[freed], c)
                    cols = src.rearrange("p (t g j) w d -> p t g (j w d)", t=CH, g=NHG)
                    for g in range(NHG):
                        dst = S[:, bank + g // 2].bitcast(F16).rearrange("p (g t n) -> p g t n", g=2, t=CH)
                        for t in range(CH):
                            last = tr(dst[:, g % 2, t, :], cols[:, t, g, :], ident16[:])
                    last.then_inc(s[done], 1)

            def scores(n, st, a, h, first=False, new=None):
                if new is not None:
                    pe.wait_ge(s["staged"], new)
                if not first:
                    pe.wait_ge(s["exp_done"], 2 * n + (h - 1))
                for j in (2 * h, 2 * h + 1):
                    last = mm(S[:, j], KST[:, a, P * st:P * st + P], QST[:, a, j, :], start=True, stop=True)
                last.then_inc(s["qk_ready"], 1)

            def values(n, st, a, half, g=None):
                if half == 0:
                    pe.wait_ge(s["exp_done"], 2 * n + 2)
                    if g is not None:
                        pe.wait_ge(s["a_evac"], g)
                cols = slice(BLK // 2 * half, BLK // 2 * (half + 1))
                for j in range(HG):
                    last = mm(AV[32 * j:32 * j + VW, cols], VST[:, a, st, j, :], PR[:, st % PBUF, j, cols],
                              start=(st == 0 and half == 0), stop=(st == KT_TILES - 1), skip_group_check=True)
                if half:
                    last.then_inc(s["av_done"], 1)

            def tokens_out(g, a, y=None):
                pe.wait_ge(s["a_evac"], g)
                if y is not None:
                    pe.wait_ge(s["y_sb"], y)
                for t in range(CH):
                    last = tr(ps[7][:, P * t:P * t + P], OTs[:, 1 - a, P * t:P * t + P], ident[:])
                last.then_inc(s["ep_ps"], 1)

            def slots_in(G, first):
                for i in range(RING):
                    pe.wait_ge(ring_in_x[i], 16 * G + 16)
                if not first:
                    pe.wait_ge(s["htr_sb"], RING * G)
                for i in range(RING):
                    last = tr(ps[6][:, P * i:P * i + P], ring_in[i], ident[:])
                last.then_inc(s["bt_ps"], 1)

            def up(G, i):
                pe.wait_ge(ring_in_a[i], 48 * G + 48)
                pe.wait_ge(s["bt_sb"], G + 1)
                if i >= 2:
                    pe.wait_ge(s["h_sb"], RING * G + (i - 1))
                if i == 0:
                    pe.wait_ge(s["bt_sb"], G + 1)
                for e in range(2):
                    last = mm(ps[5 + i % 2][CAP * e:CAP * e + CAP, :], BT[:, P * i + CAP * e:P * i + CAP * e + CAP], ring_w1[i][:, e, :],
                              start=True, stop=True)
                last.then_inc(s["up_done"], 1)

            def hidden(G, i):
                pe.wait_ge(s["gelu_done"], RING * G + (i + 1))
                if i < 2:
                    pe.wait_ge(s["h_sb"], RING * G + (i + 3))
                else:
                    pe.wait_ge(s["htr_sb"], RING * G + (i - 1))
                cols = HB[:, i].rearrange("p (m c) -> p c m", c=HC0)
                for c in range(HC0):
                    last = tr(ps[5 + i % 2][:, P * c:P * c + P], cols[:, c, :], ident[:])
                last.then_inc(s["htr_ps"], 1)

            def down(G, g, pairs):
                pe.wait_ge(s["ep_used"], g)
                for i in pairs:
                    pe.wait_ge(s["htr_sb"], RING * G + (i + 1))
                    pe.wait_ge(ring_in_b[i], 48 * G + 48)
                    for c in range(HC0):
                        for e in range(2):
                            last = mm(ps[7][CAP * e:CAP * e + CAP, D * i:D * i + D],
                                      HTS[:, i, P * c + CAP * e:P * c + CAP * e + CAP], ring_w2[i][:, e, c, :],
                                      start=(c == 0), stop=(c == HC0 - 1), skip_group_check=True)
                if RING - 1 in pairs:
                    last.then_inc(s["down_done"], 1)

            def counts():
                pe.wait_ge(s["mask_ready"], 1)
                for h in range(2):
                    rows = slice(NT // 2 * h, NT // 2 * (h + 1))
                    mm(ps[5 + h][:], before[:], MH[:, rows, :].rearrange("p t e -> p (t e)"), start=True, stop=False)
                    last = mm(ps[5 + h][:], ones[:], MPRE[:, rows, :].rearrange("p t e -> p (t e)"), start=False, stop=True)
                last.then_inc(s["count_ready"], 1)

            def group(g, a, first=False, last=False, G=None, first_G=False, H=None, y=None, count=False):
                for st in range(KT_TILES):
                    n = KT_TILES * g + st
                    before_, a_, g_ = (KT_TILES - 1, 1 - a, None) if st == 0 else (st - 1, a, g if st == 1 else None)
                    if first:
                        g_ = None
                    have = not (first and st == 0)
                    if st < KT_TILES - 1:
                        scores(n + 1, st + 1, a, 1)
                    elif not last:
                        scores(n + 1, 0, 1 - a, 1)
                    if have and st != 1:
                        values(n - 1, before_, a_, 0)
                    if H is not None and st == 4 and not last:
                        down(H, g, range(RING))
                    if st < KT_TILES - 2:
                        scores(n + 2, st + 2, a, 0)
                    elif not last:
                        scores(n + 2, st + 2 - KT_TILES, 1 - a, 0, new=g + 2 if st == KT_TILES - 2 else None)
                    if st == 1:
                        values(n - 1, before_, a_, 0, g=g_)
                    if have:
                        values(n - 1, before_, a_, 1)
                    if last:
                        if st <= 1:
                            down(H, g - 1, range(2 * st, 2 * st + 2))
                        if st == 3:
                            tokens_out(g, a, y)
                    elif st == 1 and not first:
                        tokens_out(g, a, y)
                    if count and st == 4:
                        counts()
                    if G is not None:
                        if st == 0:
                            slots_in(G, first_G)
                        if st == 1:
                            up(G, 0)
                        if st == 2:
                            up(G, 1)
                        if st == 3:
                            up(G, 2)
                            up(G, 3)
                        if st == 5:
                            hidden(G, 0)
                            hidden(G, 1)
                        if 6 <= st <= 7:
                            hidden(G, st - 4)

            pe.wait_ge(s["kt_sb"], NC)
            pe.wait_ge(s["qt_sb"], NC)
            pe.wait_ge(s["lg_sb"], NC)
            scores(0, 0, 0, 0, first=True, new=1)
            scores(0, 0, 0, 1, first=True)
            scores(1, 1, 0, 0)
            group(0, 0, first=True)
            group(1, 1)
            group(2, 0, count=True)
            with pe.Fori(1, (MOE_FROM - 1) // 2) as i:
                group(2 * i + 1, 1)
                group(2 * i + 2, 0)
            pe.wait_ge(s["slots_ready"], 1)
            group(MOE_FROM, 1, G=0, first_G=True)
            group(MOE_FROM + 1, 0, G=1, H=0)
            with pe.Fori(1, ROUNDS // 2) as i:
                group(2 * i + MOE_FROM, 1, G=2 * i, H=2 * i - 1, y=2 * i - 1)
                group(2 * i + (MOE_FROM + 1), 0, G=2 * i + 1, H=2 * i, y=2 * i)
            group(NG - 1, 1, last=True, H=ROUNDS - 1, y=ROUNDS)
            for half in range(2):
                values(KT_TILES * NG - 1, KT_TILES - 1, 1, half)
            tokens_out(NG, 0, y=ROUNDS)

            def attention_cols(c):
                pe.wait_ge(s["ep_used"], NHG * (c + 1))
                if c:
                    pe.wait_ge(s["rvk_sb"], 3 * c)
                for t in range(CH):
                    last = tr(ps[6][:, P * t:P * t + P], OH[:, c, t].rearrange("p g w -> p (g w)"), ident[:])
                last.then_inc(s["ot_ps"], 1)

            def attention_out(c):
                pe.wait_ge(s["ot_sb"], c + 1)
                if c:
                    pe.wait_ge(s["gt_sb"], c)
                else:
                    pe.wait_ge(s["ep_used"], NG)
                for t in range(CH):
                    last = mm(ps[7][:, P * t:P * t + P], OTT[:, P * t:P * t + P], WT[:, 3, :], start=True, stop=True)
                last.then_inc(s["x1_ps"], 1)

            def normed(c):
                pe.wait_ge(s["xn2_ready"], c + 1)
                if c >= 2:
                    pe.wait_ge(s["fin_sb"], c)
                for t in range(CH):
                    last = tr(ps[6][:, P * t:P * t + P], XN2[:, t, :], ident[:])
                last.then_inc(s["xn2t_ps"], 1)

            def rvk(c, j, bank):
                mm(ps[bank][:], WT[:, j, :], XN2T[:, c % 2, :], start=True, stop=True).then_inc(s["rvk_ps"], 1)

            def logits_keys(c):
                pe.wait_ge(s["xn2t_sb"], c + 1)
                for t in range(CH):
                    last = mm(ps[7][:, E1 * t:E1 * t + E1], XN2T[:, c % 2, P * t:P * t + P], WG[:], start=True, stop=True)
                last.then_inc(s["lg2_ps"], 1)
                if c == 1:
                    pe.wait_ge(s["fin_sb"], 1)
                rvk(c, 6, 6)

            def values_receptance(c):
                pe.wait_ge(s["l8_ready"], c + 1)
                rvk(c, 5, 7)
                pe.wait_ge(s["rvk_sb"], 3 * c + 1)
                rvk(c, 4, 6)

            def gates_out(c):
                pe.wait_ge(s["g_ready"], c + 1)
                pe.wait_ge(s["rvk_sb"], 3 * c + 2)
                for t in range(CH):
                    last = tr(ps[7][0:E1, P * t:P * t + P], G8[:, c % 2, t, :], ident[:])
                last.then_inc(s["gt_ps"], 1)

            def up2(c, e):
                for k in range(HC1):
                    n = HC1 * (E1 * c + e) + k
                    if n >= 4:
                        pe.wait_ge(s["relu_done"], n - 3)
                    mm(ps[2 * (e % 2) + k][:], MW1[:, e, P * k:P * k + P], XN2T[:, c % 2, :], start=True, stop=True).then_inc(s["up2"], 1)

            def down2(c, e):
                n = E1 * c + e
                pe.wait_ge(s["relu_done"], HC1 * (n + 1))
                if n >= 2:
                    pe.wait_ge(s["acc_done"], n - 1)
                for t in range(CH):
                    for k in range(HC1):
                        last = mm(ps[4 + e % 2][:, D * t:D * t + D], HS[:, e % 2, k, P * t:P * t + P], MW2[:, e, k, :],
                                  start=(k == 0), stop=(k == HC1 - 1))
                last.then_inc(s["down2"], 1)

            def finish(c):
                pe.wait_ge(s["rw_ready"], c + 1)
                pe.wait_ge(s["gt_sb"], c + 1)
                pe.wait_ge(s["rvk_sb"], 3 * c + 3)
                if c == 0:
                    pe.wait_ge(s["xn2t_sb"], 2)
                for t in range(CH):
                    cols = slice(P * t, P * t + P)
                    mm(ps[6][:, cols], RWT[c % 2][:, cols], WT[:, 7, :], start=True, stop=False)
                    last = mm(ps[6][:, cols], GTT[0:E1, c % 2, cols], MB2[:], start=False, stop=True)
                last.then_inc(s["fin_ps"], 1)

            pe.wait_ge(s["l1_in"], 32)
            attention_cols(0)
            attention_out(0)
            normed(0)
            logits_keys(0)
            pe.wait_ge(s["mw_in"], 32)
            up2(0, 0)
            values_receptance(0)
            for c in range(NC):
                x = c + 1
                for e in range(E1):
                    if e + 1 < E1:
                        up2(c, e + 1)
                    elif x < NC:
                        up2(x, 0)
                    down2(c, e)
                    if c == 0 and e == 0:
                        gates_out(0)
                    if x < NC:
                        if e == 0:
                            attention_cols(x)
                        if e == 1:
                            attention_out(x)
                    if e == (2 if c else 4):
                        finish(c)
                    if x < NC:
                        if e == 3:
                            normed(x)
                        if e == 4:
                            logits_keys(x)
                        if e == 5:
                            values_receptance(x)
                        if e == 6:
                            gates_out(x)

_INS = ["L0_attn_x", "L0_attn_ln_w", "L0_attn_ln_b", "L0_attn_qkv_w", "L0_attn_qkv_b", "L0_attn_out_w", "L0_attn_out_b",
        "L0_ffn_gate_w", "L0_ffn_gate_b", "L0_ffn_w1", "L0_ffn_b1", "L0_ffn_w2", "L0_ffn_b2", "L1_attn_W_rvk", "L1_attn_W_out",
        "L1_attn_time_decay", "L1_attn_time_first", "L1_ffn_Wg", "L1_ffn_W1", "L1_ffn_b1", "L1_ffn_W2", "L1_ffn_b2"]


def kernel(**inputs):
    import numpy as np
    import concourse.bacc as bacc
    from concourse.bass_utils import run_bass_kernel_spmd

    nc = bacc.Bacc("TRN2", target_bir_lowering=False, num_devices=1)
    arrays, args = {}, []
    for name in _INS:
        a = np.ascontiguousarray(inputs[name])
        arrays[f"in_{name}"] = a
        args.append(nc.dram_tensor(f"in_{name}", a.shape, mybir.dt.from_np(a.dtype), kind="ExternalInput").ap())
    args.append(nc.dram_tensor("out_0", inputs["L0_attn_x"].shape, F32, kind="ExternalOutput").ap())
    build(nc, *args)
    return run_bass_kernel_spmd(nc, [arrays], core_ids=[0]).results[0]["out_0"]
```

```python
from contextlib import ExitStack

import concourse.bass as bass
from concourse import mybir

ALU = mybir.AluOpType
ACT = mybir.ActivationFunctionType
AX = mybir.AxisListType.X
F32 = mybir.dt.float32
F16 = mybir.dt.float16
BF16 = mybir.dt.bfloat16
U32 = mybir.dt.uint32

P = 128
D = 128
LN_EPS = 1e-5
NORM_EPS = 1e-12
NEG_BIG = -1e38


def build(nc, x_d, ln_w_d, ln_b_d, qkv_w_d, qkv_b_d, out_w_d, out_b_d, gate_w_d, gate_b_d, w1_d, b1_d, w2_d, b2_d,
          rvk_w_d, rout_w_d, decay_d, first_d, wg_d, mw1_d, mb1_d, mw2_d, mb2_d, out_d):
    B, N, _ = x_d.shape
    T = B * N
    NT = T // P
    CH = 4
    NC = NT // CH
    BLK = CH * P
    HEADS, HD = 16, 8
    HG = 4
    NHG = HEADS // HG
    NG = NC * NHG
    KT_TILES = N // P
    VW = 16
    E0, TOPK, CAP, H0 = w1_d.shape[0], 3, 64, w1_d.shape[2]
    SLOTS = E0 * CAP
    NPAIR = E0 // 2
    E1, H1 = mw1_d.shape[0], mw1_d.shape[2]
    HC0 = H0 // P
    HC1 = H1 // P
    SCALE = float(HD) ** 0.5
    RING = 4
    ROUNDS = NPAIR // RING
    MOE_FROM = NG - 2 - ROUNDS
    EARLY = N // BLK
    LATE = 2
    PBUF = 4

    x_v = x_d.rearrange("b n d -> (b n) d").rearrange("(t p) d -> p t d", p=P)
    out_v = out_d.rearrange("b n d -> (b n) d").rearrange("(t p) d -> p t d", p=P)
    slot_in = nc.dram_tensor("slot_in", [SLOTS, D], F32, kind="Internal").ap()
    slot_out = nc.dram_tensor("slot_out", [SLOTS, D], F32, kind="Internal").ap()

    with ExitStack() as ctx:
        def sb(name, shape, dt=F32):
            return ctx.enter_context(nc.sbuf_tensor(name, shape, dt))

        def sem(name):
            return ctx.enter_context(nc.semaphore(name))

        RA = sb("region_a", [P, 11776])
        RB = sb("region_b", [P, 20480])

        def carve(region, at, words, dt=F32):
            v = region[:, at:at + words]
            return v if dt == F32 else v.bitcast(dt)

        X = carve(RA, 0, 2048).rearrange("p (t d) -> p t d", d=D)
        QKA = carve(RA, 2048, 4096).rearrange("p (s t d) -> p s t d", s=2, d=D)
        KS = carve(RA, 6144, 1024, F16).rearrange("p (n w d) -> p n w d", w=4, d=HD)
        QS = carve(RA, 7168, 1024, F16).rearrange("p (n w d) -> p n w d", w=4, d=HD)
        LG = carve(RA, 8192, 1024).rearrange("p (t e) -> p t e", e=E0)
        TMP = carve(RA, 9216, 1024)
        EQ = carve(RA, 10240, 1536, BF16).rearrange("p (k t e) -> p k t e", k=TOPK, e=E0)
        RW = 2816
        ring_w1 = [carve(RA, RW * i, 1024).rearrange("p (e n) -> p e n", e=2) for i in range(RING)]
        ring_w2 = [carve(RA, RW * i + 1024, 1024).rearrange("p (e c d) -> p e c d", e=2, d=D) for i in range(RING)]
        ring_b1 = [carve(RA, RW * i + 2048, 512) for i in range(RING)]
        ring_b2 = carve(RA, 0, RW * RING).rearrange("p (i w) -> p i w", i=RING)[:, :, 2560:2688]
        ring_in = [carve(RA, RW * i + 2688, 128) for i in range(RING)]
        MW1 = carve(RA, 0, 2048).rearrange("p (e h) -> p e h", e=E1)
        MW2 = carve(RA, 2048, 2048).rearrange("p (e c d) -> p e c d", e=E1, d=D)
        KT = carve(RB, 0, 4096, F16).rearrange("p (g n) -> p g n", g=NHG)
        QT = carve(RB, 4096, 4096, F16).rearrange("p (g n) -> p g n", g=NHG)
        VA = carve(RB, 8192, 4096).rearrange("p (t h w) -> p t h w", h=HEADS, w=VW)
        PR = carve(RB, 12288, 8192).rearrange("p (a j n) -> p a j n", a=PBUF, j=HG)
        HN = carve(RB, 12288, 2048).rearrange("p (t d) -> p t d", d=D)
        XNT = carve(RB, 14336, 1024).rearrange("p (a n) -> p a n", a=2)
        HT = carve(RB, 15360, 1024).rearrange("p (a n) -> p a n", a=2)
        TMPs = [TMP, carve(RB, 16384, 1024)]
        KSs = [KS, carve(RB, 17408, 1024, F16).rearrange("p (n w d) -> p n w d", w=4, d=HD)]
        QSs = [QS, carve(RB, 18432, 1024, F16).rearrange("p (n w d) -> p n w d", w=4, d=HD)]
        WL1 = carve(RB, 19456, 512).rearrange("p (j n) -> p j n", n=P)
        YG = carve(RB, 0, 6144).rearrange("p (t k d) -> p t k d", k=TOPK, d=D)
        HS = carve(RB, 14336, 2048).rearrange("p (a c n) -> p a c n", a=2, c=HC1)
        wkv = [carve(RB, 6144 + 512 * i, 512) for i in range(16)]
        KX, VX, ER, D1, D2, PM, F1, F2, EV, NU, DE, T1, RWa, RWb, _, _ = wkv
        RWT = [RWa, RWb]

        BASE = sb("base", [P, NT, D])
        XN = sb("xn", [P, NT, D])
        ident = sb("ident", [P, P])
        ident16 = sb("ident16", [P, P], F16)
        before = sb("before", [P, P], BF16)
        ones = sb("ones", [P, P], BF16)
        iota_e = sb("iota_e", [P, E0])
        WL = TMP[:, 0:4 * P].rearrange("p (j n) -> p j n", n=P)
        WT = sb("w_cols", [P, 8, P])
        SMALL = sb("small_rows", [18, P])
        LN_ROWS = sb("ln_rows", [2, P])
        COL = sb("small_cols", [P, 20])
        qkv_b = sb("qkv_b", [P, 3 * D])
        gate_w = sb("gate_w", [P, 2, E0])
        gate_b = sb("gate_b", [P, E0])
        out_b = sb("out_b", [P, D])
        WG = sb("wg", [P, E1])
        MB2 = sb("mb2", [E1, D])
        ST = sb("bn", [P, NT, 6])
        MV = sb("mean_var", [P, NT, 2])
        SD = sb("std", [P, NT])
        RS = sb("rstd", [P, NT])
        VE = sb("var_eps", [P, NT])
        V2 = sb("var2", [P, NT])
        RH = sb("rstd2", [P, NT])
        NB = sb("shift2", [P, NT])
        EPS = sb("eps", [P, 1])
        NQ = sb("norm2", [P, 128])
        NS = sb("norm", [P, 128])
        MX = sb("top", [P, NT, 8])
        IX = sb("top_i", [P, NT, 8], U32)
        IXF = sb("top_if", [P, NT, TOPK])
        GE = sb("gates", [P, NT, TOPK])
        GS = sb("gate_sum", [P, NT])
        POS = sb("pos", [P, TOPK, NT])
        VAL = sb("valid", [P, TOPK, NT])
        SLF = sb("slot_f", [P, TOPK, NT])
        SLG = sb("slot_gather", [P, TOPK, NT], U32)
        SLS = sb("slot_scatter", [P, TOPK, NT], U32)
        MH = sb("mask_bf", [P, NT, E0], BF16)
        MPRE = sb("mask_prefix", [P, NT, E0], BF16)
        OH = sb("heads_out", [P, NC, CH, NHG, 32])
        OTs = sb("av_out", [P, 2, BLK])
        STG = sb("staged_kqv", [P, 4096])
        KST = carve(STG, 0, 1024, F16).rearrange("p (a n) -> p a n", a=2)
        QST = carve(STG, 1024, 2048, F16).rearrange("p (a j n) -> p a j n", a=2, j=HG)
        VST = carve(STG, 3072, 1024).rearrange("p (a s j w) -> p a s j w", a=2, s=KT_TILES, j=HG)
        HB = sb("h_rows", [P, RING, H0])
        MIO = sb("slots_io", [P, 2 * RING * P])
        BT = MIO[:, 0:RING * P]
        HTS = XN[:].rearrange("p (i t) d -> p i (t d)", i=RING)
        Y = MIO[:, RING * P:2 * RING * P].rearrange("p (i d) -> p i d", d=D)
        KSL = sb("k_split", [P, 1024])
        NL = sb("norms_late", [P, NC - EARLY, 128])

        def halves(words):
            return words.bitcast(F16).rearrange("p (n w d) -> p n w d", w=4, d=HD)

        hb = HB[:].rearrange("p i n -> p (i n)")
        late_k = [halves(hb[:, 0:1024]), halves(KSL[:])]
        late_q = [halves(hb[:, 1024:2048]), halves(MIO[:])]
        XN2 = carve(STG, 0, 512).rearrange("p (t d) -> p t d", d=D)
        XN2T = carve(STG, 512, 1024).rearrange("p (a n) -> p a n", a=2)
        GTT = carve(STG, 1536, 1024).rearrange("p (a n) -> p a n", a=2)
        OTT = KSL[:, 0:BLK]
        G8 = sb("g8", [P, 2, CH, E1])
        L8 = sb("l8", [P, CH, E1])
        P8 = sb("p8", [P, CH, E1])
        M8 = sb("m8", [P, CH, 8])
        I8 = sb("i8", [P, CH, 8], U32)
        I8F = sb("i8f", [P, CH, 2])
        S4 = sb("s4", [P, CH])
        WDEC = sb("w_decay", [P, 1])
        PP, AA, BB = (HB[:].rearrange("p i n -> p (i n)")[:, (BLK + 1) * i:(BLK + 1) * (i + 1)] for i in range(3))
        NEGW = sb("neg_w", [P, 1])

        ps = [ctx.enter_context(nc.psum_tensor(f"bank{i}", [P, 512], F32)) if i > 3 else None for i in range(8)]
        S = ctx.enter_context(nc.psum_tensor("scores", [P, HG, 512], F32))
        for i in range(4):
            ps[i] = S[:, i]
        AV = ps[4]

        DECAY, FIRST, LNW, LNB = (COL[:, 16 + i:17 + i] for i in range(4))

        names = """w_in c_in l1_in mw_in y_out const_ready zero_ready zeroed base_done pool_chain dve_chain
            var_ready std_ready xn_ready hvar_ready hstd_ready hscale_ready hn_ready w1_in wt_ps wt_sb xnt_ps xnt_sb hnt_ps ht_sb qkv_ps qkv_sb lg_ps lg_sb
            sq_ready nq_ready ns_ready inv_ready kn_ready qn_ready hi_k hi_q lo_k lo_q kt_ps qt_ps kt_sb qt_sb late_in late_sq late_std late_split late_ps late_sb
            staged qk_ready exp_done av_done a_evac ep_ps ep_used top_ready gexp_ready mask_ready count_ready slots_ready
            scattered bt_ps bt_sb up_done h_sb gelu_done htr_ps htr_sb down_done y_sb
            ot_ps ot_sb x1_ps x1_sb var2_ready std2_ready xn2_ready xn2t_ps xn2t_sb lg2_ps l8_ready p8_exp g_ready
            rvk_ps rvk_sb gt_ps gt_sb d_ready d_exp combined pool_wkv rw_ready decay_exp up2 relu_done down2 acc_done fin_ps fin_sb""".split()
        s = {n: sem(n) for n in names}
        x_in = [sem(f"x_in{c}") for c in range(NC)]
        ring_in_a = [sem(f"ring_a{i}") for i in range(RING)]
        ring_in_b = [sem(f"ring_b{i}") for i in range(RING)]
        ring_in_x = [sem(f"ring_x{i}") for i in range(RING)]
        
        gathered = [sem(f"gathered{c}") for c in range(NC)]
        out_done = [sem(f"out_done{i}") for i in range(2)]

        def chain(eng, name):
            count = [0]

            def link(ins):
                count[0] += 1
                ins.then_inc(s[name], 1)
                eng.wait_ge(s[name], count[0])
            return link

        block = ctx.enter_context(nc.Block())

        @block.sync
        def _(sp):
            for c in range(NC):
                sp.dma_start(X[:, CH * c:CH * c + CH, :], x_v[:, CH * c:CH * c + CH, :]).then_inc(x_in[c], 16)
            sp.dma_start(WL[:, 3], out_w_d).then_inc(s["w_in"], 16)
            sp.dma_start(qkv_b[:], qkv_b_d.partition_broadcast(P)).then_inc(s["c_in"], 16)
            for h in range(2):
                sp.dma_start(gate_w[:, h], gate_w_d).then_inc(s["c_in"], 16)
            sp.dma_start(gate_b[:], gate_b_d.partition_broadcast(P)).then_inc(s["c_in"], 16)
            sp.dma_start(out_b[:], out_b_d.partition_broadcast(P)).then_inc(s["c_in"], 16)
            for dst, src in ((WL1[:, 0:3], rvk_w_d.rearrange("(j p) d -> p j d", p=P)), (WL1[:, 3], rout_w_d),
                             (SMALL[0:16], mb1_d.rearrange("e (c p) -> (e c) p", p=P)),
                             (SMALL[16:17], decay_d.unsqueeze(0)), (SMALL[17:18], first_d.unsqueeze(0))):
                sp.dma_start(dst, src).then_inc(s["w1_in"], 16)
            sp.wait_ge(s["zero_ready"], 1)
            half = slot_in.rearrange("(a p r) d -> a p (r d)", a=2, p=P)
            for a in range(2):
                sp.dma_start(half[a], HB[:].rearrange("p i n -> p (i n)")).then_inc(s["zeroed"], 16)
            sp.dma_start(WG[:], wg_d).then_inc(s["l1_in"], 16)
            sp.dma_start(MB2[:], mb2_d).then_inc(s["l1_in"], 16)

            def load_up(m, i):
                sp.dma_start(ring_w1[i], w1_d[bass.ds(2 * m, 2)].rearrange("e p h -> p e h")).then_inc(ring_in_a[i], 16)
                for e in range(2):
                    rows = slice(CAP * e, CAP * e + CAP)
                    sp.dma_start(ring_b1[i][rows, :], b1_d[bass.ds(2 * m + e, 1)].rearrange("a n -> (a n)").partition_broadcast(CAP)
                                 ).then_inc(ring_in_a[i], 16)

            def load_down(m, i):
                sp.dma_start(ring_w2[i].rearrange("p e c d -> p e (c d)"),
                             w2_d[bass.ds(2 * m, 2)].rearrange("e (p c) d -> p e (c d)", c=HC0)).then_inc(ring_in_b[i], 16)
                for e in range(2):
                    rows = slice(CAP * e, CAP * e + CAP)
                    sp.dma_start(ring_b2[rows, i, :], b2_d[bass.ds(2 * m + e, 1)].rearrange("a n -> (a n)").partition_broadcast(CAP)
                                 ).then_inc(ring_in_b[i], 16)

            def load_slots(m, i):
                sp.dma_start(ring_in[i], slot_in[bass.ds(P * m, P)]).then_inc(ring_in_x[i], 16)

            def store_y(G):
                sp.wait_ge(s["y_sb"], G + 1)
                sp.dma_start(slot_out[bass.ds(P * RING * G, P * RING)].rearrange("(i p) d -> p i d", p=P), Y).then_inc(s["y_out"], 16)

            def next_in(G):
                sp.wait_ge(s["bt_ps"], G + 1)
                for i in range(RING):
                    load_slots(RING * G + (RING + i), i)
                for i in range(RING):
                    sp.wait_ge(s["h_sb"], RING * G + (i + 1))
                    load_up(RING * G + (RING + i), i)

            sp.wait_ge(s["slots_ready"], 1)
            sp.wait_ge(s["base_done"], 2)
            sp.wait_ge(s["late_split"], 2 * (NC - EARLY))
            for i in range(RING):
                load_up(i, i)
                load_down(i, i)
            sp.wait_ge(s["scattered"], 16 * TOPK * NT)
            for i in range(RING):
                load_slots(i, i)
            next_in(0)
            with sp.Fori(1, ROUNDS - 1) as G:
                next_in(G)
                store_y(G - 1)
                for i in range(RING):
                    load_down(RING * G + i, i)
            store_y(ROUNDS - 2)
            for i in range(RING):
                load_down(RING * (ROUNDS - 1) + i, i)
            store_y(ROUNDS - 1)
            sp.dma_start(MW1, mw1_d.rearrange("e p h -> p e h")).then_inc(s["mw_in"], 16)
            sp.dma_start(MW2, mw2_d.rearrange("e (c p) d -> p e c d", p=P)).then_inc(s["mw_in"], 16)
            for c in range(NC):
                sp.wait_ge(s["acc_done"], E1 * (c + 1))
                sp.wait_ge(s["fin_sb"], c + 1)
                sp.dma_start(out_v[:, CH * c:CH * c + CH, :], BASE[:, CH * c:CH * c + CH, :]).then_inc(out_done[c % 2], 16)
            for a in range(2):
                sp.wait_ge(out_done[a], 16 * NC // 2)

        @block.gpsimd
        def _(pool):
            link = chain(pool, "pool_chain")
            g = nc.gpsimd
            link(g.memset(ident[:], 0.0))
            g.affine_select(out=ident[:], in_=ident[:], compare_op=ALU.not_equal, fill=1.0, base=0,
                            pattern=[[-1, P]], channel_multiplier=1).then_inc(s["const_ready"], 1)
            link(g.memset(VA, 0.0))
            g.memset(VA[:, :, :, HD:HD + 1], 1.0).then_inc(s["const_ready"], 1)
            g.memset(HB[:], 0.0).then_inc(s["zero_ready"], 1)
            link(g.memset(ident16[:], 0.0))
            g.affine_select(out=ident16[:], in_=ident16[:], compare_op=ALU.not_equal, fill=1.0, base=0,
                            pattern=[[-1, P]], channel_multiplier=1)
            g.memset(ones[:], 1.0)
            link(g.memset(before[:], 1.0))
            g.affine_select(out=before[:], in_=before[:], compare_op=ALU.is_gt, fill=0.0, base=0,
                            pattern=[[1, P]], channel_multiplier=-1)
            g.iota(iota_e[:], [[1, E0]], base=0, channel_multiplier=0, allow_small_or_imprecise_dtypes=True)
            g.memset(QST, 0.0).then_inc(s["const_ready"], 1)
            pool.wait_ge(s["xn_ready"], NC)
            pool.wait_ge(s["c_in"], 80)
            g.tensor_tensor(BASE[:], X, XN[:], ALU.add).then_inc(s["base_done"], 1)
            pool.wait_ge(s["base_done"], 1)
            g.tensor_tensor(BASE[:], BASE[:], out_b[:].unsqueeze(1).to_broadcast([P, NT, D]), ALU.add).then_inc(s["base_done"], 1)
            def late_squares(c):
                pool.wait_ge(s["qkv_sb"], CH * (c + 1))
                pool.wait_ge(s["nq_ready"], c % 2 + 1)
                qk = QKA[:, :, CH * c:CH * c + CH, :].rearrange("p s t d -> p s (t d)")
                g.tensor_tensor(TMPs[c % 2].rearrange("p (s n) -> p s n", s=2), qk, qk, ALU.mult).then_inc(s["late_in"], 1)

            for c in range(EARLY):
                qa = QKA[:, 0, CH * c:CH * c + CH, :].rearrange("p t (h d) -> p (t h) d", d=HD)
                pool.wait_ge(s["inv_ready"], c + 1)
                g.tensor_tensor(qa, qa, NS[:, 0:64].unsqueeze(2).to_broadcast([P, CH * HEADS, HD]), ALU.mult).then_inc(s["qn_ready"], 1)
                if c == EARLY - 1:
                    late_squares(NC - 1)
                pool.wait_ge(s["hi_q"], c + 1)
                qs = QSs[c % 2]
                g.tensor_tensor(qs[:, :, 2:4, :], qa.unsqueeze(2).to_broadcast([P, CH * HEADS, 2, HD]), qs[:, :, 0:2, :],
                                ALU.subtract).then_inc(s["lo_q"], 1)
                if c == 0:
                    late_squares(EARLY)
            pool.wait_ge(s["zeroed"], 32)
            pool.wait_ge(s["slots_ready"], 1)
            for k in range(TOPK):
                for t in range(NT):
                    g.indirect_dma_start(slot_in, bass.IndirectOffsetOnAxis(SLS[:, k, t:t + 1], 0), XN[:, t, :], None,
                                         bounds_check=SLOTS - 1, oob_is_err=False).then_inc(s["scattered"], 16)
            pool.wait_ge(s["y_out"], 16 * ROUNDS)
            pool.wait_ge(s["staged"], NG)

            def gather(c):
                for t in range(CH * c, CH * c + CH):
                    for k in range(TOPK):
                        g.indirect_dma_start(YG[:, t, k, :], None, slot_out, bass.IndirectOffsetOnAxis(SLG[:, k, t:t + 1], 0),
                                             bounds_check=SLOTS - 1, oob_is_err=True).then_inc(gathered[c], 16)

            def combine(c):
                pool.wait_ge(gathered[c], 16 * TOPK * CH)
                chunk = slice(CH * c, CH * c + CH)
                n = (TOPK + 1) * (c - 1)
                g.tensor_tensor(YG[:, chunk], YG[:, chunk], GE[:, chunk, :].unsqueeze(3).to_broadcast([P, CH, TOPK, D]), ALU.mult
                                ).then_inc(s["combined"], 1)
                for k in range(TOPK):
                    pool.wait_ge(s["combined"], n + k + 1)
                    g.tensor_tensor(BASE[:, chunk, :], BASE[:, chunk, :], YG[:, chunk, k, :], ALU.add).then_inc(s["combined"], 1)

            gather(0)
            gather(1)
            combine(1)
            for c in range(NC):
                pool.wait_ge(s["d_ready"], 4 * c + 1)
                if c:
                    pool.wait_ge(s["rw_ready"], c)
                g.tensor_tensor(D2, KX, PP[:, 1:BLK + 1], ALU.subtract).then_inc(s["pool_wkv"], 1)
                pool.wait_ge(s["d_ready"], 4 * c + 3)
                g.tensor_tensor(F1, PP[:, 0:BLK], PM, ALU.subtract).then_inc(s["pool_wkv"], 1)
                pool.wait_ge(s["d_exp"], 4 * c + 2)
                g.tensor_tensor(EV, D2, VX, ALU.mult).then_inc(s["pool_wkv"], 1)
                pool.wait_ge(s["d_exp"], 4 * c + 4)
                g.tensor_tensor(T1, F2, VX, ALU.mult).then_inc(s["pool_wkv"], 1)
                if c + 2 < NC:
                    gather(c + 2)
                    combine(c + 2)

        @block.scalar
        def _(act):
            a = nc.scalar
            for dst, src in ((WL[:, 0:3], qkv_w_d.rearrange("(j p) d -> p j d", p=P)),
                             (LN_ROWS[0:1], ln_w_d.unsqueeze(0)), (LN_ROWS[1:2], ln_b_d.unsqueeze(0))):
                act.dma_start(dst, src).then_inc(s["w_in"], 16)

            def deviations(c):
                act.wait_ge(s["var_ready"], c + 1)
                a.activation(SD[:, CH * c:CH * c + CH], VE[:, CH * c:CH * c + CH], ACT.Sqrt).then_inc(s["std_ready"], 1)

            def deviations2(n, tiles):
                act.wait_ge(s["hvar_ready"], n)
                a.activation(RH[:, tiles], V2[:, tiles], ACT.Sqrt, bias=EPS[:]).then_inc(s["hstd_ready"], 1)

            def normed_rows(c):
                act.wait_ge(s["hscale_ready"], min(c, 2) + 1)
                for t in range(CH * c, CH * c + CH):
                    last = a.activation(HN[:, t, :], X[:, t, :], ACT.Identity, bias=NB[:, t:t + 1], scale=RH[:, t:t + 1])
                last.then_inc(s["hn_ready"], 1)

            def gate_cols(c):
                act.wait_ge(s["xnt_ps"], c + 1)
                if c >= 2:
                    act.wait_ge(s["lg_ps"], c - 1)
                a.activation(XNT[:, c % 2], ps[c % 2][:], ACT.Copy).then_inc(s["xnt_sb"], 1)

            def qkv_cols(c):
                act.wait_ge(s["hnt_ps"], c + 1)
                if c >= 2:
                    act.wait_ge(s["qkv_ps"], CH * (c - 1))
                a.activation(HT[:, c % 2], ps[2 + c % 2][:], ACT.Identity, bias=LNB, scale=LNW).then_inc(s["ht_sb"], 1)

            def squares(c):
                act.wait_ge(s["qkv_sb"], CH * (c + 1))
                if c >= 2:
                    act.wait_ge(s["nq_ready"], c - 1)
                a.activation(TMPs[c % 2].rearrange("p (s n) -> p s n", s=2),
                             QKA[:, :, CH * c:CH * c + CH, :].rearrange("p s t d -> p s (t d)"), ACT.Square).then_inc(s["sq_ready"], 1)

            def norms(c):
                act.wait_ge(s["nq_ready"], c + 1)
                a.activation(NS[:], NQ[:], ACT.Sqrt).then_inc(s["ns_ready"], 1)

            def high_halves(c):
                for si, dst, where, ready, done in ((1, KSs[c % 2], slice(0, 4, 2), "kn_ready", "hi_k"),
                                                    (0, QSs[c % 2], slice(0, 2), "qn_ready", "hi_q")):
                    act.wait_ge(s[ready], c + 1)
                    if c >= 2:
                        act.wait_ge(s["kt_ps" if si else "qt_ps"], c - 1)
                    src = QKA[:, si, CH * c:CH * c + CH, :].rearrange("p t (h d) -> p (t h) d", d=HD)
                    a.activation(dst[:, :, where, :], src.unsqueeze(2).to_broadcast([P, CH * HEADS, 2, HD]), ACT.Copy
                                 ).then_inc(s[done], 1)

            deviations(0)
            deviations(1)
            deviations2(1, slice(0, CH))
            deviations(2)
            normed_rows(0)
            deviations2(2, slice(CH, 2 * CH))
            deviations(3)
            gate_cols(0)
            for i, (dst, bank, n) in enumerate(((COL[:, 18:20], 6, 2), (WT[:, 0:4].rearrange("p j n -> p (j n)"), 4, 512))):
                act.wait_ge(s["wt_ps"], i + 1)
                a.activation(dst, ps[bank][:, 0:n], ACT.Copy).then_inc(s["wt_sb"], 1)
            act.wait_ge(s["wt_sb"], 1)
            qkv_cols(0)
            normed_rows(1)
            deviations2(3, slice(2 * CH, NT))
            gate_cols(1)
            normed_rows(2)
            qkv_cols(1)
            normed_rows(3)
            squares(0)
            gate_cols(2)
            qkv_cols(2)
            norms(0)
            gate_cols(3)
            squares(1)
            qkv_cols(3)
            for c in range(EARLY):
                high_halves(c)
                if c + 1 < EARLY:
                    norms(c + 1)
            act.wait_ge(s["late_sq"], NC - EARLY)
            a.activation(NL[:], NL[:], ACT.Sqrt).then_inc(s["late_std"], 1)
            for i, (dst, bank, n) in enumerate(((WT[:, 4:8].rearrange("p j n -> p (j n)"), 4, 512), (COL[:, 0:18], 5, 18))):
                act.wait_ge(s["wt_ps"], i + 3)
                a.activation(dst, ps[bank][:, 0:n], ACT.Copy).then_inc(s["wt_sb"], 1)
            act.wait_ge(s["wt_sb"], 4)
            a.activation(WDEC[:], DECAY, ACT.Exp).then_inc(s["decay_exp"], 1)

            def exps(n, st, first=False):
                for h in range(2):
                    act.wait_ge(s["qk_ready"], 2 * n + (h + 1))
                    if not first and h == 0:
                        act.wait_ge(s["av_done"], n - (PBUF - 1))
                    a.activation(PR[:, st % PBUF, 2 * h:2 * h + 2, :], S[:, 2 * h:2 * h + 2, :], ACT.Exp, scale=SCALE
                                 ).then_inc(s["exp_done"], 1)

            def gelus(G):
                for i in range(RING):
                    act.wait_ge(s["h_sb"], RING * G + (i + 1))
                    a.activation(HB[:, i], HB[:, i], ACT.Gelu).then_inc(s["gelu_done"], 1)

            for st in range(KT_TILES):
                exps(st, st, first=st < PBUF)
                if st == 6:
                    act.wait_ge(s["top_ready"], 1)
                    a.activation(GE[:], GE[:], ACT.Exp).then_inc(s["gexp_ready"], 1)
            with act.Fori(1, MOE_FROM) as g:
                for st in range(KT_TILES):
                    exps(KT_TILES * g + st, st)
            with act.Fori(0, ROUNDS) as G:
                for st in range(KT_TILES):
                    exps(KT_TILES * G + (KT_TILES * MOE_FROM + st), st)
                    if st == 4:
                        gelus(G)
            for st in range(KT_TILES):
                exps(KT_TILES * (NG - 2) + st, st)

            def sqrt2(c):
                act.wait_ge(s["var2_ready"], c + 1)
                a.activation(SD[:, 0:CH], MV[:, 0:CH, 1], ACT.Sqrt).then_inc(s["std2_ready"], 1)

            def before_norm(c):
                act.wait_ge(s["ot_ps"], c + 1)
                if c:
                    act.wait_ge(s["x1_ps"], c)
                a.activation(OTT, ps[6][:], ACT.Copy).then_inc(s["ot_sb"], 1)

            def after_norm(c):
                act.wait_ge(s["xn2t_ps"], c + 1)
                if c >= 2:
                    act.wait_ge(s["up2"], E1 * HC1 * (c - 1))
                a.activation(XN2T[:, c % 2], ps[6][:], ACT.Copy).then_inc(s["xn2t_sb"], 1)

            def keys(c):
                if c:
                    act.wait_ge(s["rw_ready"], c)
                act.wait_ge(s["rvk_ps"], 3 * c + 1)
                a.activation(KX, ps[6][:], ACT.Copy).then_inc(s["rvk_sb"], 1)
                act.wait_ge(s["l8_ready"], c + 1)
                a.activation(P8[:], L8[:], ACT.Exp).then_inc(s["p8_exp"], 1)

            def values_receptance(c):
                act.wait_ge(s["rvk_ps"], 3 * c + 2)
                a.activation(VX, ps[7][:], ACT.Copy).then_inc(s["rvk_sb"], 1)
                act.wait_ge(s["rvk_ps"], 3 * c + 3)
                a.activation(ER, ps[6][:], ACT.Exp, scale=-1.0).then_inc(s["rvk_sb"], 1)

            def gates_cols(c):
                act.wait_ge(s["gt_ps"], c + 1)
                a.activation(GTT[0:E1, c % 2], ps[7][0:E1], ACT.Copy).then_inc(s["gt_sb"], 1)

            def state_exps(c):
                act.wait_ge(s["d_ready"], 4 * c + 2)
                a.activation(D1, D1, ACT.Exp).then_inc(s["d_exp"], 1)
                act.wait_ge(s["pool_wkv"], 4 * c + 1)
                a.activation(D2, D2, ACT.Exp).then_inc(s["d_exp"], 1)

            def output_exps(c):
                act.wait_ge(s["pool_wkv"], 4 * c + 2)
                a.activation(F1, F1, ACT.Exp).then_inc(s["d_exp"], 1)
                act.wait_ge(s["d_ready"], 4 * c + 4)
                a.activation(F2, F2, ACT.Exp).then_inc(s["d_exp"], 1)

            def relus(c, e):
                for k in range(HC1):
                    n = HC1 * (E1 * c + e) + k
                    act.wait_ge(s["up2"], n + 1)
                    if E1 * c + e >= 2 and k == 0:
                        act.wait_ge(s["down2"], E1 * c + e - 1)
                    a.activation(HS[:, e % 2, k], ps[2 * (e % 2) + k][:], ACT.Relu, bias=COL[:, HC1 * e + k:HC1 * e + k + 1]
                                 ).then_inc(s["relu_done"], 1)

            for st in range(KT_TILES):
                exps(KT_TILES * (NG - 1) + st, st)
                if st == 5:
                    before_norm(0)
            sqrt2(0)
            after_norm(0)
            keys(0)
            relus(0, 0)
            values_receptance(0)
            for c in range(NC):
                x = c + 1
                for e in range(E1):
                    if e + 1 < E1:
                        relus(c, e + 1)
                    elif x < NC:
                        relus(x, 0)
                    if c == 0:
                        if e == 0:
                            gates_cols(0)
                            state_exps(0)
                        if e == 1:
                            output_exps(0)
                    if x < NC:
                        if e == 0:
                            before_norm(x)
                        if e == 2:
                            sqrt2(x)
                        if e == 3:
                            after_norm(x)
                        if e == 4:
                            keys(x)
                        if e == 5:
                            values_receptance(x)
                        if e == 6:
                            state_exps(x)
                            gates_cols(x)
                        if e == 7:
                            output_exps(x)

        @block.vector
        def _(dve):
            link = chain(dve, "dve_chain")
            v = nc.vector

            def variances(c):
                dve.wait_ge(x_in[c], 16)
                for t in range(CH * c, CH * c + CH):
                    last = v.bn_stats(ST[:, t, :], X[:, t, :])
                link(last)
                for t in range(CH * c, CH * c + CH):
                    last = v.bn_aggr(MV[:, t, :], ST[:, t, :])
                link(last)
                v.tensor_scalar(VE[:, CH * c:CH * c + CH], MV[:, CH * c:CH * c + CH, 1], LN_EPS, None, ALU.add).then_inc(s["var_ready"], 1)

            def normalise(c):
                dve.wait_ge(s["std_ready"], c + 1)
                link(v.reciprocal(RS[:, CH * c:CH * c + CH], SD[:, CH * c:CH * c + CH]))
                for t in range(CH * c, CH * c + CH):
                    last = v.tensor_scalar(XN[:, t, :], X[:, t, :], MV[:, t, 0:1], RS[:, t:t + 1], ALU.subtract, ALU.mult)
                last.then_inc(s["xn_ready"], 1)

            def variances2(tiles):
                link(v.tensor_tensor(V2[:, tiles], MV[:, tiles, 1], RS[:, tiles], ALU.mult))
                v.tensor_tensor(V2[:, tiles], V2[:, tiles], RS[:, tiles], ALU.mult).then_inc(s["hvar_ready"], 1)

            def scales2(n, tiles):
                dve.wait_ge(s["hstd_ready"], n)
                link(v.reciprocal(RH[:, tiles], RH[:, tiles]))
                link(v.tensor_tensor(RH[:, tiles], RH[:, tiles], RS[:, tiles], ALU.mult))
                v.scalar_tensor_tensor(NB[:, tiles], MV[:, tiles, 0], -1.0, RH[:, tiles], ALU.mult, ALU.mult).then_inc(s["hscale_ready"], 1)

            v.memset(EPS[:], LN_EPS)
            variances(0)
            variances(1)
            normalise(0)
            variances2(slice(0, CH))
            variances(2)
            scales2(1, slice(0, CH))
            normalise(1)
            variances2(slice(CH, 2 * CH))
            variances(3)
            scales2(2, slice(CH, 2 * CH))
            normalise(2)
            normalise(3)
            variances2(slice(2 * CH, NT))
            scales2(3, slice(2 * CH, NT))

            def square_sums(c):
                dve.wait_ge(s["sq_ready"], c + 1)
                v.tensor_reduce(NQ[:], TMPs[c % 2].rearrange("p (n d) -> p n d", d=HD), AX, ALU.add).then_inc(s["nq_ready"], 1)

            dve.wait_ge(s["c_in"], 80)
            dve.wait_ge(s["const_ready"], 2)

            def projected(c):
                for t in range(CH * c, CH * c + CH):
                    dve.wait_ge(s["qkv_ps"], t + 1)
                    q = ps[4 + t % 3]
                    v.tensor_tensor(QKA[:, :, t, :], q[:, 0:2 * D].rearrange("p (s d) -> p s d", s=2),
                                    qkv_b[:, 0:2 * D].rearrange("p (s d) -> p s d", s=2), ALU.add)
                    v.tensor_tensor(VA[:, t, :, 0:HD], q[:, 2 * D:3 * D].rearrange("p (h d) -> p h d", d=HD),
                                    qkv_b[:, 2 * D:3 * D].rearrange("p (h d) -> p h d", d=HD), ALU.add).then_inc(s["qkv_sb"], 1)
                dve.wait_ge(s["lg_ps"], c + 1)
                v.tensor_tensor(LG[:, CH * c:CH * c + CH, :], ps[7][:].rearrange("p (t n) -> p t n", n=P)[:, :, 0:E0],
                                gate_b[:].unsqueeze(1).to_broadcast([P, CH, E0]), ALU.add).then_inc(s["lg_sb"], 1)

            def split_cols(c, dst, bank, ready, done):
                dve.wait_ge(s[ready], c + 1)
                v.tensor_copy(dst[:, :, BLK * c:BLK * c + BLK], S[:, bank:bank + 2].rearrange("p b n -> p (b n)").bitcast(F16)
                              .rearrange("p (g n) -> p g n", g=NHG)).then_inc(s[done], 1)

            def keys_cols(c):
                split_cols(c, KT, 0, "kt_ps", "kt_sb")

            def queries_cols(c):
                split_cols(c, QT, 2, "qt_ps", "qt_sb")

            def unit_length(c):
                dve.wait_ge(s["ns_ready"], c + 1)
                link(v.tensor_scalar(NS[:], NS[:], NORM_EPS, None, ALU.max))
                v.reciprocal(NS[:], NS[:]).then_inc(s["inv_ready"], 1)
                dve.wait_ge(s["inv_ready"], c + 1)
                ka = QKA[:, 1, CH * c:CH * c + CH, :].rearrange("p t (h d) -> p (t h) d", d=HD)
                v.tensor_tensor(ka, ka, NS[:, 64:128].unsqueeze(2).to_broadcast([P, CH * HEADS, HD]), ALU.mult).then_inc(s["kn_ready"], 1)

            def low_keys(c):
                dve.wait_ge(s["hi_k"], c + 1)
                k = KSs[c % 2]
                ka = QKA[:, 1, CH * c:CH * c + CH, :].rearrange("p t (h d) -> p (t h) d", d=HD)
                v.tensor_tensor(k[:, :, 1:4:2, :], ka.unsqueeze(2).to_broadcast([P, CH * HEADS, 2, HD]), k[:, :, 0:4:2, :],
                                ALU.subtract).then_inc(s["lo_k"], 1)

            projected(0)
            projected(1)
            square_sums(0)
            projected(2)
            unit_length(0)
            square_sums(1)
            projected(3)

            def late_sums(c):
                dve.wait_ge(s["late_in"], c - EARLY + 1)
                v.tensor_reduce(NL[:, c - EARLY, :], TMPs[c % 2].rearrange("p (n d) -> p n d", d=HD), AX, ALU.add).then_inc(s["late_sq"], 1)

            low_keys(0)
            unit_length(1)
            keys_cols(0)
            queries_cols(0)
            low_keys(1)
            late_sums(2)
            late_sums(3)
            keys_cols(1)

            def late_lengths():
                dve.wait_ge(s["late_std"], 1)
                link(v.tensor_scalar(NL[:], NL[:], NORM_EPS, None, ALU.max))
                link(v.reciprocal(NL[:], NL[:]))

            def late_split(c):
                n = CH * HEADS
                parts = ((1, late_k[c - EARLY], slice(0, 4, 2), slice(1, 4, 2)), (0, late_q[c - EARLY], slice(0, 2), slice(2, 4)))
                for si, dst, hi, lo in parts:
                    x = QKA[:, si, CH * c:CH * c + CH, :].rearrange("p t (h d) -> p (t h) d", d=HD)
                    inv = NL[:, c - EARLY, 64 * si:64 * si + 64].unsqueeze(2).to_broadcast([P, n, HD])
                    link(v.tensor_tensor(x, x, inv, ALU.mult))
                    x2 = x.unsqueeze(2).to_broadcast([P, n, 2, HD])
                    link(v.tensor_copy(dst[:, :, hi, :], x2))
                    v.tensor_tensor(dst[:, :, lo, :], x2, dst[:, :, hi, :], ALU.subtract).then_inc(s["late_split"], 1)

            def late_cols(i, c):
                dve.wait_ge(s["late_ps"], i + 1)
                dst = (QT if i % 2 else KT)[:, :, BLK * c:BLK * c + BLK]
                for h in range(2):
                    last = v.tensor_copy(dst[:, 2 * h:2 * h + 2, :], ps[5 + h][:].bitcast(F16).rearrange("p (g n) -> p g n", g=2))
                last.then_inc(s["late_sb"], 1)

            def stage(g):
                c, hg, a = g // NHG, g % NHG, g % 2
                b = c * BLK // N
                if g >= 2:
                    dve.wait_ge(s["qk_ready"], 2 * KT_TILES * (g - 1))
                    dve.wait_ge(s["av_done"], KT_TILES * (g - 1))
                v.tensor_copy(KST[:, a], KT[:, hg, N * b:N * b + N])
                for j in range(HG):
                    rows = slice(32 * j, 32 * j + 32)
                    v.tensor_copy(QST[rows, a, j, :], QT[rows, hg, BLK * c:BLK * c + BLK])
                v.tensor_copy(VST[:, a].rearrange("p s j w -> p s (j w)"),
                              VA[:, KT_TILES * b:KT_TILES * (b + 1), HG * hg:HG * hg + HG, :].rearrange("p t h w -> p t (h w)")
                              ).then_inc(s["staged"], 1)

            def evacuate(g):
                dve.wait_ge(s["av_done"], KT_TILES * (g + 1))
                if g >= 2:
                    dve.wait_ge(s["ep_ps"], g - 1)
                v.tensor_copy(OTs[:, g % 2], AV[:]).then_inc(s["a_evac"], 1)

            def divide(g):
                dve.wait_ge(s["ep_ps"], g + 1)
                o = ps[7][:].rearrange("p (t j w) -> p t j w", t=CH, w=32)
                sums = NQ[:, 0:CH * HG].rearrange("p (t j) -> p t j", t=CH)
                link(v.reciprocal(sums, o[:, :, :, HD]))
                for t in range(CH):
                    last = v.tensor_tensor(OH[:, g // NHG, t, g % NHG, :].rearrange("p (j d) -> p j d", d=HD), o[:, t, :, 0:HD],
                                           sums[:, t, :].unsqueeze(2).to_broadcast([P, HG, HD]), ALU.mult)
                last.then_inc(s["ep_used"], 1)

            dve.wait_ge(s["kt_sb"], EARLY)
            dve.wait_ge(s["qt_sb"], 1)
            dve.wait_ge(s["const_ready"], 3)
            stage(0)
            queries_cols(1)
            stage(1)

            for t in range(NT):
                last = v.max(MX[:, t, :], LG[:, t, :])
            link(last)
            for t in range(NT):
                last = v.max_index(IX[:, t, :], MX[:, t, :], LG[:, t, :])
            link(last)
            v.tensor_tensor(GE[:], MX[:, :, 0:TOPK], MX[:, :, 0:1].to_broadcast([P, NT, TOPK]), ALU.subtract
                            ).then_inc(s["top_ready"], 1)
            link(v.tensor_copy(IXF[:], IX[:, :, 0:TOPK]))
            for k in range(TOPK):
                last = v.tensor_tensor(EQ[:, k], iota_e[:].unsqueeze(1).to_broadcast([P, NT, E0]),
                                       IXF[:, :, k:k + 1].to_broadcast([P, NT, E0]), ALU.is_equal)
            link(last)
            link(v.tensor_tensor(MH[:], EQ[:, 0], EQ[:, 1], ALU.add))
            link(v.tensor_tensor(MH[:], MH[:], EQ[:, 2], ALU.add))
            link(v.memset(MPRE[:, 0, :], 0.0))
            for t in range(1, NT):
                last = v.tensor_tensor(MPRE[:, t, :], MPRE[:, t - 1, :], MH[:, t - 1, :], ALU.add)
                if t < NT - 1:
                    link(last)
            last.then_inc(s["mask_ready"], 1)
            dve.wait_ge(s["gexp_ready"], 1)
            link(v.tensor_reduce(GS[:], GE[:], AX, ALU.add))
            link(v.reciprocal(GS[:], GS[:]))
            link(v.tensor_tensor(GE[:], GE[:], GS[:].unsqueeze(2).to_broadcast([P, NT, TOPK]), ALU.mult))

            def slots():
                dve.wait_ge(s["count_ready"], 1)
                tmp = TMP.rearrange("p (t e) -> p t e", e=E0)
                for k in range(TOPK):
                    for h in range(2):
                        rows = slice(NT // 2 * h, NT // 2 * (h + 1))
                        last = v.tensor_tensor(tmp[:, rows, :], ps[5 + h][:].rearrange("p (t e) -> p t e", e=E0), EQ[:, k, rows, :], ALU.mult)
                    link(last)
                    link(v.tensor_reduce(POS[:, k, :], tmp, AX, ALU.add))
                link(v.tensor_scalar(VAL[:], POS[:], float(CAP), None, ALU.is_lt))
                link(v.tensor_scalar(SLF[:], POS[:], float(CAP - 1), None, ALU.min))
                ix = IXF[:].rearrange("p t k -> p k t")
                link(v.scalar_tensor_tensor(SLF[:], ix, float(CAP), SLF[:], ALU.mult, ALU.add))
                link(v.tensor_copy(SLG[:], SLF[:]))
                link(v.tensor_scalar(POS[:], POS[:], float(CAP), float(2 * SLOTS), ALU.is_ge, ALU.mult))
                link(v.tensor_tensor(SLF[:], SLF[:], POS[:], ALU.add))
                link(v.tensor_copy(SLS[:], SLF[:]))
                v.tensor_tensor(GE[:], GE[:], VAL[:].rearrange("p k t -> p t k"), ALU.mult).then_inc(s["slots_ready"], 1)

            def moe_in(G):
                dve.wait_ge(s["bt_ps"], G + 1)
                if G:
                    dve.wait_ge(s["up_done"], RING * G)
                v.tensor_copy(BT, ps[6][:]).then_inc(s["bt_sb"], 1)

            def moe_h(G, i):
                dve.wait_ge(s["up_done"], RING * G + i + 1)
                if G:
                    dve.wait_ge(s["htr_ps"], RING * (G - 1) + i + 1)
                dve.wait_ge(ring_in_a[i], 48 * (G + 1))
                v.tensor_tensor(HB[:, i], ps[5 + i % 2][:], ring_b1[i], ALU.add).then_inc(s["h_sb"], 1)

            def moe_cols(G):
                for i in range(RING):
                    dve.wait_ge(s["htr_ps"], RING * G + i + 1)
                    if i == 0 and G:
                        dve.wait_ge(s["down_done"], G)
                    v.tensor_copy(HTS[:, i], ps[5 + i % 2][:]).then_inc(s["htr_sb"], 1)

            def moe_y(G):
                dve.wait_ge(s["down_done"], G + 1)
                if G:
                    dve.wait_ge(s["y_out"], 16 * G)
                for i in range(RING):
                    dve.wait_ge(ring_in_b[i], 48 * (G + 1))
                v.tensor_tensor(Y, ps[7][:].rearrange("p (i d) -> p i d", d=D), ring_b2, ALU.add).then_inc(s["y_sb"], 1)

            for g in range(1, NG):
                G = g - MOE_FROM
                evacuate(g - 1)
                if 0 <= G < ROUNDS:
                    moe_in(G)
                if g + 1 < NG:
                    stage(g + 1)
                if G == ROUNDS:
                    moe_y(G - 1)
                divide(g - 1)
                if 0 <= G < ROUNDS:
                    for i in range(RING):
                        moe_h(G, i)
                if 1 <= G < ROUNDS:
                    moe_y(G - 1)
                if 0 <= G < ROUNDS:
                    moe_cols(G)
                if g == 1:
                    slots()
                if g == LATE:
                    dve.wait_ge(s["zeroed"], 32)
                    late_lengths()
                    late_split(2)
                    late_cols(0, 2)
                if g == LATE + 1:
                    late_cols(1, 2)
                    late_split(3)
                    late_cols(2, 3)
                if g == LATE + 2:
                    late_cols(3, 3)
                    dve.wait_ge(s["late_sb"], 4)

            def combine(c):
                dve.wait_ge(gathered[c], 16 * TOPK * CH)
                for k in range(TOPK):
                    for t in range(CH * c, CH * c + CH):
                        last = v.scalar_tensor_tensor(BASE[:, t, :], YG[:, t, k, :], GE[:, t, k:k + 1], BASE[:, t, :], ALU.mult, ALU.add)
                    link(last)

            def x1_norm(c):
                chunk = slice(CH * c, CH * c + CH)
                dve.wait_ge(s["x1_ps"], c + 1)
                if c:
                    dve.wait_ge(s["combined"], (TOPK + 1) * c)
                xs = BASE[:, chunk, :]
                v.tensor_tensor(xs, xs, ps[7][:].rearrange("p (t d) -> p t d", d=D), ALU.add).then_inc(s["x1_sb"], 1)
                dve.wait_ge(s["x1_sb"], c + 1)
                for t in range(CH):
                    last = v.bn_stats(ST[:, t, :], BASE[:, CH * c + t, :])
                link(last)
                for t in range(CH):
                    last = v.bn_aggr(MV[:, t, :], ST[:, t, :])
                link(last)
                v.tensor_scalar(MV[:, 0:CH, 1], MV[:, 0:CH, 1], LN_EPS, None, ALU.add).then_inc(s["var2_ready"], 1)

            def x1_scale(c):
                dve.wait_ge(s["std2_ready"], c + 1)
                link(v.reciprocal(RS[:, 0:CH], SD[:, 0:CH]))
                if c:
                    dve.wait_ge(s["xn2t_ps"], c)
                else:
                    dve.wait_ge(s["qk_ready"], 2 * KT_TILES * (NG - 1))
                for t in range(CH):
                    last = v.tensor_scalar(XN2[:, t, :], BASE[:, CH * c + t, :], MV[:, t, 0:1], RS[:, t:t + 1], ALU.subtract, ALU.mult)
                last.then_inc(s["xn2_ready"], 1)

            def gates_in(c):
                dve.wait_ge(s["lg2_ps"], c + 1)
                lg = ps[7][:, 0:CH * E1].rearrange("p (t e) -> p t e", e=E1)
                link(v.tensor_reduce(S4[:], lg, AX, ALU.max))
                v.tensor_tensor(L8[:], lg, S4[:].unsqueeze(2).to_broadcast([P, CH, E1]), ALU.subtract).then_inc(s["l8_ready"], 1)

            def gates(c):
                dve.wait_ge(s["p8_exp"], c + 1)
                link(v.tensor_reduce(S4[:], P8[:], AX, ALU.add))
                link(v.reciprocal(S4[:], S4[:]))
                link(v.tensor_tensor(P8[:], P8[:], S4[:].unsqueeze(2).to_broadcast([P, CH, E1]), ALU.mult))
                for t in range(CH):
                    last = v.max(M8[:, t, :], P8[:, t, :])
                link(last)
                for t in range(CH):
                    last = v.max_index(I8[:, t, :], M8[:, t, :], P8[:, t, :])
                link(last)
                link(v.tensor_copy(I8F[:], I8[:, :, 0:2]))
                g8 = G8[:, c % 2]
                iota = iota_e[:, 0:E1].unsqueeze(1).to_broadcast([P, CH, E1])
                v.tensor_tensor(g8, iota, I8F[:, :, 0:1].to_broadcast([P, CH, E1]), ALU.is_equal)
                link(v.tensor_tensor(L8[:], iota, I8F[:, :, 1:2].to_broadcast([P, CH, E1]), ALU.is_equal))
                link(v.tensor_tensor(g8, g8, L8[:], ALU.add))
                v.tensor_tensor(g8, g8, P8[:], ALU.mult).then_inc(s["g_ready"], 1)

            def time_mix(c):
                scan = v.tensor_tensor_scan
                dve.wait_ge(s["rvk_sb"], 3 * c + 1)
                for st, first in ((PP, NEG_BIG), (AA, 0.0), (BB, 0.0)):
                    if (c * BLK) % N == 0:
                        last = v.memset(st[:, 0:1], first)
                    else:
                        last = v.tensor_copy(st[:, 0:1], st[:, BLK:BLK + 1])
                link(last)
                now, new = slice(0, BLK), slice(1, BLK + 1)
                scan(PP[:, new], NEGW[:].to_broadcast([P, BLK]), KX, PP[:, 0:1], ALU.add, ALU.max).then_inc(s["d_ready"], 1)
                dve.wait_ge(s["d_ready"], 4 * c + 1)
                v.scalar_tensor_tensor(D1, PP[:, now], NEGW[:], PP[:, new], ALU.add, ALU.subtract).then_inc(s["d_ready"], 1)
                v.scalar_tensor_tensor(PM, KX, FIRST, PP[:, now], ALU.add, ALU.max).then_inc(s["d_ready"], 1)
                dve.wait_ge(s["d_ready"], 4 * c + 3)
                v.scalar_tensor_tensor(F2, KX, FIRST, PM, ALU.add, ALU.subtract).then_inc(s["d_ready"], 1)

            def time_mix_states(c):
                scan = v.tensor_tensor_scan
                new = slice(1, BLK + 1)
                dve.wait_ge(s["d_exp"], 4 * c + 2)
                scan(BB[:, new], D1, D2, BB[:, 0:1], ALU.mult, ALU.add)
                dve.wait_ge(s["pool_wkv"], 4 * c + 3)
                link(scan(AA[:, new], D1, EV, AA[:, 0:1], ALU.mult, ALU.add))

            def time_mix_out(c):
                now = slice(0, BLK)
                dve.wait_ge(s["d_exp"], 4 * c + 4)
                v.tensor_tensor(NU, F1, AA[:, now], ALU.mult)
                link(v.tensor_tensor(DE, F1, BB[:, now], ALU.mult))
                link(v.tensor_tensor(DE, DE, F2, ALU.add))
                dve.wait_ge(s["pool_wkv"], 4 * c + 4)
                v.tensor_tensor(NU, NU, T1, ALU.add)
                dve.wait_ge(s["rvk_sb"], 3 * c + 3)
                link(v.scalar_tensor_tensor(DE, ER, 1.0, DE, ALU.add, ALU.mult))

            def time_mix_end(c):
                link(v.reciprocal(DE, DE))
                if c >= 2:
                    dve.wait_ge(s["fin_ps"], c - 1)
                v.tensor_tensor(RWT[c % 2], NU, DE, ALU.mult).then_inc(s["rw_ready"], 1)

            def accumulate(c, e):
                if e == 0:
                    dve.wait_ge(s["g_ready"], c + 1)
                dve.wait_ge(s["down2"], E1 * c + e + 1)
                for t in range(CH):
                    y = BASE[:, CH * c + t, :]
                    last = v.scalar_tensor_tensor(y, ps[4 + e % 2][:, D * t:D * t + D], G8[:, c % 2, t, e:e + 1], y, ALU.mult, ALU.add)
                last.then_inc(s["acc_done"], 1)
                dve.wait_ge(s["acc_done"], E1 * c + e + 1)

            def mixed(c):
                dve.wait_ge(s["fin_ps"], c + 1)
                xs = BASE[:, CH * c:CH * c + CH, :]
                v.tensor_tensor(xs, xs, ps[6][:].rearrange("p (t d) -> p t d", d=D), ALU.add).then_inc(s["fin_sb"], 1)
                dve.wait_ge(s["fin_sb"], c + 1)

            dve.wait_ge(s["decay_exp"], 1)
            link(v.tensor_scalar(NEGW[:], WDEC[:], -1.0, None, ALU.mult))
            combine(0)
            x1_norm(0)
            x1_scale(0)
            evacuate(NG - 1)
            divide(NG - 1)
            gates_in(0)
            gates(0)
            time_mix(0)
            for c in range(NC):
                x = c + 1
                for e in range(E1):
                    accumulate(c, e)
                    if e == 0:
                        if c == 0:
                            time_mix_states(0)
                        else:
                            time_mix_end(c)
                    if c == 0 and e == 5:
                        mixed(0)
                    if x < NC:
                        if e == 1:
                            x1_norm(x)
                        if e == 2:
                            x1_scale(x)
                            if c == 0:
                                time_mix_out(0)
                                time_mix_end(0)
                        if e == 4:
                            gates_in(x)
                        if e == 5:
                            gates(x)
                            time_mix(x)
                        if e == 6:
                            time_mix_states(x)
                        if e == 7:
                            time_mix_out(x)
                    if e == 2 and c:
                        mixed(c)

        @block.tensor
        def _(pe):
            mm, tr = nc.tensor.matmul, nc.tensor.transpose
            def turn(src, c, bank, ready, done, freed):
                pe.wait_ge(s[ready], c + 1)
                if c >= 2:
                    pe.wait_ge(s[freed], c - 1)
                for j in range(CH):
                    last = tr(ps[bank][:, P * j:P * j + P], src[:, CH * c + j, :], ident[:])
                last.then_inc(s[done], 1)

            def turn_xn(c):
                turn(XN, c, c % 2, "xn_ready", "xnt_ps", "xnt_sb")

            def turn_hn(c):
                turn(HN, c, 2 + c % 2, "hn_ready", "hnt_ps", "ht_sb")

            def project(c):
                pe.wait_ge(s["ht_sb"], c + 1)
                for j in range(CH):
                    t = CH * c + j
                    if t >= 3:
                        pe.wait_ge(s["qkv_sb"], t - 2)
                    mm(ps[4 + t % 3][:, 0:3 * D], HT[:, c % 2, P * j:P * j + P], WT[:, 0:3].rearrange("p j n -> p (j n)"),
                       start=True, stop=True).then_inc(s["qkv_ps"], 1)
                pe.wait_ge(s["xnt_sb"], c + 1)
                if c:
                    pe.wait_ge(s["lg_sb"], c)
                for j in range(CH):
                    last = mm(ps[7][:, P * j:P * j + P], XNT[:, c % 2, P * j:P * j + P], gate_w[:].rearrange("p h e -> p (h e)"), start=True, stop=True)
                last.then_inc(s["lg_ps"], 1)

            pe.wait_ge(s["const_ready"], 1)
            turn_xn(0)
            pe.wait_ge(s["w_in"], 16 * 4)
            tr(ps[6][:, 0:2], LN_ROWS[:], ident[0:2, 0:2]).then_inc(s["wt_ps"], 1)
            for j in range(4):
                last = tr(ps[4][:, P * j:P * j + P], WL[:, j, :], ident[:])
            last.then_inc(s["wt_ps"], 1)
            turn_hn(0)
            turn_xn(1)
            pe.wait_ge(s["wt_sb"], 2)
            pe.wait_ge(s["c_in"], 80)
            for c in range(NC):
                if 1 <= c < NC - 1:
                    turn_hn(c + 1)
                project(c)
                if c == 0:
                    turn_hn(1)
                if c + 2 < NC:
                    turn_xn(c + 2)
            pe.wait_ge(s["w1_in"], 16 * 5)
            pe.wait_ge(s["qkv_sb"], NT)
            for j in range(4):
                last = tr(ps[4][:, P * j:P * j + P], WL1[:, j, :], ident[:])
            last.then_inc(s["wt_ps"], 1)
            tr(ps[5][:, 0:18], SMALL[:], ident[0:18, 0:18]).then_inc(s["wt_ps"], 1)

            pe.wait_ge(s["const_ready"], 3)
            pe.wait_ge(s["ht_sb"], NC)
            for c in range(EARLY):
                for src, bank, hi, lo, done, freed in ((KSs[c % 2], 0, "hi_k", "lo_k", "kt_ps", "kt_sb"),
                                                       (QSs[c % 2], 2, "hi_q", "lo_q", "qt_ps", "qt_sb")):
                    pe.wait_ge(s[hi], c + 1)
                    pe.wait_ge(s[lo], c + 1)
                    if c:
                        pe.wait_ge(s[freed], c)
                    cols = src.rearrange("p (t g j) w d -> p t g (j w d)", t=CH, g=NHG)
                    for g in range(NHG):
                        dst = S[:, bank + g // 2].bitcast(F16).rearrange("p (g t n) -> p g t n", g=2, t=CH)
                        for t in range(CH):
                            last = tr(dst[:, g % 2, t, :], cols[:, t, g, :], ident16[:])
                    last.then_inc(s[done], 1)

            def late_turn(i):
                pe.wait_ge(s["late_split"], i + 1)
                if i:
                    pe.wait_ge(s["late_sb"], i)
                else:
                    pe.wait_ge(s["slots_ready"], 1)
                cols = (late_q if i % 2 else late_k)[i // 2].rearrange("p (t g j) w d -> p t g (j w d)", t=CH, g=NHG)
                for g in range(NHG):
                    dst = ps[5 + g // 2][:].bitcast(F16).rearrange("p (g t n) -> p g t n", g=2, t=CH)
                    for t in range(CH):
                        last = tr(dst[:, g % 2, t, :], cols[:, t, g, :], ident16[:])
                last.then_inc(s["late_ps"], 1)

            def scores(n, st, a, h, first=False, new=None):
                if new is not None:
                    pe.wait_ge(s["staged"], new)
                if not first:
                    pe.wait_ge(s["exp_done"], 2 * n + (h - 1))
                for j in (2 * h, 2 * h + 1):
                    last = mm(S[:, j], KST[:, a, P * st:P * st + P], QST[:, a, j, :], start=True, stop=True)
                last.then_inc(s["qk_ready"], 1)

            def values(n, st, a, half, g=None):
                if half == 0:
                    pe.wait_ge(s["exp_done"], 2 * n + 2)
                    if g is not None:
                        pe.wait_ge(s["a_evac"], g)
                cols = slice(BLK // 2 * half, BLK // 2 * (half + 1))
                for j in range(HG):
                    last = mm(AV[32 * j:32 * j + VW, cols], VST[:, a, st, j, :], PR[:, st % PBUF, j, cols],
                              start=(st == 0 and half == 0), stop=(st == KT_TILES - 1), skip_group_check=True)
                if half:
                    last.then_inc(s["av_done"], 1)

            def tokens_out(g, a, y=None):
                pe.wait_ge(s["a_evac"], g)
                if y is not None:
                    pe.wait_ge(s["y_sb"], y)
                for t in range(CH):
                    last = tr(ps[7][:, P * t:P * t + P], OTs[:, 1 - a, P * t:P * t + P], ident[:])
                last.then_inc(s["ep_ps"], 1)

            def slots_in(G, first):
                for i in range(RING):
                    pe.wait_ge(ring_in_x[i], 16 * G + 16)
                if not first:
                    pe.wait_ge(s["htr_sb"], RING * G)
                for i in range(RING):
                    last = tr(ps[6][:, P * i:P * i + P], ring_in[i], ident[:])
                last.then_inc(s["bt_ps"], 1)

            def up(G, i):
                pe.wait_ge(ring_in_a[i], 48 * G + 48)
                pe.wait_ge(s["bt_sb"], G + 1)
                if i >= 2:
                    pe.wait_ge(s["h_sb"], RING * G + (i - 1))
                for e in range(2):
                    last = mm(ps[5 + i % 2][CAP * e:CAP * e + CAP, :], BT[:, P * i + CAP * e:P * i + CAP * e + CAP], ring_w1[i][:, e, :],
                              start=True, stop=True)
                last.then_inc(s["up_done"], 1)

            def hidden(G, i):
                pe.wait_ge(s["gelu_done"], RING * G + (i + 1))
                if i < 2:
                    pe.wait_ge(s["h_sb"], RING * G + (i + 3))
                else:
                    pe.wait_ge(s["htr_sb"], RING * G + (i - 1))
                cols = HB[:, i].rearrange("p (m c) -> p c m", c=HC0)
                for c in range(HC0):
                    last = tr(ps[5 + i % 2][:, P * c:P * c + P], cols[:, c, :], ident[:])
                last.then_inc(s["htr_ps"], 1)

            def down(G, g, pairs):
                pe.wait_ge(s["ep_used"], g)
                for i in pairs:
                    pe.wait_ge(s["htr_sb"], RING * G + (i + 1))
                    pe.wait_ge(ring_in_b[i], 48 * G + 48)
                    for c in range(HC0):
                        for e in range(2):
                            last = mm(ps[7][CAP * e:CAP * e + CAP, D * i:D * i + D],
                                      HTS[:, i, P * c + CAP * e:P * c + CAP * e + CAP], ring_w2[i][:, e, c, :],
                                      start=(c == 0), stop=(c == HC0 - 1), skip_group_check=True)
                if RING - 1 in pairs:
                    last.then_inc(s["down_done"], 1)

            def counts():
                pe.wait_ge(s["mask_ready"], 1)
                for h in range(2):
                    rows = slice(NT // 2 * h, NT // 2 * (h + 1))
                    mm(ps[5 + h][:], before[:], MH[:, rows, :].rearrange("p t e -> p (t e)"), start=True, stop=False)
                    last = mm(ps[5 + h][:], ones[:], MPRE[:, rows, :].rearrange("p t e -> p (t e)"), start=False, stop=True)
                last.then_inc(s["count_ready"], 1)

            def attention_cols(c):
                pe.wait_ge(s["ep_used"], NHG * (c + 1))
                if c:
                    pe.wait_ge(s["rvk_sb"], 3 * c)
                for t in range(CH):
                    last = tr(ps[6][:, P * t:P * t + P], OH[:, c, t].rearrange("p g w -> p (g w)"), ident[:])
                last.then_inc(s["ot_ps"], 1)

            def attention_out(c):
                pe.wait_ge(s["ot_sb"], c + 1)
                if c:
                    pe.wait_ge(s["gt_sb"], c)
                else:
                    pe.wait_ge(s["ep_used"], NG - 1)
                for t in range(CH):
                    last = mm(ps[7][:, P * t:P * t + P], OTT[:, P * t:P * t + P], WT[:, 3, :], start=True, stop=True)
                last.then_inc(s["x1_ps"], 1)

            def group(g, a, first=False, last=False, G=None, first_G=False, H=None, y=None, count=False, late={}):
                for st in range(KT_TILES):
                    n = KT_TILES * g + st
                    due_tile, due_a = (KT_TILES - 1, 1 - a) if st == 0 else (st - 1, a)
                    due = not (first and st == 0)
                    if st < KT_TILES - 1:
                        scores(n + 1, st + 1, a, 1)
                    elif not last:
                        scores(n + 1, 0, 1 - a, 1)
                    if due and st != 1:
                        values(n - 1, due_tile, due_a, 0)
                    if H is not None and G is not None and st == 4:
                        down(H, g, range(RING))
                    if st < KT_TILES - 2:
                        scores(n + 2, st + 2, a, 0)
                    elif not last:
                        scores(n + 2, st + 2 - KT_TILES, 1 - a, 0, new=g + 2 if st == KT_TILES - 2 else None)
                    if st == 1:
                        values(n - 1, due_tile, due_a, 0, g=None if first else g)
                    if due:
                        values(n - 1, due_tile, due_a, 1)
                    if G is None and H is not None:
                        if st <= 1:
                            down(H, g - 1, range(2 * st, 2 * st + 2))
                        if st == 3:
                            tokens_out(g, a, y)
                    elif st == 1 and not first:
                        tokens_out(g, a, y)
                    if last and st == 4:
                        attention_cols(0)
                    if last and st == 6:
                        attention_out(0)
                    if count and st == 1:
                        counts()
                    if st in late:
                        late_turn(late[st])
                    if G is not None:
                        if st == 0:
                            slots_in(G, first_G)
                        if st == 1:
                            up(G, 0)
                        if st == 2:
                            up(G, 1)
                        if st == 3:
                            up(G, 2)
                            up(G, 3)
                        if st == 5:
                            hidden(G, 0)
                            hidden(G, 1)
                        if 6 <= st <= 7:
                            hidden(G, st - 4)

            pe.wait_ge(s["kt_sb"], EARLY)
            pe.wait_ge(s["lg_sb"], NC)
            scores(0, 0, 0, 0, first=True, new=1)
            pe.wait_ge(s["qt_sb"], EARLY)
            scores(0, 0, 0, 1, first=True)
            scores(1, 1, 0, 0)
            group(0, 0, first=True)
            group(1, 1, count=True)
            for g in range(2, MOE_FROM):
                group(g, g % 2, late={LATE: {5: 0, 7: 1}, LATE + 1: {5: 2, 7: 3}}.get(g, {}))
            pe.wait_ge(s["late_sb"], 2 * (NC - EARLY))
            group(MOE_FROM, 0, G=0, first_G=True)
            group(MOE_FROM + 1, 1, G=1, H=0)
            with pe.Fori(1, ROUNDS // 2) as i:
                group(2 * i + MOE_FROM, 0, G=2 * i, H=2 * i - 1, y=2 * i - 1)
                group(2 * i + (MOE_FROM + 1), 1, G=2 * i + 1, H=2 * i, y=2 * i)
            group(NG - 2, 0, H=ROUNDS - 1, y=ROUNDS)
            group(NG - 1, 1, last=True)
            for half in range(2):
                values(KT_TILES * NG - 1, KT_TILES - 1, 1, half)

            def normed(c):
                pe.wait_ge(s["xn2_ready"], c + 1)
                if c >= 2:
                    pe.wait_ge(s["fin_sb"], c)
                for t in range(CH):
                    last = tr(ps[6][:, P * t:P * t + P], XN2[:, t, :], ident[:])
                last.then_inc(s["xn2t_ps"], 1)

            def rvk(c, j, bank):
                mm(ps[bank][:], WT[:, j, :], XN2T[:, c % 2, :], start=True, stop=True).then_inc(s["rvk_ps"], 1)

            def keys_logits(c):
                pe.wait_ge(s["xn2t_sb"], c + 1)
                rvk(c, 6, 6)
                if c == 0:
                    pe.wait_ge(s["ep_used"], NG)
                for t in range(CH):
                    last = mm(ps[7][:, E1 * t:E1 * t + E1], XN2T[:, c % 2, P * t:P * t + P], WG[:], start=True, stop=True)
                last.then_inc(s["lg2_ps"], 1)

            def values_receptance(c):
                pe.wait_ge(s["l8_ready"], c + 1)
                rvk(c, 5, 7)
                if c == 1:
                    finish(0)
                    pe.wait_ge(s["fin_sb"], 1)
                pe.wait_ge(s["rvk_sb"], 3 * c + 1)
                rvk(c, 4, 6)

            def gates_out(c):
                pe.wait_ge(s["g_ready"], c + 1)
                pe.wait_ge(s["rvk_sb"], 3 * c + 2)
                for t in range(CH):
                    last = tr(ps[7][0:E1, P * t:P * t + P], G8[:, c % 2, t, :], ident[:])
                last.then_inc(s["gt_ps"], 1)

            def up2(c, e):
                for k in range(HC1):
                    n = HC1 * (E1 * c + e) + k
                    if n >= 4:
                        pe.wait_ge(s["relu_done"], n - 3)
                    mm(ps[2 * (e % 2) + k][:], MW1[:, e, P * k:P * k + P], XN2T[:, c % 2, :], start=True, stop=True).then_inc(s["up2"], 1)

            def down2(c, e):
                n = E1 * c + e
                pe.wait_ge(s["relu_done"], HC1 * (n + 1))
                if n >= 2:
                    pe.wait_ge(s["acc_done"], n - 1)
                for t in range(CH):
                    for k in range(HC1):
                        last = mm(ps[4 + e % 2][:, D * t:D * t + D], HS[:, e % 2, k, P * t:P * t + P], MW2[:, e, k, :],
                                  start=(k == 0), stop=(k == HC1 - 1))
                last.then_inc(s["down2"], 1)

            def finish(c):
                pe.wait_ge(s["rw_ready"], c + 1)
                pe.wait_ge(s["gt_sb"], c + 1)
                pe.wait_ge(s["rvk_sb"], 3 * c + 3)
                if c == 0:
                    pe.wait_ge(s["rvk_sb"], 4)
                for t in range(CH):
                    cols = slice(P * t, P * t + P)
                    mm(ps[6][:, cols], RWT[c % 2][:, cols], WT[:, 7, :], start=True, stop=False)
                    last = mm(ps[6][:, cols], GTT[0:E1, c % 2, cols], MB2[:], start=False, stop=True)
                last.then_inc(s["fin_ps"], 1)

            pe.wait_ge(s["l1_in"], 32)
            normed(0)
            pe.wait_ge(s["x1_sb"], 1)
            tokens_out(NG, 0)
            keys_logits(0)
            pe.wait_ge(s["mw_in"], 32)
            up2(0, 0)
            values_receptance(0)
            for c in range(NC):
                x = c + 1
                for e in range(E1):
                    if e + 1 < E1:
                        up2(c, e + 1)
                    elif x < NC:
                        up2(x, 0)
                    down2(c, e)
                    if c == 0 and e == 0:
                        gates_out(0)
                    if x < NC:
                        if e == 0:
                            attention_cols(x)
                        if e == 1:
                            attention_out(x)
                    if e == 2 and c:
                        finish(c)
                    if x < NC:
                        if e == 3:
                            normed(x)
                        if e == 4:
                            keys_logits(x)
                        if e == 5:
                            values_receptance(x)
                        if e == 6:
                            gates_out(x)

_INS = ["L0_attn_x", "L0_attn_ln_w", "L0_attn_ln_b", "L0_attn_qkv_w", "L0_attn_qkv_b", "L0_attn_out_w", "L0_attn_out_b",
        "L0_ffn_gate_w", "L0_ffn_gate_b", "L0_ffn_w1", "L0_ffn_b1", "L0_ffn_w2", "L0_ffn_b2", "L1_attn_W_rvk", "L1_attn_W_out",
        "L1_attn_time_decay", "L1_attn_time_first", "L1_ffn_Wg", "L1_ffn_W1", "L1_ffn_b1", "L1_ffn_W2", "L1_ffn_b2"]


def kernel(**inputs):
    import numpy as np
    import concourse.bacc as bacc
    from concourse.bass_utils import run_bass_kernel_spmd

    nc = bacc.Bacc("TRN2", target_bir_lowering=False, num_devices=1)
    arrays, args = {}, []
    for name in _INS:
        a = np.ascontiguousarray(inputs[name])
        arrays[f"in_{name}"] = a
        args.append(nc.dram_tensor(f"in_{name}", a.shape, mybir.dt.from_np(a.dtype), kind="ExternalInput").ap())
    args.append(nc.dram_tensor("out_0", inputs["L0_attn_x"].shape, F32, kind="ExternalOutput").ap())
    build(nc, *args)
    return run_bass_kernel_spmd(nc, [arrays], core_ids=[0]).results[0]["out_0"]
```
